# Optimizing a Trainium2 kernel written in Bass

```python
import numpy as np
import jax
import jax.numpy as jnp

def _softmax(x, axis=-1):
    return jax.nn.softmax(x, axis=axis)

def _gelu(x):
    return jax.nn.gelu(x, approximate=True)

def _silu(x):
    return jax.nn.silu(x)

def _sigmoid(x):
    return jax.nn.sigmoid(x)

def _layernorm(x, axis=-1, eps=1e-05):
    m = jnp.mean(x, axis=axis, keepdims=True)
    v = jnp.var(x, axis=axis, keepdims=True)
    return (x - m) / jnp.sqrt(v + eps)

def _scatter_add(tgt, idx, src, axis=0):
    return tgt.at[idx].add(src)

def _segment_sum(src, seg, n):
    return jax.ops.segment_sum(src, seg, n)
kernel_name = 'mk_conv_seq_d2_conv_nhwc768_r4_56bd74'

def setup_inputs(seed: int=0):
    np.random.seed(seed)
    _w = jnp.asarray

    def _rec_inputs():
        import jax
        import jax.numpy as jnp
        _gk = jax.random.key(seed)
        x = -0.0002221 + 1 * jax.random.normal(jax.random.fold_in(_gk, 1), (8, 16, 16, 192), jnp.float32)
        return x
    x = _rec_inputs()

    def _L0_conv_setup():
        import jax, jax.numpy as jnp
        import numpy as np
        WINDOW_SIZE = 14
        NUM_HEADS = 12
        LN_EPS = 1e-06

        def window_partition(x, ws):
            B, H, W, C = x.shape
            pad_h = -H % ws
            pad_w = -W % ws
            x = jnp.pad(x, ((0, 0), (0, pad_h), (0, pad_w), (0, 0)))
            Hp, Wp = (H + pad_h, W + pad_w)
            x = x.reshape(B, Hp // ws, ws, Wp // ws, ws, C)
            x = x.transpose(0, 1, 3, 2, 4, 5).reshape(-1, ws, ws, C)
            return (x, (Hp, Wp))

        def window_unpartition(windows, ws, pad_hw, hw):
            Hp, Wp = pad_hw
            H, W = hw
            C = windows.shape[-1]
            B = windows.shape[0] // (Hp * Wp // ws // ws)
            x = windows.reshape(B, Hp // ws, Wp // ws, ws, ws, C)
            x = x.transpose(0, 1, 3, 2, 4, 5).reshape(B, Hp, Wp, C)
            return x[:, :H, :W, :]

        def apply_rot_embed_cat(x, rope):
            d = x.shape[-1] // 2
            sin, cos = (rope[..., :d], rope[..., d:])
            x1, x2 = (x[..., :d], x[..., d:])
            return jnp.concatenate([x1 * cos - x2 * sin, x2 * cos + x1 * sin], axis=-1)

        def layer_norm(x, g, b):
            m = jnp.mean(x, axis=-1, keepdims=True)
            v = jnp.var(x, axis=-1, keepdims=True)
            return (x - m) * jax.lax.rsqrt(v + LN_EPS) * g + b

        def attention(x, rope, w_qkv, b_qkv, w_proj, b_proj):
            B, H, W, C = x.shape
            N = H * W
            hd = C // NUM_HEADS
            qkv = x.reshape(B, N, C) @ w_qkv.T + b_qkv
            qkv = qkv.reshape(B, N, 3, NUM_HEADS, hd).transpose(2, 0, 3, 1, 4)
            q, k, v = (qkv[0], qkv[1], qkv[2])
            if rope is not None:
                q = apply_rot_embed_cat(q, rope)
                k = apply_rot_embed_cat(k, rope)
            attn = jax.nn.softmax(jnp.einsum('bhqd,bhkd->bhqk', q * hd ** (-0.5), k), axis=-1)
            out = jnp.einsum('bhqk,bhkd->bhqd', attn, v)
            out = out.transpose(0, 2, 1, 3).reshape(B, H, W, C)
            return out @ w_proj.T + b_proj
        key = jax.random.key(seed)
        ks = jax.random.split(key, 12)
        C = 192
        hd = C // NUM_HEADS
        Hf = 4 * C
        s = lambda k, shp, fan: jax.random.normal(k, shp, jnp.float32) * fan ** (-0.5)
        return {'x': jax.random.normal(ks[0], (8, 16, 16, C), jnp.float32), 'rope_2d': jax.random.normal(ks[1], (1, 16, 16, hd), jnp.float32), 'ln1_g': jnp.ones((C,), jnp.float32), 'ln1_b': jnp.zeros((C,), jnp.float32), 'w_qkv': s(ks[2], (3 * C, C), C), 'b_qkv': jnp.zeros((3 * C,), jnp.float32), 'w_proj': s(ks[3], (C, C), C), 'b_proj': jnp.zeros((C,), jnp.float32), 'gamma_1': jnp.full((C,), 0.1, jnp.float32), 'ln2_g': jnp.ones((C,), jnp.float32), 'ln2_b': jnp.zeros((C,), jnp.float32), 'w_fc1': s(ks[4], (Hf, C), C), 'b_fc1': jnp.zeros((Hf,), jnp.float32), 'w_fc2': s(ks[5], (C, Hf), Hf), 'b_fc2': jnp.zeros((C,), jnp.float32), 'gamma_2': jnp.full((C,), 0.1, jnp.float32)}
    _L0_conv_all = _L0_conv_setup()
    _L0_conv_in = {k: v for k, v in _L0_conv_all.items() if k in ('rope_2d', 'ln1_g', 'ln1_b', 'w_qkv', 'b_qkv', 'w_proj', 'b_proj', 'gamma_1', 'ln2_g', 'ln2_b', 'w_fc1', 'b_fc1', 'w_fc2', 'b_fc2', 'gamma_2')}
    del _L0_conv_all

    def _L1_conv_setup():
        import jax, jax.numpy as jnp
        import numpy as np
        DIM = 192
        NH = 12
        HD = DIM // NH
        WS = 14
        EPS = 1e-05

        def _ln(x, w, b):
            m = jnp.mean(x, -1, keepdims=True)
            v = jnp.var(x, -1, keepdims=True)
            return (x - m) * jax.lax.rsqrt(v + EPS) * w + b

        def _block(x, ln1_w, ln1_b, qkv_w, qkv_b, proj_w, proj_b, rel_pos_h, rel_pos_w, ln2_w, ln2_b, fc1_w, fc1_b, fc2_w, fc2_b):
            B, H, W, C = x.shape
            shortcut = x
            xn = _ln(x, ln1_w, ln1_b)
            pad_h = -H % WS
            pad_w = -W % WS
            xp = jnp.pad(xn, ((0, 0), (0, pad_h), (0, pad_w), (0, 0)))
            Hp, Wp = (H + pad_h, W + pad_w)
            nh, nw = (Hp // WS, Wp // WS)
            xw = xp.reshape(B, nh, WS, nw, WS, C).transpose(0, 1, 3, 2, 4, 5)
            xw = xw.reshape(B * nh * nw, WS, WS, C)
            Bw = B * nh * nw
            N = WS * WS
            qkv = xw.reshape(Bw, N, C) @ qkv_w + qkv_b
            qkv = qkv.reshape(Bw, N, 3, NH, HD).transpose(2, 0, 3, 1, 4)
            q, k, v = (qkv[0], qkv[1], qkv[2])
            scale = HD ** (-0.5)
            attn = jnp.einsum('bhnd,bhmd->bhnm', q * scale, k)
            idx = jnp.arange(WS)[:, None] - jnp.arange(WS)[None, :] + (WS - 1)
            Rh = rel_pos_h[idx]
            Rw = rel_pos_w[idx]
            rq = q.reshape(Bw, NH, WS, WS, HD)
            rel_h = jnp.einsum('bnhwc,hkc->bnhwk', rq, Rh)
            rel_w = jnp.einsum('bnhwc,wkc->bnhwk', rq, Rw)
            attn = (attn.reshape(Bw, NH, WS, WS, WS, WS) + rel_h[..., :, None] + rel_w[..., None, :]).reshape(Bw, NH, N, N)
            attn = jax.nn.softmax(attn, axis=-1)
            out = jnp.einsum('bhnm,bhmd->bhnd', attn, v)
            out = out.transpose(0, 2, 1, 3).reshape(Bw, WS, WS, C)
            out = out @ proj_w + proj_b
            out = out.reshape(B, nh, nw, WS, WS, C).transpose(0, 1, 3, 2, 4, 5)
            out = out.reshape(B, Hp, Wp, C)[:, :H, :W, :]
            x = shortcut + out
            h = _ln(x, ln2_w, ln2_b)
            h = jax.nn.gelu(h @ fc1_w + fc1_b, approximate=False)
            x = x + (h @ fc2_w + fc2_b)
            return x
        key = jax.random.key(seed)
        ks = jax.random.split(key, 8)

        def n(k, shape, s=0.02):
            return jax.random.normal(k, shape, jnp.float32) * s
        return {'x': jax.random.normal(ks[0], (4, 16, 16, DIM), jnp.float32), 'ln1_w': jnp.ones((DIM,), jnp.float32), 'ln1_b': jnp.zeros((DIM,), jnp.float32), 'qkv_w': n(ks[1], (DIM, 3 * DIM)), 'qkv_b': jnp.zeros((3 * DIM,), jnp.float32), 'proj_w': n(ks[2], (DIM, DIM)), 'proj_b': jnp.zeros((DIM,), jnp.float32), 'rel_pos_h': n(ks[3], (2 * WS - 1, HD)), 'rel_pos_w': n(ks[4], (2 * WS - 1, HD)), 'ln2_w': jnp.ones((DIM,), jnp.float32), 'ln2_b': jnp.zeros((DIM,), jnp.float32), 'fc1_w': n(ks[5], (DIM, 4 * DIM)), 'fc1_b': jnp.zeros((4 * DIM,), jnp.float32), 'fc2_w': n(ks[6], (4 * DIM, DIM)), 'fc2_b': jnp.zeros((DIM,), jnp.float32)}
    _L1_conv_all = _L1_conv_setup()
    _L1_conv_in = {k: v for k, v in _L1_conv_all.items() if k in ('ln1_w', 'ln1_b', 'qkv_w', 'qkv_b', 'proj_w', 'proj_b', 'rel_pos_h', 'rel_pos_w', 'ln2_w', 'ln2_b', 'fc1_w', 'fc1_b', 'fc2_w', 'fc2_b')}
    del _L1_conv_all
    return {'x': x, 'L0_conv_rope_2d': _L0_conv_in['rope_2d'], 'L0_conv_ln1_g': _L0_conv_in['ln1_g'], 'L0_conv_ln1_b': _L0_conv_in['ln1_b'], 'L0_conv_w_qkv': _L0_conv_in['w_qkv'], 'L0_conv_b_qkv': _L0_conv_in['b_qkv'], 'L0_conv_w_proj': _L0_conv_in['w_proj'], 'L0_conv_b_proj': _L0_conv_in['b_proj'], 'L0_conv_gamma_1': _L0_conv_in['gamma_1'], 'L0_conv_ln2_g': _L0_conv_in['ln2_g'], 'L0_conv_ln2_b': _L0_conv_in['ln2_b'], 'L0_conv_w_fc1': _L0_conv_in['w_fc1'], 'L0_conv_b_fc1': _L0_conv_in['b_fc1'], 'L0_conv_w_fc2': _L0_conv_in['w_fc2'], 'L0_conv_b_fc2': _L0_conv_in['b_fc2'], 'L0_conv_gamma_2': _L0_conv_in['gamma_2'], 'L1_conv_ln1_w': _L1_conv_in['ln1_w'], 'L1_conv_ln1_b': _L1_conv_in['ln1_b'], 'L1_conv_qkv_w': _L1_conv_in['qkv_w'], 'L1_conv_qkv_b': _L1_conv_in['qkv_b'], 'L1_conv_proj_w': _L1_conv_in['proj_w'], 'L1_conv_proj_b': _L1_conv_in['proj_b'], 'L1_conv_rel_pos_h': _L1_conv_in['rel_pos_h'], 'L1_conv_rel_pos_w': _L1_conv_in['rel_pos_w'], 'L1_conv_ln2_w': _L1_conv_in['ln2_w'], 'L1_conv_ln2_b': _L1_conv_in['ln2_b'], 'L1_conv_fc1_w': _L1_conv_in['fc1_w'], 'L1_conv_fc1_b': _L1_conv_in['fc1_b'], 'L1_conv_fc2_w': _L1_conv_in['fc2_w'], 'L1_conv_fc2_b': _L1_conv_in['fc2_b']}

def reference(x, L0_conv_rope_2d, L0_conv_ln1_g, L0_conv_ln1_b, L0_conv_w_qkv, L0_conv_b_qkv, L0_conv_w_proj, L0_conv_b_proj, L0_conv_gamma_1, L0_conv_ln2_g, L0_conv_ln2_b, L0_conv_w_fc1, L0_conv_b_fc1, L0_conv_w_fc2, L0_conv_b_fc2, L0_conv_gamma_2, L1_conv_ln1_w, L1_conv_ln1_b, L1_conv_qkv_w, L1_conv_qkv_b, L1_conv_proj_w, L1_conv_proj_b, L1_conv_rel_pos_h, L1_conv_rel_pos_w, L1_conv_ln2_w, L1_conv_ln2_b, L1_conv_fc1_w, L1_conv_fc1_b, L1_conv_fc2_w, L1_conv_fc2_b):
    import jax
    import jax.numpy as jnp

    def _L0_conv_ref(x, rope_2d, ln1_g, ln1_b, w_qkv, b_qkv, w_proj, b_proj, gamma_1, ln2_g, ln2_b, w_fc1, b_fc1, w_fc2, b_fc2, gamma_2):
        import jax, jax.numpy as jnp
        import numpy as np
        WINDOW_SIZE = 14
        NUM_HEADS = 12
        LN_EPS = 1e-06

        def window_partition(x, ws):
            B, H, W, C = x.shape
            pad_h = -H % ws
            pad_w = -W % ws
            x = jnp.pad(x, ((0, 0), (0, pad_h), (0, pad_w), (0, 0)))
            Hp, Wp = (H + pad_h, W + pad_w)
            x = x.reshape(B, Hp // ws, ws, Wp // ws, ws, C)
            x = x.transpose(0, 1, 3, 2, 4, 5).reshape(-1, ws, ws, C)
            return (x, (Hp, Wp))

        def window_unpartition(windows, ws, pad_hw, hw):
            Hp, Wp = pad_hw
            H, W = hw
            C = windows.shape[-1]
            B = windows.shape[0] // (Hp * Wp // ws // ws)
            x = windows.reshape(B, Hp // ws, Wp // ws, ws, ws, C)
            x = x.transpose(0, 1, 3, 2, 4, 5).reshape(B, Hp, Wp, C)
            return x[:, :H, :W, :]

        def apply_rot_embed_cat(x, rope):
            d = x.shape[-1] // 2
            sin, cos = (rope[..., :d], rope[..., d:])
            x1, x2 = (x[..., :d], x[..., d:])
            return jnp.concatenate([x1 * cos - x2 * sin, x2 * cos + x1 * sin], axis=-1)

        def layer_norm(x, g, b):
            m = jnp.mean(x, axis=-1, keepdims=True)
            v = jnp.var(x, axis=-1, keepdims=True)
            return (x - m) * jax.lax.rsqrt(v + LN_EPS) * g + b

        def attention(x, rope, w_qkv, b_qkv, w_proj, b_proj):
            B, H, W, C = x.shape
            N = H * W
            hd = C // NUM_HEADS
            qkv = x.reshape(B, N, C) @ w_qkv.T + b_qkv
            qkv = qkv.reshape(B, N, 3, NUM_HEADS, hd).transpose(2, 0, 3, 1, 4)
            q, k, v = (qkv[0], qkv[1], qkv[2])
            if rope is not None:
                q = apply_rot_embed_cat(q, rope)
                k = apply_rot_embed_cat(k, rope)
            attn = jax.nn.softmax(jnp.einsum('bhqd,bhkd->bhqk', q * hd ** (-0.5), k), axis=-1)
            out = jnp.einsum('bhqk,bhkd->bhqd', attn, v)
            out = out.transpose(0, 2, 1, 3).reshape(B, H, W, C)
            return out @ w_proj.T + b_proj
        ws = WINDOW_SIZE
        B_img, H, W, C = x.shape
        shortcut = x
        h = layer_norm(x, ln1_g, ln1_b)
        h, pad_hw = window_partition(h, ws)
        rope_w, _ = window_partition(rope_2d, ws)
        rope_w = jnp.tile(rope_w, (B_img, 1, 1, 1))
        rope_w = rope_w.reshape(-1, 1, ws * ws, rope_w.shape[-1])
        h = attention(h, rope_w, w_qkv, b_qkv, w_proj, b_proj)
        h = window_unpartition(h, ws, pad_hw, (H, W))
        x = shortcut + gamma_1 * h
        shortcut = x
        h = layer_norm(x, ln2_g, ln2_b)
        h = jax.nn.gelu(h @ w_fc1.T + b_fc1, approximate=False) @ w_fc2.T + b_fc2
        return shortcut + gamma_2 * h

    def _L1_conv_ref(x, ln1_w, ln1_b, qkv_w, qkv_b, proj_w, proj_b, rel_pos_h, rel_pos_w, ln2_w, ln2_b, fc1_w, fc1_b, fc2_w, fc2_b):
        import jax, jax.numpy as jnp
        import numpy as np
        DIM = 192
        NH = 12
        HD = DIM // NH
        WS = 14
        EPS = 1e-05

        def _ln(x, w, b):
            m = jnp.mean(x, -1, keepdims=True)
            v = jnp.var(x, -1, keepdims=True)
            return (x - m) * jax.lax.rsqrt(v + EPS) * w + b

        def _block(x, ln1_w, ln1_b, qkv_w, qkv_b, proj_w, proj_b, rel_pos_h, rel_pos_w, ln2_w, ln2_b, fc1_w, fc1_b, fc2_w, fc2_b):
            B, H, W, C = x.shape
            shortcut = x
            xn = _ln(x, ln1_w, ln1_b)
            pad_h = -H % WS
            pad_w = -W % WS
            xp = jnp.pad(xn, ((0, 0), (0, pad_h), (0, pad_w), (0, 0)))
            Hp, Wp = (H + pad_h, W + pad_w)
            nh, nw = (Hp // WS, Wp // WS)
            xw = xp.reshape(B, nh, WS, nw, WS, C).transpose(0, 1, 3, 2, 4, 5)
            xw = xw.reshape(B * nh * nw, WS, WS, C)
            Bw = B * nh * nw
            N = WS * WS
            qkv = xw.reshape(Bw, N, C) @ qkv_w + qkv_b
            qkv = qkv.reshape(Bw, N, 3, NH, HD).transpose(2, 0, 3, 1, 4)
            q, k, v = (qkv[0], qkv[1], qkv[2])
            scale = HD ** (-0.5)
            attn = jnp.einsum('bhnd,bhmd->bhnm', q * scale, k)
            idx = jnp.arange(WS)[:, None] - jnp.arange(WS)[None, :] + (WS - 1)
            Rh = rel_pos_h[idx]
            Rw = rel_pos_w[idx]
            rq = q.reshape(Bw, NH, WS, WS, HD)
            rel_h = jnp.einsum('bnhwc,hkc->bnhwk', rq, Rh)
            rel_w = jnp.einsum('bnhwc,wkc->bnhwk', rq, Rw)
            attn = (attn.reshape(Bw, NH, WS, WS, WS, WS) + rel_h[..., :, None] + rel_w[..., None, :]).reshape(Bw, NH, N, N)
            attn = jax.nn.softmax(attn, axis=-1)
            out = jnp.einsum('bhnm,bhmd->bhnd', attn, v)
            out = out.transpose(0, 2, 1, 3).reshape(Bw, WS, WS, C)
            out = out @ proj_w + proj_b
            out = out.reshape(B, nh, nw, WS, WS, C).transpose(0, 1, 3, 2, 4, 5)
            out = out.reshape(B, Hp, Wp, C)[:, :H, :W, :]
            x = shortcut + out
            h = _ln(x, ln2_w, ln2_b)
            h = jax.nn.gelu(h @ fc1_w + fc1_b, approximate=False)
            x = x + (h @ fc2_w + fc2_b)
            return x
        return _block(x, ln1_w, ln1_b, qkv_w, qkv_b, proj_w, proj_b, rel_pos_h, rel_pos_w, ln2_w, ln2_b, fc1_w, fc1_b, fc2_w, fc2_b)

    def _gn(v, G=32, eps=1e-05):
        B_, H_, W_, C_ = v.shape
        g = v.reshape(B_, H_, W_, G, C_ // G)
        m = jnp.mean(g, axis=(1, 2, 4), keepdims=True)
        s = jnp.var(g, axis=(1, 2, 4), keepdims=True)
        return ((g - m) / jnp.sqrt(s + eps)).reshape(v.shape)

    def _ln_c(v, eps=1e-06):
        m = jnp.mean(v, axis=-1, keepdims=True)
        s = jnp.var(v, axis=-1, keepdims=True)
        return (v - m) / jnp.sqrt(s + eps)

    def _ln_t(v, eps=1e-05):
        m = jnp.mean(v, axis=-1, keepdims=True)
        s = jnp.var(v, axis=-1, keepdims=True)
        return (v - m) / jnp.sqrt(s + eps)

    def _to_tokens(v):
        B_, H_, W_, C_ = v.shape
        return v.reshape(B_, H_ * W_, C_)

    def _from_tokens(t, like):
        return t.reshape(like.shape)
    x = _L0_conv_ref(x, L0_conv_rope_2d, L0_conv_ln1_g, L0_conv_ln1_b, L0_conv_w_qkv, L0_conv_b_qkv, L0_conv_w_proj, L0_conv_b_proj, L0_conv_gamma_1, L0_conv_ln2_g, L0_conv_ln2_b, L0_conv_w_fc1, L0_conv_b_fc1, L0_conv_w_fc2, L0_conv_b_fc2, L0_conv_gamma_2)
    x = _L1_conv_ref(x, L1_conv_ln1_w, L1_conv_ln1_b, L1_conv_qkv_w, L1_conv_qkv_b, L1_conv_proj_w, L1_conv_proj_b, L1_conv_rel_pos_h, L1_conv_rel_pos_w, L1_conv_ln2_w, L1_conv_ln2_b, L1_conv_fc1_w, L1_conv_fc1_b, L1_conv_fc2_w, L1_conv_fc2_b)
    return x

_drawn_inputs = setup_inputs


def setup_inputs(seed=0):
    import zlib

    import numpy as np

    out = dict(_drawn_inputs(seed))
    spreads = {'L0_conv_ln1_g': (1.0, 0.6),
     'L0_conv_ln1_b': (0.0, 0.586),
     'L0_conv_b_qkv': (0.0, 0.493),
     'L0_conv_b_proj': (0.0, 0.795),
     'L0_conv_gamma_1': (0.10000000149011612, 0.6),
     'L0_conv_ln2_g': (1.0, 0.6),
     'L0_conv_ln2_b': (0.0, 0.8),
     'L0_conv_b_fc1': (0.0, 0.8),
     'L0_conv_b_fc2': (0.0, 0.8),
     'L0_conv_gamma_2': (0.10000000149011612, 0.6),
     'L1_conv_ln1_w': (1.0, 0.6),
     'L1_conv_ln1_b': (0.0, 0.8),
     'L1_conv_qkv_b': (0.0, 0.1),
     'L1_conv_proj_b': (0.0, 0.1),
     'L1_conv_ln2_w': (1.0, 0.6),
     'L1_conv_ln2_b': (0.0, 0.8),
     'L1_conv_fc1_b': (0.0, 0.284),
     'L1_conv_fc2_b': (0.0, 0.1)}
    factors = {'L1_conv_qkv_w': 6.698, 'L1_conv_rel_pos_h': 8.0, 'L1_conv_rel_pos_w': 8.0}
    for name, (base, spread) in spreads.items():
        noise = np.random.default_rng([zlib.crc32(name.encode()), seed]).standard_normal(out[name].shape)
        drawn = base * np.exp(spread * noise) if base else spread * noise
        out[name] = jnp.asarray(drawn.astype(out[name].dtype))
    for name, factor in factors.items():
        out[name] = (out[name] * factor).astype(out[name].dtype)
    return out
```

```python
from collections import namedtuple
from contextlib import ExitStack

import concourse.bass as bass
from concourse import mybir

ALU = mybir.AluOpType
ACT = mybir.ActivationFunctionType
AX = mybir.AxisListType.X
F32 = mybir.dt.float32
F32R = mybir.dt.float32r
I32 = mybir.dt.int32

B, H, W, C = 8, 16, 16, 192
NH, HD = 12, 16
WS = 14
NT = H * W
NM = WS * WS
NE = NT - NM
CH = NM // 2
NV = 4
NK = NT + NV
EK = NE + NV
ND = NM + 2 * EK
SB = NM + EK
F = 4 * C
MT = F // 128
PAIRS = NH // 2
NG = 2 * WS + 1
E0 = NM - 128
HP = 96
BIG = 1.0e30
EPS1 = (1e-6, 1e-5)
KSCALE = float(HD) ** -0.5

KQ_ACT, KQ_DVE = "act", "dve"
KQ_ENGINE = (
    {"k0": KQ_ACT, "k1": KQ_DVE, "k2": KQ_ACT, "q0": KQ_DVE, "q1": KQ_ACT, "q2": KQ_ACT},
    {"k0": KQ_ACT, "k1": KQ_DVE, "k2": KQ_ACT, "q0": KQ_DVE, "q1": KQ_ACT, "q2": KQ_ACT,
     "q3": KQ_DVE, "q4": KQ_ACT, "q5": KQ_ACT},
)


Block = namedtuple("Block", "wqkv w1 wproj w2 ln bqkv bproj b2 b1 gamma1 gamma2 rbd")


def build(nc, x, rope_cos, rope_sin, layers, consts, out):
    ctx = ExitStack()
    with ctx:
        def sb(name, shape, dt=F32):
            return ctx.enter_context(nc.sbuf_tensor(name, shape, dt))

        def sem(name):
            return ctx.enter_context(nc.semaphore(name))

        ps = ctx.enter_context(nc.psum_tensor("ps", [128, 8, 512], F32))
        S_BANK, ST_BANK, O_BANK, MISC = 0, 2, 4, 6

        X = sb("X", [128, 2 * B, C])
        XB = sb("XB", [128, 2, C])
        xn = sb("xn", [128, 2, C + 64])
        stats = sb("stats", [128, 2, 6])
        mv = sb("mv", [128, 2, 2])
        veps = sb("veps", [128, 2])
        rstd = sb("rstd", [128, 2])
        nhalf = sb("nhalf", [128, 2])
        XH = sb("XH", [128, 2, ND], F32R)
        XL = sb("XL", [128, ND], F32R)
        WQ = sb("WQ", [128, 4, 3 * C], F32R)
        WF = [sb(f"WF{l}", [128, 4, F], F32R) for l in range(2)]
        WP = [sb(f"WP{l}", [HP, 2, C]) for l in range(2)]
        W2 = [sb(f"W2{l}", [128, MT, C]) for l in range(2)]
        b_qkv = [sb(f"b_qkv{l}", [128, 3 * C]) for l in range(2)]
        b_v0 = [sb(f"b_v0{l}", [128, 2 * C]) for l in range(2)]
        b_p = [sb(f"b_p{l}", [128, C]) for l in range(2)]
        b_2 = [sb(f"b_2{l}", [128, C]) for l in range(2)]
        b_1 = [sb(f"b_1{l}", [128, MT]) for l in range(2)]
        gam = sb("gam", [128, 2, C])
        lnp = sb("lnp", [128, 2, 4])
        g4 = sb("g4", [128, 2])
        lnb_w = sb("lnb_w", [128, 2, 2, 128])
        raw = sb("raw", [128, 2, 3 * C + F])
        ident = sb("ident", [128, 128])
        sel = sb("sel", [128, NH, CH], F32R)
        cos_t = sb("cos_t", [128, 2, HD])
        sin_t = sb("sin_t", [128, 2, HD])
        padq = sb("padq", [128, 2, 16])
        padk = sb("padk", [128, 3, 16])
        kvirt = sb("kvirt", [128, NH, NV])
        hot = sb("hot", [128, NK])
        vcon = sb("vcon", [128, 2, 2, 2])
        shm = sb("shm", [128, 4, 4], I32)
        Rbd = sb("Rbd", [HP, 6 * 2 * NG])
        QK = sb("QK", [128, 2, 2 * C])
        QKab = sb("QKab", [128, 4, 2 * C])
        QKa, QKb = QKab[:, 0:2, :], QKab[:, 2:4, :]
        QS = sb("QS", [128, 2, NH, 128], F32R)
        QS0 = QS[:, :, 0:PAIRS, :].rearrange("p t m (s d) -> p t (m s) d", s=2)
        KS = sb("KS", [128, 2, NH, 64], F32R)
        QT = [sb(f"QT{p}", [128, NH, NT], F32R) for p in range(2)]
        KM = [sb(f"KM{p}", [128, NH, NK], F32R) for p in range(2)]
        V01 = [sb(f"V01{p}", [CH, 2, NH, 32]) for p in range(2)]
        VE = [sb(f"VE{p}", [128, PAIRS, 64]) for p in range(2)]
        mneg = sb("mneg", [128, 2, 128])
        mT = [sb(f"mT{p}", [128, NT], F32R) for p in range(2)]
        PTb = sb("PTb", [128, 4 * 2 * NM])
        PT = PTb[0:CH, :].rearrange("p (s n) -> p s n", s=4)
        EL = sb("EL", [128, NH, EK])
        PE_ = sb("PE_", [128, NH, EK])
        PET = [sb(f"PET{p}", [128, PAIRS, NE]) for p in range(2)]
        OT = sb("OT", [128, 3, NT])
        rden = sb("rden", [128, 2, NH])
        ON = sb("ON", [128, 2, C])
        ONT = sb("ONT", [HP, 2, NT])
        rawf = raw[:].rearrange("p r n -> p (r n)")
        nG = 4 * NH * NG
        G = rawf[:, 0:nG].rearrange("p (a h j) -> p a h j", a=4, h=NH)
        QF = rawf[0:HP, nG:nG + 2 * NT].rearrange("p (f t) -> p f t", f=2)
        at = nG + 2 * NT
        DX = rawf[:, at:at + 2 * NH * WS].rearrange("p (a h j) -> p a h j", a=2, h=NH)
        at += 2 * NH * WS
        Mx = rawf[:, at:at + 4 * NH].rearrange("p (k a h) -> p k a h", k=2, a=2)
        SX = rawf[:, at + 4 * NH:at + 8 * NH].rearrange("p (k a h) -> p k a h", k=2, a=2)
        at += 8 * NH
        Mr = rawf[:, at:at + 3 * NH].rearrange("p (h r) -> p h r", r=3)
        Wr = rawf[:, at + 3 * NH:at + 6 * NH].rearrange("p (h r) -> p h r", r=3)
        KB = EL[0:4, :, :]
        GT = [PTb[:, 0:MT * NT].rearrange("p (m t) -> p m t", m=MT),
              QKab[:].rearrange("p a n -> p (a n)").rearrange("p (m t) -> p m t", m=MT)]
        Y = [OT[:].rearrange("p k t -> p (k t)")[:, 2 * C * p:2 * C * p + 2 * C].rearrange("p (t c) -> p t c", t=2)
             for p in range(2)]

        def events(prefix, names):
            return namedtuple(prefix, names)(*[sem(f"{prefix}_{n}") for n in names.split()])

        ATT = ("stats aggr veps rstd xn xT xh xl xd qkmm qk vmm v01 ve "
               "t1 t2 qkr hi lo kqT kq_act kq_dve "
               "smm mneg esub mTmm mT eexp eTmm pet "
               "stmm pexp av ave ot oTmm rden on onTmm ont proj xb x1")
        REL = "qfT qf gmm g sh rmax rsub rexp rsum rmul qrel ew"
        E = [events("a0", ATT), events("a1", ATT + " " + REL)]
        M = [events(f"m{l}", "stats aggr veps rstd xn xT xh xl f1 gelu f2 xb y") for l in range(2)]
        x_in, c_in = sem("x_in"), sem("c_in")
        store = [sem(f"store{p}") for p in range(2)]
        w_in = [sem(f"w_in{l}") for l in range(2)]
        ready_setup = sem("ready_setup")
        s_dve, s_pe = sem("s_dve"), sem("s_pe")
        phase = sem("phase")

        def prep_uses(l):
            rel = ["qf", "g0", "g1", "g2", "g3"] if l else []
            return ["x", "qk0", "qk1", "v01", "ve"] + rel + list(KQ_ENGINE[l])

        def turns(l):
            order = [(u, 0) for u in prep_uses(l)] + [(u, 0) for u in ("m", "e0", "e1")]
            for i in range(B):
                if i + 1 < B:
                    order += [(u, i + 1) for u in prep_uses(l)]
                order += [(u, i) for u in ("o0", "o1", "on", "pr")]
                if i + 1 < B:
                    order += [(u, i + 1) for u in ("m", "e0", "e1")]
            return order

        ORDER = [turns(l) for l in range(2)]
        TURN = [{u: n for n, u in enumerate(o)} for o in ORDER]

        def kq_count(l, u, i):
            mine = [n for n, e in KQ_ENGINE[l].items() if e == KQ_ENGINE[l][u]]
            return len(mine) * i + mine.index(u) + 1

        def misc_emptied(l, u, i):
            e = E[l]
            if u in KQ_ENGINE[l]:
                return (e.kq_act if KQ_ENGINE[l][u] == KQ_ACT else e.kq_dve), kq_count(l, u, i)
            if u[0] == "g":
                return e.g, 4 * i + int(u[1]) + 1
            return {"x": (e.xl, i + 1), "qk0": (e.qk, 2 * i + 1), "qk1": (e.qk, 2 * i + 2),
                    "v01": (e.v01, i + 1), "ve": (e.ve, i + 1),
                    "qf": (e.qf if l else None, i + 1),
                    "m": (e.mT, i + 1), "e0": (e.pet, 2 * i + 1), "e1": (e.pet, 2 * i + 2),
                    "o0": (e.on, 2 * i + 1), "o1": (e.on, 2 * i + 2), "on": (e.ont, i + 1),
                    "pr": (e.x1, i + 1)}[u]

        def misc(l, u, i):
            return ps[:, MISC + TURN[l][u, i] % 2, :]

        def wait_misc_free(pe, l, u, i):
            n = TURN[l][u, i]
            if n >= 2:
                s, v = misc_emptied(l, *ORDER[l][n - 2])
                pe.wait_ge(s, v)

        def evacuate(l, i, which, copy, eng, done):
            e, p = E[l], i % 2
            names = list(KQ_ENGINE[l])
            if i >= 2:
                eng.wait_ge(e.stmm, NH * (i - 1))
            for n, u in enumerate(names):
                if KQ_ENGINE[l][u] != which:
                    continue
                eng.wait_ge(e.kqT, len(names) * i + n + 1)
                bank = misc(l, u, i).rearrange("p (m t) -> p m t", m=2)
                j = int(u[1])
                if u[0] == "q":
                    copy(QT[p][:, 2 * j:2 * j + 2, :], bank).then_inc(done, 1)
                else:
                    odd = slice(64, 128) if l == 0 else slice(0, 64)
                    copy(KM[p][0:64, 4 * j:4 * j + 3:2, 0:NT], bank[0:64])
                    copy(KM[p][odd, 4 * j + 1:4 * j + 4:2, 0:NT], bank[64:128]).then_inc(done, 1)

        def heads(ap, n=NH):
            return ap.rearrange("p (h d) -> p h d", h=n)

        block = ctx.enter_context(nc.Block())

        PIECES = [
            (0, 0, (0, 9), (0, WS)),
            (0, 126, (9, 10), (0, 2)),
            (1, 0, (9, 10), (2, WS)),
            (1, 12, (10, WS), (0, WS)),
            (1, E0, (0, WS), (WS, W)),
            (1, E0 + 28, (WS, H), (0, W)),
        ]

        def piece_dram(t, b0, b1, rows, cols):
            return t[b0:b1, rows[0]:rows[1], cols[0]:cols[1], :].rearrange("b h w c -> h w b c")

        def piece_size(rows, cols):
            return (rows[1] - rows[0]) * (cols[1] - cols[0])

        @block.sync
        def _(sp):
            n_x = 0
            for b0 in range(B):
                for t, p0, rows, cols in PIECES:
                    n = piece_size(rows, cols)
                    sp.dma_start(X[p0:p0 + n, 2 * b0 + t, :], x[b0, rows[0]:rows[1], cols[0]:cols[1], :])\
                        .then_inc(x_in, 16)
                if b0 == 0:
                    for dst, src in ((ident[:], consts["ident"]), (padq[:], consts["padq"]),
                                     (padk[:], consts["padk"]), (cos_t[:], rope_cos), (sin_t[:], rope_sin),
                                     (vcon[:], consts["vcon"]), (kvirt[:], consts["kvirt"]),
                                     (hot[64:128, :], consts["hot"]), (shm[:], consts["shm"]),
                                     (Rbd[:], layers[1].rbd), (gam[:, 0, :], layers[0].gamma1),
                                     (gam[:, 1, :], layers[0].gamma2)):
                        sp.dma_start(dst, src).then_inc(c_in, 16)
            for i in range(B):
                sp.wait_ge(M[1].y, i + 1)
                for t, p0, rows, cols in PIECES:
                    n = piece_size(rows, cols)
                    sp.dma_start(out[i, rows[0]:rows[1], cols[0]:cols[1], :], Y[i % 2][p0:p0 + n, t, :])\
                        .then_inc(store[i % 2], 16)
            for p in range(2):
                sp.wait_ge(store[p], 16 * len(PIECES) * B // 2)

        N_CONST = 12 * 16

        def weight_loads(q, l):
            ly = layers[l]
            if l == 1:
                q.wait_ge(s_dve, setup_count("raw", 0))
                q.wait_ge(s_pe, 1)
            for dst, src in ((raw[:, 0, 0:3 * C], ly.wqkv[0:128, :]), (raw[0:64, 1, 0:3 * C], ly.wqkv[128:C, :]),
                             (raw[64:128, 1, 0:3 * C], ly.wqkv[128:C, :]),
                             (raw[:, 0, 3 * C:], ly.w1[0:128, :]), (raw[0:64, 1, 3 * C:], ly.w1[128:C, :]),
                             (raw[64:128, 1, 3 * C:], ly.w1[128:C, :]),
                             (lnp[:], ly.ln),
                             (WP[l][:], ly.wproj), (W2[l][:], ly.w2),
                             (b_qkv[l][:], ly.bqkv), (b_v0[l][:], ly.bqkv[:, C:]), (b_p[l][:], ly.bproj),
                             (b_2[l][:], ly.b2), (b_1[l][:], ly.b1)):
                q.dma_start(dst, src).then_inc(w_in[l], 16)

        N_W = 14 * 16

        SETUP_DVE = ["consts"] + [f"{n}{l}" for l in range(2) for n in ("lnbw", "raw", "bias")] + ["bare1"]

        def setup_count(name, l):
            return SETUP_DVE.index(name if l is None else f"{name}{l}") + 1

        @block.vector
        def _(dve):
            v = nc.vector

            def chain(ins, count=[0]):
                count[0] += 1
                ins.then_inc(ready_setup, 1)
                dve.wait_ge(ready_setup, count[0])

            v.memset(mneg[:], 0.0)
            v.memset(nhalf[:], -0.5)
            v.memset(XH[:].bitcast(F32), 0.0)
            v.memset(XL[:].bitcast(F32), 0.0)
            v.memset(PTb[:], 0.0)
            for p in range(2):
                v.memset(VE[p][:], 0.0)
                v.memset(V01[p][:], 0.0)
            for p in range(2):
                v.memset(KM[p][:].bitcast(F32), 0.0)
            v.memset(QS[:].bitcast(F32), 0.0)
            chain(v.memset(KS[:].bitcast(F32), 0.0))
            for p in range(2):
                chain(v.memset(V01[p][:, :, :, HD:HD + 1], 1.0))
            dve.wait_ge(c_in, N_CONST)
            for t in range(2):
                v.tensor_copy(QS0[:, t, :, 48:64], padq[:, t:t + 1, :].broadcast_to([128, NH, 16]))
                v.tensor_copy(KS[:, t, :, 48:64], padk[:, t:t + 1, :].broadcast_to([128, NH, 16]))
            for h in range(NH):
                v.tensor_copy(sel[:, h, :], ident[:, h:h + 1].broadcast_to([128, CH]))
            for p in range(2):
                v.tensor_copy(KM[p][:, :, NT:NK], kvirt[:])
            chain(v.tensor_scalar(sin_t[:, :, 0:HD // 2], sin_t[:, :, 0:HD // 2], -1.0, None, ALU.mult))
            dve.drain().then_inc(s_dve, 1)

            def weights(l):
                dve.wait_ge(w_in[l], N_W)
                for k in range(2):
                    for r in range(2):
                        last = v.tensor_copy(lnb_w[:, k, r, :], lnp[:, r, 1 + 2 * k:2 + 2 * k].broadcast_to([128, 128]))
                last.then_inc(s_dve, 1)
                chain(v.tensor_scalar(g4[:], lnp[:, :, 0], KSCALE, None, ALU.mult))
                for r in range(2):
                    for k, dst, w0, n, g in ((0, WQ, 0, C, lnp[:, r, 0:1]), (0, WQ, C, C, g4[:, r:r + 1]),
                                             (0, WQ, 2 * C, C, lnp[:, r, 0:1]),
                                             (1, WF[l], 0, F, lnp[:, r, 2:3])):
                        src = raw[:, r, 3 * C * k + w0:3 * C * k + w0 + n]
                        chain(v.tensor_scalar(dst[:, 2 * r, w0:w0 + n], src, g, None, ALU.mult))
                        v.scalar_tensor_tensor(dst[:, 2 * r + 1, w0:w0 + n], src, g, dst[:, 2 * r, w0:w0 + n].bitcast(F32),
                                               ALU.mult, ALU.subtract)
                dve.drain().then_inc(s_dve, 1)
                if l == 0:
                    chain(v.tensor_tensor(WP[l][:], WP[l][:], gam[0:HP, 0:1, :].broadcast_to([HP, 2, C]), ALU.mult))
                    chain(v.tensor_tensor(W2[l][:], W2[l][:], gam[:, 1:2, :].broadcast_to([128, MT, C]), ALU.mult))
                    chain(v.tensor_tensor(b_p[l][:], b_p[l][:], gam[:, 0, :], ALU.mult))
                    chain(v.tensor_tensor(b_2[l][:], b_2[l][:], gam[:, 1, :], ALU.mult))
                dve.wait_ge(s_pe, l + 1)
                chain(v.tensor_tensor(b_qkv[l][:, 0:2 * C], ps[:, 4, 0:2 * C], b_qkv[l][:, 0:2 * C], ALU.add))
                chain(v.tensor_tensor(b_qkv[l][:, 2 * C:], ps[:, 5, 0:C], b_qkv[l][:, 2 * C:], ALU.add))
                chain(v.tensor_scalar(b_qkv[l][:, C:2 * C], b_qkv[l][:, C:2 * C], KSCALE, None, ALU.mult))
                chain(v.tensor_scalar(b_v0[l][:, 0:C], b_v0[l][:, 0:C], KSCALE, None, ALU.mult))
                v.tensor_tensor(b_1[l][:], ps[:, 4, 2 * C:2 * C + MT], b_1[l][:], ALU.add).then_inc(s_dve, 1)

            def virtual_values(l):
                for p in range(2):
                    for k in range(2):
                        dst = VE[p][:, :, 32 * k:32 * k + HD]
                        src = b_v0[l][:, C:].rearrange("p (m k d) -> p m k d", k=2, d=HD)[:, :, k, :]
                        chain(v.tensor_scalar(dst, src, vcon[:, l, k, 0:1], None, ALU.mult))
                        chain(v.tensor_copy(VE[p][:, :, 32 * k + HD:32 * k + HD + 1],
                                      vcon[:, l, k, 1:2].unsqueeze(1).broadcast_to([128, PAIRS, 1])))

            def layer_norm(e, i, mlp):
                for t in range(2):
                    last = v.bn_stats(stats[:, t, :], X[:, 2 * i + t, :])
                last.then_inc(e.stats, 1)
                dve.wait_ge(e.stats, i + 1)
                if i >= 1:
                    dve.wait_ge(e.veps, i)
                for t in range(2):
                    last = v.bn_aggr(mv[:, t, :], stats[:, t, :])
                last.then_inc(e.aggr, 1)
                dve.wait_ge(e.rstd, i + 1)
                if i >= 1:
                    dve.wait_ge(e.xT, i)
                for t in range(2):
                    for dst, c0 in ((xn[:, t, 0:C], 0), (xn[:, t, C:C + 64], 128)):
                        last = v.tensor_scalar(dst, X[:, 2 * i + t, c0:C], mv[:, t, 0:1], rstd[:, t:t + 1],
                                               ALU.subtract, ALU.mult)
                last.then_inc(e.xn, 1)

            def split_low(e, i, bank):
                dve.wait_ge(e.xh, i + 1)
                v.tensor_tensor(XL[:, 0:NT], bank[:, 0:NT], XH[:, 0, 0:NT].bitcast(F32), ALU.subtract)
                v.tensor_tensor(XH[64:128, 1, 0:NT], bank[64:128, NT:2 * NT], XH[64:128, 1, 0:NT].bitcast(F32),
                                ALU.subtract).then_inc(e.xl, 1)

            def prep(l, i):
                e, p = E[l], i % 2
                split_low(e, i, misc(l, "x", i))
                for t in range(2):
                    dve.wait_ge(e.qkmm, 2 * i + t + 1)
                    if i >= 1 and t == 0:
                        if l == 0:
                            dve.wait_ge(e.t2, 2 * i)
                        else:
                            dve.wait_ge(e.hi, i)
                            dve.wait_ge(e.qfT, i)
                    v.tensor_tensor(QK[:, t, :], misc(l, f"qk{t}", i)[:, 0:2 * C], b_qkv[l][:, 0:2 * C],
                                    ALU.add).then_inc(e.qk, 1)
                if l == 0:
                    dve.wait_ge(e.qk, 2 * i + 2)
                    if i >= 1:
                        dve.wait_ge(e.hi, i)
                        dve.wait_ge(e.lo, i)
                    for t in range(2):
                        last = v.tensor_tensor(heads(QKa[:, t, :], 2 * NH), heads(QK[:, t, :], 2 * NH),
                                               cos_t[:, t:t + 1, :].broadcast_to([128, 2 * NH, HD]), ALU.mult)
                    last.then_inc(e.t1, 1)
                dve.wait_ge(e.vmm, 2 * i + 1)
                if i >= 2:
                    dve.wait_ge(e.av, NH * (i - 1))
                    dve.wait_ge(e.ave, PAIRS * (i - 1))
                bv = b_qkv[l][:, 2 * C:]
                for c in range(2):
                    last = v.tensor_tensor(V01[p][:, c, :, 0:HD], heads(misc(l, "v01", i)[0:CH, C * c:C * c + C]),
                                           heads(bv[0:CH, :]), ALU.add)
                last.then_inc(e.v01, 1)
                dve.wait_ge(e.vmm, 2 * i + 2)
                for k in range(2):
                    r = slice(64 * k, 64 * k + NE)
                    last = v.tensor_tensor(
                        VE[p][r, :, 32 * k:32 * k + HD],
                        misc(l, "ve", i)[r, 0:C].rearrange("p (m k d) -> p m k d", k=2, d=HD)[:, :, k, :],
                        bv[r, :].rearrange("p (m k d) -> p m k d", k=2, d=HD)[:, :, k, :], ALU.add)
                last.then_inc(e.ve, 1)
                if l == 0:
                    dve.wait_ge(e.t1, i + 1)
                    dve.wait_ge(e.t2, 2 * i + 2)
                    v.tensor_tensor(QKa, QKa, QKb, ALU.add).then_inc(e.qkr, 1)
                    src, qs = QKa, QS0
                else:
                    src, qs = QK, QS
                    relative(i)
                dve.wait_ge(e.hi, i + 1)
                for t in range(2):
                    v.tensor_tensor(qs[:, t, :, 16:32], heads(src[:, t, 0:C]), qs[:, t, :, 0:16].bitcast(F32), ALU.subtract)
                    last = v.tensor_tensor(KS[:, t, :, 32:48], heads(src[:, t, C:]), KS[:, t, :, 0:16].bitcast(F32),
                                           ALU.subtract)
                    if l == 1:
                        last = v.tensor_tensor(
                            qs[:, t, :, 96:96 + 2 * WS].rearrange("p h (a j) -> p a h j", a=2),
                            G[:, 2 * t:2 * t + 2, :, 0:WS],
                            qs[:, t, :, 64:64 + 2 * WS].bitcast(F32).rearrange("p h (a j) -> p a h j", a=2), ALU.subtract)
                if l == 1:
                    last = v.tensor_tensor(qs[:, 1, :, 124:127], Mr, qs[:, 1, :, 92:95].bitcast(F32), ALU.subtract)
                last.then_inc(e.lo, 1)
                evacuate(l, i, KQ_DVE, v.tensor_copy, dve, e.kq_dve)

            def relative(i):
                e = E[1]
                n = 6 * i
                dve.wait_ge(e.g, 4 * i + 4)
                for k, (s, w) in enumerate(((8, 21), (4, 17), (2, 15), (1, WS))):
                    if k:
                        dve.wait_ge(e.sh, 4 * i + k)
                    v.copy_predicated(G[:, :, :, 0:w], shm[:, :, k:k + 1].unsqueeze(2).broadcast_to([128, 4, NH, w]),
                                      G[:, :, :, s:s + w]).then_inc(e.sh, 1)
                dve.wait_ge(e.sh, 4 * i + 4)
                T1 = G[:, 2:4, :, 0:WS]
                v.tensor_reduce(Mx[:, 0, :, :], T1[:, :, :, 0:2], AX, ALU.max)
                v.tensor_reduce(Mx[:, 1, :, :], T1[:, :, :, 2:WS], AX, ALU.max).then_inc(e.rmax, 1)
                dve.wait_ge(e.rmax, i + 1)
                for k, (a, b) in enumerate(((0, 2), (2, WS))):
                    last = v.tensor_tensor(DX[:, :, :, a:b], T1[:, :, :, a:b],
                                           Mx[:, k, :, :].unsqueeze(3).broadcast_to([128, 2, NH, b - a]), ALU.subtract)
                for r, (a, b) in enumerate(((1, 1), (0, 1), (1, 0))):
                    last = v.tensor_tensor(Mr[:, :, r], Mx[:, a, 0, :], Mx[:, b, 1, :], ALU.add)
                last.then_inc(e.rsub, 1)
                dve.wait_ge(e.rsub, i + 1)
                if i >= 1:
                    dve.wait_ge(e.kqT, len(KQ_ENGINE[1]) * i)
                v.tensor_copy(QS[:, 1, :, 92:95], Mr).then_inc(e.qrel, 1)
                dve.wait_ge(e.rexp, i + 1)
                v.tensor_reduce(SX[:, 0, :, :], DX[:, :, :, 0:2], AX, ALU.add)
                v.tensor_reduce(SX[:, 1, :, :], DX[:, :, :, 2:WS], AX, ALU.add).then_inc(e.rsum, 1)
                dve.wait_ge(e.rsum, i + 1)
                for r, (a, b) in enumerate(((1, 1), (0, 1), (1, 0))):
                    last = v.tensor_tensor(Wr[:, :, r], SX[:, a, 0, :], SX[:, b, 1, :], ALU.mult)
                last.then_inc(e.rmul, 1)
                dve.wait_ge(e.qrel, i + 1)

            def head_max(l, i, h):
                e = E[l]
                dve.wait_ge(e.smm, NH * i + h + 1)
                if i >= 1 and h == 0:
                    dve.wait_ge(e.mTmm, i)
                bank = ps[:, S_BANK + h % 2, :]
                v.tensor_reduce(mneg[:, 0, h:h + 1], bank[:, 0:NM], AX, ALU.max, negate=True)
                v.tensor_reduce(mneg[:, 1, h:h + 1], bank[:, NM:NM + SB], AX, ALU.max, negate=True)\
                    .then_inc(e.mneg, 1)

            def edge_sub(l, i, h):
                e = E[l]
                dve.wait_ge(e.mneg, NH * i + h + 1)
                if i >= 1 and h == 0:
                    dve.wait_ge(e.eexp, i)
                bank = ps[:, S_BANK + h % 2, :]
                v.tensor_scalar(EL[:, h, :], bank[:, 2 * NM:2 * NM + EK], mneg[:, 1, h:h + 1], None, ALU.add)\
                    .then_inc(e.esub, 1)

            def normalise(l, i, t):
                e = E[l]
                dve.wait_ge(e.oTmm, 2 * i + t + 1)
                o = misc(l, f"o{t}", i)[:, 0:32 * NH].rearrange("p (h d) -> p h d", d=32)
                v.reciprocal(rden[:, t, :], o[:, :, HD]).then_inc(e.rden, 1)
                dve.wait_ge(e.rden, 2 * i + t + 1)
                if i >= 1:
                    dve.wait_ge(e.onTmm, i)
                v.tensor_tensor(heads(ON[:, t, :]), o[:, :, 0:HD],
                                rden[:, t, :].unsqueeze(2).broadcast_to([128, NH, HD]), ALU.mult).then_inc(e.on, 1)

            def residual(l, i):
                e = E[l]
                dve.wait_ge(e.proj, i + 1)
                dve.wait_ge(e.xb, i + 1)
                v.tensor_tensor(X[:, 2 * i:2 * i + 2, :], misc(l, "pr", i)[:, 0:2 * C].rearrange("p (t c) -> p t c", t=2),
                                XB[:], ALU.add).then_inc(e.x1, 1)

            def edge_weights(i):
                e = E[1]
                dve.wait_ge(e.eexp, i + 1)
                v.tensor_tensor(PE_[:, :, NE:NE + 3], PE_[:, :, NE:NE + 3], Wr, ALU.mult).then_inc(e.ew, 1)

            def attention(l):
                def scores(i, after):
                    for h in range(NH):
                        head_max(l, i, h)
                        if h:
                            edge_sub(l, i, h - 1)
                        if after is not None:
                            if h == 4:
                                normalise(l, after, 0)
                                normalise(l, after, 1)
                            if h == 9:
                                residual(l, after)
                    edge_sub(l, i, NH - 1)
                    if l:
                        edge_weights(i)

                layer_norm(E[l], 0, False)
                prep(l, 0)
                layer_norm(E[l], 1, False)
                scores(0, None)
                for i in range(B):
                    if i + 1 < B:
                        prep(l, i + 1)
                        if i + 2 < B:
                            layer_norm(E[l], i + 2, False)
                        scores(i + 1, i)
                    else:
                        normalise(l, i, 0)
                        normalise(l, i, 1)
                        residual(l, i)

            def mlp(l):
                m = M[l]
                layer_norm(m, 0, True)
                split_low(m, 0, ps[:, 7, :])
                layer_norm(m, 1, True)
                for i in range(B):
                    if i + 1 < B:
                        split_low(m, i + 1, ps[:, 7, :])
                    if i + 2 < B:
                        layer_norm(m, i + 2, True)
                    dve.wait_ge(m.f2, i + 1)
                    dve.wait_ge(m.xb, i + 1)
                    o = ps[:, 6, 0:2 * C].rearrange("p (t c) -> p t c", t=2)
                    if l == 0:
                        v.tensor_tensor(X[:, 2 * i:2 * i + 2, :], o, XB[:], ALU.add).then_inc(m.y, 1)
                    else:
                        if i >= 2:
                            dve.wait_ge(store[i % 2], 16 * len(PIECES) * (i // 2))
                        v.tensor_tensor(Y[i % 2], o, XB[:], ALU.add).then_inc(m.y, 1)

            def bare_keys():
                bk = heads(b_v0[1][0:4, 0:C])
                for k in range(2):
                    chain(v.tensor_copy(KB[:, :, 16 * k:16 * k + 16].bitcast(F32R), bk))
                v.tensor_tensor(KB[:, :, 32:48].bitcast(F32R), bk, KB[:, :, 0:16], ALU.subtract)
                v.tensor_copy(KB[:, :, 48:64], padk[0:4, 2:3, :].broadcast_to([4, NH, 16]))
                dve.drain().then_inc(s_dve, 1)
                for p in range(2):
                    v.tensor_copy(KM[p][64:128, :, :], hot[64:128, :].unsqueeze(1).broadcast_to([64, NH, NK]))
                dve.wait_ge(s_pe, 3)
                bank = ps[:, 5, 0:PAIRS * NV].rearrange("p (m k) -> p m k", m=PAIRS)
                for p in range(2):
                    v.tensor_copy(KM[p][0:64, 0:NH:2, NT:NK], bank[0:64])
                    v.tensor_copy(KM[p][0:64, 1:NH:2, NT:NK], bank[64:128])

            weights(0)
            virtual_values(0)
            dve.wait_ge(x_in, 16 * len(PIECES) * B)
            dve.drain().then_inc(phase, 1)
            for l in range(2):
                dve.wait_ge(phase, 4 * (2 * l + 1))
                attention(l)
                dve.drain().then_inc(phase, 1)
                dve.wait_ge(phase, 4 * (2 * l + 2))
                if l == 0:
                    weights(1)
                    for p in range(2):
                        chain(v.memset(VE[p][:], 0.0))
                    chain(v.memset(QS[:].bitcast(F32), 0.0))
                    for t in range(2):
                        v.tensor_copy(QS[:, t, :, 48:64], padq[:, t:t + 1, :].broadcast_to([128, NH, 16]))
                    virtual_values(1)
                    bare_keys()
                mlp(l)
                if l == 0:
                    dve.drain().then_inc(phase, 1)

        @block.scalar
        def _(act):
            a = nc.scalar

            def copy(dst, src):
                return a.activation(dst, src, ACT.Copy)

            def split_high(e, i, bank, used, n):
                act.wait_ge(e.xT, i + 1)
                if i >= 1:
                    act.wait_ge(used, n * i)
                copy(XH[:, :, 0:NT], bank.rearrange("p (r t) -> p r t", r=2)).then_inc(e.xh, 1)

            def stack_high(l, i):
                e = E[l]
                src, qs = (QKa, QS0) if l == 0 else (QK, QS)
                if l == 0:
                    act.wait_ge(e.qkr, i + 1)
                else:
                    act.wait_ge(e.qk, 2 * i + 2)
                    act.wait_ge(e.sh, 4 * i + 4)
                if i >= 1:
                    act.wait_ge(e.kqT, len(KQ_ENGINE[l]) * i)
                for t in range(2):
                    q = heads(src[:, t, 0:C]).unsqueeze(2).broadcast_to([128, NH, 2, HD])
                    k = heads(src[:, t, C:]).unsqueeze(2).broadcast_to([128, NH, 2, HD])
                    copy(qs[:, t, :, 0:64].rearrange("p h (s d) -> p h s d", s=2)[:, :, :, 0:HD], q)
                    last = copy(KS[:, t, :, 0:32].rearrange("p h (s d) -> p h s d", s=2), k)
                    if l == 1:
                        last = copy(qs[:, t, :, 64:64 + 2 * WS].rearrange("p h (a j) -> p a h j", a=2),
                                    G[:, 2 * t:2 * t + 2, :, 0:WS])
                last.then_inc(e.hi, 1)

            def relative_terms(i):
                e = E[1]
                act.wait_ge(e.qfT, i + 1)
                if i >= 1:
                    act.wait_ge(e.gmm, 4 * i)
                copy(QF, misc(1, "qf", i)[0:HP, :].rearrange("p (f t) -> p f t", f=2)).then_inc(e.qf, 1)
                if i >= 1:
                    act.wait_ge(e.lo, i)
                for n in range(4):
                    act.wait_ge(e.gmm, 4 * i + n + 1)
                    t, f = n // 2, n % 2
                    copy(G[:, 2 * t:2 * t + 2, 6 * f:6 * f + 6, :],
                         misc(1, f"g{n}", i)[:, 0:12 * NG].rearrange("p (h a j) -> p a h j", h=6, a=2))\
                        .then_inc(e.g, 1)

            def relative_exp(i):
                e = E[1]
                act.wait_ge(e.rsub, i + 1)
                a.activation(DX, DX, ACT.Exp).then_inc(e.rexp, 1)

            def probabilities(l, i, h):
                e = E[l]
                n = NH * i + h
                act.wait_ge(e.stmm, n + 1)
                if n >= 4:
                    act.wait_ge(e.av, n - 3)
                a.activation(PT[:, h % 4, :], ps[0:CH, ST_BANK + h % 2, 0:2 * NM], ACT.Exp).then_inc(e.pexp, 1)

            def output(l, i, part):
                e = E[l]
                act.wait_ge(e.ave, PAIRS * i + (4, 6)[part])
                if i >= 1 and part == 0:
                    act.wait_ge(e.oTmm, 2 * i)
                if part == 0:
                    copy(OT[:, 0:2, :], ps[:, O_BANK, :].rearrange("p (k t) -> p k t", k=2)).then_inc(e.ot, 1)
                else:
                    copy(OT[:, 2, :], ps[:, O_BANK + 1, 0:NT]).then_inc(e.ot, 1)

            def output_T(l, i):
                e = E[l]
                act.wait_ge(e.onTmm, i + 1)
                if i >= 1:
                    act.wait_ge(e.proj, i)
                copy(ONT[:], misc(l, "on", i)[0:HP, :].rearrange("p (f t) -> p f t", f=2)).then_inc(e.ont, 1)

            def maxima_and_edges(l, i):
                e, p = E[l], i % 2
                act.wait_ge(e.mTmm, i + 1)
                if i >= 2:
                    act.wait_ge(e.stmm, NH * (i - 1))
                copy(mT[p][:], misc(l, "m", i)[:, 0:NT]).then_inc(e.mT, 1)
                act.wait_ge(e.esub, NH * (i + 1))
                if i >= 1:
                    act.wait_ge(e.eTmm, 2 * i)
                a.activation(PE_[:], EL[:], ACT.Exp).then_inc(e.eexp, 1)
                for n, (m0, m1) in enumerate(((0, 4), (4, 6))):
                    act.wait_ge(e.eTmm, 2 * i + n + 1)
                    if i >= 2:
                        act.wait_ge(e.ave, PAIRS * (i - 1))
                    src = misc(l, f"e{n}", i)[:, 0:128 * (m1 - m0)].rearrange("p (m q) -> p m q", q=128)
                    copy(PET[p][:, m0:m1, :], src[:, :, E0:128]).then_inc(e.pet, 1)

            def attention(l):
                e = E[l]

                def prep(i):
                    split_high(e, i, misc(l, "x", i), e.vmm, 2)

                prep(0)
                if l:
                    relative_terms(0)
                    relative_exp(0)
                stack_high(l, 0)
                evacuate(l, 0, KQ_ACT, copy, act, e.kq_act)
                maxima_and_edges(l, 0)
                for i in range(B):
                    for h in range(NH):
                        probabilities(l, i, h)
                        if i + 1 < B:
                            if h == 1:
                                prep(i + 1)
                            if l and h == 5:
                                relative_terms(i + 1)
                            if l == 0 and h == 9:
                                stack_high(l, i + 1)
                        if h == 10:
                            output(l, i, 0)
                    if l and i + 1 < B:
                        stack_high(l, i + 1)
                        relative_exp(i + 1)
                    output(l, i, 1)
                    if i + 1 < B:
                        evacuate(l, i + 1, KQ_ACT, copy, act, e.kq_act)
                    output_T(l, i)
                    if i + 1 < B:
                        maxima_and_edges(l, i + 1)

            def mlp(l):
                m = M[l]
                split_high(m, 0, ps[:, 7, :], m.f1, 3)
                for i in range(B):
                    for k in range(MT):
                        n = 3 * i + k // 2
                        act.wait_ge(m.f1, n + 1)
                        if i >= 2 and k == 0:
                            act.wait_ge(m.f2, i - 1)
                        a.activation(GT[i % 2][:, k, :], ps[:, n % 4, NT * (k % 2):NT * (k % 2) + NT], ACT.Gelu,
                                     bias=b_1[l][:, k:k + 1]).then_inc(m.gelu, 1)
                    if i + 1 < B:
                        split_high(m, i + 1, ps[:, 7, :], m.f1, 3)

            act.drain().then_inc(phase, 1)
            for l in range(2):
                act.wait_ge(phase, 4 * (2 * l + 1))
                attention(l)
                act.drain().then_inc(phase, 1)
                act.wait_ge(phase, 4 * (2 * l + 2))
                if l == 0:
                    act.wait_ge(s_dve, setup_count("consts", None))
                mlp(l)
                if l == 0:
                    act.drain().then_inc(phase, 1)

        @block.gpsimd
        def _(pool):
            g = nc.gpsimd

            def inv_std(e, i, l):
                pool.wait_ge(e.aggr, i + 1)
                g.tensor_scalar(veps[:], mv[:, :, 1], EPS1[l], 1.0, ALU.add, ALU.mult).then_inc(e.veps, 1)
                pool.wait_ge(e.veps, i + 1)
                if i >= 1:
                    pool.wait_ge(e.xn, i)
                g.tensor_tensor(rstd[:], veps[:], nhalf[:], ALU.pow).then_inc(e.rstd, 1)

            def edge_copies(e, i):
                pool.wait_ge(e.xl, i + 1)
                for ap in (XH[:, 0, :], XH[:, 1, :], XL[:, :]):
                    g.tensor_scalar(ap[:, NK:NK + NE], ap[:, NM:NT].bitcast(F32), 1.0, 0.0, ALU.mult, ALU.add)\
                        .then_inc(e.xd, 1)

            def sine_half(i):
                e = E[0]
                pool.wait_ge(e.qk, 2 * i + 2)
                if i >= 1:
                    pool.wait_ge(e.qkr, i)
                half = HD // 2
                for k in range(2):
                    for t in range(2):
                        last = g.tensor_tensor(
                            heads(QKb[:, t, :], 2 * NH)[:, :, half * k:half * k + half],
                            heads(QK[:, t, :], 2 * NH)[:, :, half - half * k:HD - half * k],
                            sin_t[:, t:t + 1, half * k:half * k + half].broadcast_to([128, 2 * NH, half]), ALU.mult)
                    last.then_inc(e.t2, 1)

            def residual_bias(e, i, bias, done):
                if i >= 1:
                    pool.wait_ge(done, i)
                for t in range(2):
                    last = g.tensor_tensor(XB[:, t, :], X[:, 2 * i + t, :], bias[:], ALU.add)
                last.then_inc(e.xb, 1)

            weight_loads(pool, 0)
            weight_loads(pool, 1)
            pool.wait_ge(s_dve, setup_count("bias", 0))
            pool.wait_ge(x_in, 16 * len(PIECES) * B)
            pool.drain().then_inc(phase, 1)
            for l in range(2):
                e, m = E[l], M[l]
                pool.wait_ge(phase, 4 * (2 * l + 1))
                inv_std(e, 0, l)
                edge_copies(e, 0)
                if l == 0:
                    sine_half(0)
                inv_std(e, 1, l)
                for i in range(B):
                    if i + 1 < B:
                        edge_copies(e, i + 1)
                    if l == 0 and i + 1 < B:
                        sine_half(i + 1)
                    if i + 2 < B:
                        inv_std(e, i + 2, l)
                    residual_bias(e, i, b_p[l], e.x1)
                pool.drain().then_inc(phase, 1)
                pool.wait_ge(phase, 4 * (2 * l + 2))
                inv_std(m, 0, l)
                inv_std(m, 1, l)
                for i in range(B):
                    if i + 2 < B:
                        inv_std(m, i + 2, l)
                    residual_bias(m, i, b_2[l], m.y)
                if l == 0:
                    pool.drain().then_inc(phase, 1)

        @block.tensor
        def _(pe):
            mm = nc.tensor.matmul
            T = nc.tensor.transpose

            def fold_biases(l):
                pe.wait_ge(s_dve, setup_count("lnbw", l))
                for w0, n, o in ((0, 2 * C, ps[:, 4, 0:2 * C]), (2 * C, C, ps[:, 5, 0:C])):
                    mm(o, lnb_w[:, 0, 0, :], raw[:, 0, w0:w0 + n], start=True, stop=False)
                    mm(o, lnb_w[0:64, 0, 1, :], raw[0:64, 1, w0:w0 + n], start=False, stop=True)
                for k in range(MT):
                    w0 = 3 * C + 128 * k
                    o = ps[:, 4, 2 * C + k:2 * C + k + 1]
                    mm(o, raw[:, 0, w0:w0 + 128], lnp[:, 0, 3:4], start=True, stop=False)
                    last = mm(o, raw[0:64, 1, w0:w0 + 128], lnp[0:64, 1, 3:4], start=False, stop=True)
                last.then_inc(s_pe, 1)

            def bare_keys():
                pe.wait_ge(s_dve, setup_count("bare1", None))
                for k in range(PAIRS):
                    last = T(ps[:, 5, NV * k:NV * k + NV], KB[:, 2 * k:2 * k + 2, :], ident[0:NV, 0:NV])
                last.then_inc(s_pe, 1)

            def transpose_tokens(e, i, bank):
                pe.wait_ge(e.xn, i + 1)
                for t in range(2):
                    T(bank[:, 128 * t:128 * t + 128], xn[:, t, 0:128], ident[:])
                    last = T(bank[:, NT + 128 * t:NT + 128 * t + 128],
                             xn[:, t, 128:C + 64], ident[:])
                last.then_inc(e.xT, 1)

            def split_product(o, parts, w, flip=False):
                x0, xl, x1 = parts
                steps = ((x0, w[0]), (xl, w[0]), (x0, w[1]), (x1, w[2]), (x1, w[3]))
                for n, (x_, w_) in enumerate(steps):
                    last = mm(o, w_ if flip else x_, x_ if flip else w_, start=n == 0, stop=n == 4)
                return last

            def project_qk(l, i):
                e = E[l]
                pe.wait_ge(e.xl, i + 1)
                for t in range(2):
                    wait_misc_free(pe, l, f"qk{t}", i)
                    c = slice(128 * t, 128 * t + 128)
                    split_product(misc(l, f"qk{t}", i)[:, 0:2 * C], (XH[:, 0, c], XL[:, c], XH[:, 1, c]),
                                  [WQ[:, k, 0:2 * C] for k in range(4)]).then_inc(e.qkmm, 1)

            def project_v(l, i):
                e = E[l]
                w = [WQ[:, k, 2 * C:] for k in range(4)]
                wait_misc_free(pe, l, "v01", i)
                for n in range(2):
                    c = slice(CH * n, CH * n + CH)
                    last = split_product(misc(l, "v01", i)[0:CH, C * n:C * n + C],
                                         (XH[:, 0, c], XL[:, c], XH[:, 1, c]), w)
                last.then_inc(e.vmm, 1)
                wait_misc_free(pe, l, "ve", i)
                pe.wait_ge(e.xd, 3 * (i + 1))
                split_product(misc(l, "ve", i)[:, 0:C], (XH[:, 0, NM:ND], XL[:, NM:ND], XH[:, 1, NM:ND]), w)\
                    .then_inc(e.vmm, 1)

            def relative_products(i):
                e = E[1]
                pe.wait_ge(e.qk, 2 * i + 2)
                wait_misc_free(pe, 1, "qf", i)
                bank = misc(1, "qf", i)
                for f in range(2):
                    for t in range(2):
                        last = T(bank[0:HP, NT * f + 128 * t:NT * f + 128 * t + 128], QK[:, t, HP * f:HP * f + HP],
                                 ident[:])
                last.then_inc(e.qfT, 1)
                pe.wait_ge(e.qf, i + 1)
                for n in range(4):
                    wait_misc_free(pe, 1, f"g{n}", i)
                    t, f = n // 2, n % 2
                    mm(misc(1, f"g{n}", i)[:, 0:12 * NG], QF[:, f, 128 * t:128 * t + 128], Rbd[:],
                       start=True, stop=True).then_inc(e.gmm, 1)

            def transpose_stacks(l, i):
                e = E[l]
                pe.wait_ge(e.lo, i + 1)
                if l:
                    pe.wait_ge(e.qrel, i + 1)
                for u in KQ_ENGINE[l]:
                    wait_misc_free(pe, l, u, i)
                    j = int(u[1])
                    for m in range(2):
                        for t in range(2):
                            if u[0] == "k":
                                src = KS[:, t, 4 * j + 2 * m:4 * j + 2 * m + 2, :]
                            elif l == 0:
                                src = QS0[:, t, 4 * j + 2 * m:4 * j + 2 * m + 2, :]
                            else:
                                src = QS[:, t, 2 * j + m, :]
                            last = T(misc(l, u, i)[:, NT * m + 128 * t:NT * m + 128 * t + 128], src.bitcast(F32), ident[:])
                    last.then_inc(e.kqT, 1)

            def query(l, i, h):
                return QT[i % 2][:, h // 2 if l == 0 else h, :]

            def scores(l, i, h):
                e, p = E[l], i % 2
                n = NH * i + h
                if h == 0:
                    for u in (KQ_ACT, KQ_DVE):
                        k = list(KQ_ENGINE[l].values()).count(u)
                        pe.wait_ge(e.kq_act if u == KQ_ACT else e.kq_dve, k * (i + 1))
                if n >= 2:
                    pe.wait_ge(e.esub, n - 1)
                q = query(l, i, h)
                bank = ps[:, S_BANK + h % 2, :]
                mm(bank[:, 0:NM], q[:, 0:128], KM[p][:, h, 0:NM], start=True, stop=True)
                mm(bank[:, NM:NM + SB], q[:, 128:NT], KM[p][:, h, :], start=True, stop=True).then_inc(e.smm, 1)

            def transpose_maxima(l, i):
                e = E[l]
                pe.wait_ge(e.mneg, NH * (i + 1))
                wait_misc_free(pe, l, "m", i)
                for t in range(2):
                    last = T(misc(l, "m", i)[:, 128 * t:128 * t + 128], mneg[:, t, :], ident[:])
                last.then_inc(e.mTmm, 1)

            def transpose_edges(l, i):
                e = E[l]
                if l:
                    pe.wait_ge(e.ew, i + 1)
                else:
                    pe.wait_ge(e.eexp, i + 1)
                for n, (m0, m1) in enumerate(((0, 4), (4, 6))):
                    wait_misc_free(pe, l, f"e{n}", i)
                    for m in range(m0, m1):
                        last = T(misc(l, f"e{n}", i)[:, 128 * (m - m0):128 * (m - m0) + 128],
                                 PE_[:, 2 * m:2 * m + 2, :], ident[:])
                    last.then_inc(e.eTmm, 1)

            def scores_T(l, i, h):
                e, p = E[l], i % 2
                n = NH * i + h
                if h == 0:
                    pe.wait_ge(e.mT, i + 1)
                if n >= 2:
                    pe.wait_ge(e.pexp, n - 1)
                q = query(l, i, h)
                for c in range(2):
                    o = ps[0:CH, ST_BANK + h % 2, NM * c:NM * c + NM]
                    mm(o, KM[p][:, h, CH * c:CH * c + CH], q[:, 0:NM], start=True, stop=False)
                    last = mm(o, sel[:, h, :], mT[p][:, 0:NM], start=False, stop=True)
                last.then_inc(e.stmm, 1)

            def weighted_values(l, i, h):
                e, p = E[l], i % 2
                n = NH * i + h
                pe.wait_ge(e.pexp, n + 1)
                if h == 0:
                    pe.wait_ge(e.v01, i + 1)
                    pe.wait_ge(e.ve, i + 1)
                    pe.wait_ge(e.pet, 2 * i + 2)
                    if i >= 1:
                        pe.wait_ge(e.ot, 2 * i)
                k, j = h // 4, h % 4
                block_o = ps[:, O_BANK + k // 2, NT * (k % 2):NT * (k % 2) + NT]
                for c in range(2):
                    last = mm(block_o[32 * j:32 * j + 32, 0:NM], V01[p][:, c, h, :],
                              PT[:, h % 4, NM * c:NM * c + NM], start=c == 0, stop=c == 1)
                last.then_inc(e.av, 1)
                if h % 2:
                    m = h // 2
                    r = 64 * (m % 2)
                    mm(block_o[r:r + 64, NM:NT], VE[p][:, m, :], PET[p][:, m, :], start=True, stop=True)\
                        .then_inc(e.ave, 1)

            def transpose_output(l, i):
                e = E[l]
                pe.wait_ge(e.ot, 2 * i + 2)
                for t in range(2):
                    wait_misc_free(pe, l, f"o{t}", i)
                    for k in range(3):
                        last = T(misc(l, f"o{t}", i)[:, 128 * k:128 * k + 128], OT[:, k, 128 * t:128 * t + 128],
                                 ident[:])
                    last.then_inc(e.oTmm, 1)

            def transpose_normalised(l, i):
                e = E[l]
                pe.wait_ge(e.on, 2 * i + 2)
                wait_misc_free(pe, l, "on", i)
                for f in range(2):
                    for t in range(2):
                        last = T(misc(l, "on", i)[0:HP, NT * f + 128 * t:NT * f + 128 * t + 128],
                                 ON[:, t, HP * f:HP * f + HP], ident[:])
                last.then_inc(e.onTmm, 1)

            def project_output(l, i):
                e = E[l]
                pe.wait_ge(e.ont, i + 1)
                wait_misc_free(pe, l, "pr", i)
                for t in range(2):
                    for f in range(2):
                        last = mm(misc(l, "pr", i)[:, C * t:C * t + C], ONT[:, f, 128 * t:128 * t + 128],
                                  WP[l][:, f, :], start=f == 0, stop=f == 1)
                last.then_inc(e.proj, 1)

            def attention(l):
                e = E[l]

                def tokens(i):
                    wait_misc_free(pe, l, "x", i)
                    transpose_tokens(e, i, misc(l, "x", i))

                tokens(0)
                project_qk(l, 0)
                project_v(l, 0)
                if l:
                    relative_products(0)
                transpose_stacks(l, 0)
                for h in range(NH):
                    scores(l, 0, h)
                transpose_maxima(l, 0)
                transpose_edges(l, 0)
                for i in range(B):
                    more = i + 1 < B
                    for h in range(NH):
                        scores_T(l, i, h)
                        if h:
                            weighted_values(l, i, h - 1)
                        if more:
                            if h == 1:
                                tokens(i + 1)
                            if h == 3:
                                project_qk(l, i + 1)
                            if h == 5:
                                project_v(l, i + 1)
                            if l and h == 6:
                                relative_products(i + 1)
                    weighted_values(l, i, NH - 1)
                    if more:
                        transpose_stacks(l, i + 1)
                        for h in range(NH):
                            scores(l, i + 1, h)
                            if h == 2:
                                transpose_output(l, i)
                            if h == 6:
                                transpose_normalised(l, i)
                            if h == 9:
                                project_output(l, i)
                        transpose_maxima(l, i + 1)
                        transpose_edges(l, i + 1)
                    else:
                        transpose_output(l, i)
                        transpose_normalised(l, i)
                        project_output(l, i)

            def hidden(l, i):
                m = M[l]
                pe.wait_ge(m.xl, i + 1)
                for j in range(3):
                    n = 3 * i + j
                    if n >= 4:
                        pe.wait_ge(m.gelu, 2 * (n - 3))
                    for k in (2 * j, 2 * j + 1):
                        w = [WF[l][:, r, 128 * k:128 * k + 128] for r in range(4)]
                        last = split_product(ps[:, n % 4, NT * (k % 2):NT * (k % 2) + NT],
                                             (XH[:, 0, 0:NT], XL[:, 0:NT], XH[:, 1, 0:NT]), w, flip=True)
                    last.then_inc(m.f1, 1)

            def down(l, i):
                m = M[l]
                pe.wait_ge(m.gelu, MT * (i + 1))
                if i >= 1:
                    pe.wait_ge(m.y, i)
                for t in range(2):
                    for k in range(MT):
                        last = mm(ps[:, 6, C * t:C * t + C], GT[i % 2][:, k, 128 * t:128 * t + 128], W2[l][:, k, :],
                                  start=k == 0, stop=k == MT - 1)
                last.then_inc(m.f2, 1)

            def mlp(l):
                m = M[l]
                transpose_tokens(m, 0, ps[:, 7, :])
                for i in range(B):
                    hidden(l, i)
                    if i + 1 < B:
                        transpose_tokens(m, i + 1, ps[:, 7, :])
                    if i:
                        down(l, i - 1)
                down(l, B - 1)

            pe.wait_ge(w_in[0], N_W)
            pe.wait_ge(s_dve, setup_count("consts", None))
            fold_biases(0)
            pe.drain().then_inc(phase, 1)
            for l in range(2):
                pe.wait_ge(phase, 4 * (2 * l + 1))
                attention(l)
                pe.drain().then_inc(phase, 1)
                pe.wait_ge(phase, 4 * (2 * l + 2))
                if l == 0:
                    fold_biases(1)
                    bare_keys()
                mlp(l)
                if l == 0:
                    pe.drain().then_inc(phase, 1)


def tables():
    import numpy as np

    rows = np.array([n // WS for n in range(NM)] + [r for r in range(WS) for _ in range(W - WS)]
                    + [r for r in range(WS, H) for _ in range(W)])
    cols = np.array([n % WS for n in range(NM)] + [c for _ in range(WS) for c in range(WS, W)]
                    + [c for _ in range(WS, H) for c in range(W)])
    group = np.where((rows < WS) & (cols < WS), 3, np.where(rows < WS, 0, np.where(cols < WS, 1, 2)))
    qr, qc = rows % WS, cols % WS
    onehot = (group[:, None] == np.arange(4)[None, :]).astype(np.float32)
    t = {"ident": np.eye(128, dtype=np.float32)}

    def tiles(a):
        return np.ascontiguousarray(a.reshape(2, 128, *a.shape[1:]).swapaxes(0, 1))

    padq = np.zeros((NT, 16), np.float32)
    padq[:, 0:4] = onehot
    padk = np.zeros((NT, 16), np.float32)
    padk[:, 0:4] = -BIG * (1 - onehot)
    seen = np.array([[1, 1, 1, 0], [1, 0, 1, 0], [0, 1, 1, 0], [0, 0, 0, 0]], np.float32)
    virt = np.zeros((128, 1, 16), np.float32)
    virt[0:4, 0, 0:4] = -BIG * (1 - seen)
    t["padq"] = tiles(padq)
    t["padk"] = np.concatenate([tiles(padk), virt], 1)
    own = np.concatenate([np.eye(4, dtype=np.float32)[0:3], np.zeros((1, 4), np.float32)])
    kv = np.zeros((128, NH, NV), np.float32)
    for h in range(NH):
        r = 64 * (h % 2) + 48
        kv[r:r + 4, h, :] = -BIG * (1 - own.T)
    t["kvirt"] = kv
    hot = np.zeros((64, NK), np.float32)
    for r0 in (0, 32):
        hot[r0 + qr, np.arange(NT)] = 1
        hot[r0 + WS + qc, np.arange(NT)] = 1
        hot[r0 + 2 * WS + np.arange(3), NT + np.arange(3)] = 1
    t["hot"] = hot
    vc = np.zeros((128, 2, 2, 2), np.float32)
    counts = [NM - WS * (W - WS), NM - WS * (H - WS), NM - (H - WS) * (W - WS)]
    for k in range(2):
        r = 64 * k
        vc[r:r + NE, :, k, 1] = 1
        for g in range(3):
            vc[r + NE + g, 0, k, :] = counts[g]
            vc[r + NE + g, 1, k, :] = 1
    t["vcon"] = vc
    shm = np.zeros((NT, 2, 4), np.int32)
    for k, s in enumerate((8, 4, 2, 1)):
        shm[:, 0, k] = ((WS - 1 - qr) & s) > 0
        shm[:, 1, k] = ((WS - 1 - qc) & s) > 0
    t["shm"] = np.ascontiguousarray(tiles(shm).reshape(128, 4, 4))
    token = rows * W + cols
    return t, token


def kernel(**inputs):
    import numpy as np
    import concourse.bacc as bacc
    from concourse.bass_utils import run_bass_kernel_spmd

    a = {k: np.asarray(v) for k, v in inputs.items()}
    tab, token = tables()
    arrays = {"x": a["x"]}

    def bc(v):
        return np.ascontiguousarray(np.broadcast_to(v, (128, v.shape[-1])))

    def by_tile(v):
        return np.ascontiguousarray(v.reshape(2, 128, -1).swapaxes(0, 1))

    rope = a["L0_conv_rope_2d"].reshape(NT, HD)[token]
    half = HD // 2
    sin, cos = rope[:, :half], rope[:, half:]
    arrays["cos"] = by_tile(np.concatenate([cos, cos], 1))
    arrays["sin"] = by_tile(np.concatenate([sin, sin], 1))
    for n, v in tab.items():
        arrays[n] = v
    arrays["gamma1"], arrays["gamma2"] = bc(a["L0_conv_gamma_1"]), bc(a["L0_conv_gamma_2"])
    R = np.zeros((2, NG, HD), np.float32)
    for k, n in enumerate(("h", "w")):
        R[k, 0:2 * WS - 1] = a[f"L1_conv_rel_pos_{n}"][::-1]
    rbd = np.zeros((6, HD, 6, 2, NG), np.float32)
    for h in range(6):
        rbd[h, :, h] = R.transpose(2, 0, 1)
    arrays["rbd"] = rbd.reshape(HP, 6 * 2 * NG)
    for l in range(2):
        g = (lambda n: a[f"L0_conv_{n}"]) if l == 0 else (lambda n: a[f"L1_conv_{n}"])
        if l == 0:
            wqkv, wproj, w1, w2 = g("w_qkv").T, g("w_proj").T, g("w_fc1").T, g("w_fc2").T
            ln = [g("ln1_g"), g("ln1_b"), g("ln2_g"), g("ln2_b")]
            bs = [g("b_qkv"), g("b_proj"), g("b_fc1"), g("b_fc2")]
        else:
            wqkv, wproj, w1, w2 = g("qkv_w"), g("proj_w"), g("fc1_w"), g("fc2_w")
            ln = [g("ln1_w"), g("ln1_b"), g("ln2_w"), g("ln2_b")]
            bs = [g("qkv_b"), g("proj_b"), g("fc1_b"), g("fc2_b")]
        arrays[f"wqkv{l}"] = wqkv
        arrays[f"w1{l}"] = w1
        arrays[f"wproj{l}"] = wproj.reshape(2, HP, C).swapaxes(0, 1)
        arrays[f"w2{l}"] = w2.reshape(MT, 128, C).swapaxes(0, 1)
        ln = np.stack(ln, 1)
        arrays[f"ln{l}"] = np.stack([ln[0:128], np.concatenate([ln[128:C], ln[128:C]])], 1)
        arrays[f"bqkv{l}"], arrays[f"bproj{l}"], arrays[f"b2{l}"] = bc(bs[0]), bc(bs[1]), bc(bs[3])
        arrays[f"b1{l}"] = bs[2].reshape(MT, 128).T

    nc = bacc.Bacc("TRN2", target_bir_lowering=False, num_devices=1)
    arrays = {f"in_{n}": np.ascontiguousarray(v) for n, v in arrays.items()}
    d = {n[3:]: nc.dram_tensor(n, v.shape, mybir.dt.from_np(v.dtype), kind="ExternalInput").ap()
         for n, v in arrays.items()}
    out = nc.dram_tensor("out_0", (B, H, W, C), F32, kind="ExternalOutput").ap()
    names = ("wqkv", "w1", "wproj", "w2", "ln", "bqkv", "bproj", "b2", "b1")
    extra = (dict(gamma1=d["gamma1"], gamma2=d["gamma2"], rbd=None), dict(gamma1=None, gamma2=None, rbd=d["rbd"]))
    layers = [Block(**{n: d[f"{n}{l}"] for n in names}, **extra[l]) for l in range(2)]
    build(nc, d["x"], d["cos"], d["sin"], layers, {n: d[n] for n in tab}, out)
    r = run_bass_kernel_spmd(nc, [arrays], core_ids=[0])
    return r.results[0]["out_0"]
```

```python
from collections import namedtuple
from contextlib import ExitStack

import concourse.bass as bass
from concourse import mybir

ALU = mybir.AluOpType
ACT = mybir.ActivationFunctionType
AX = mybir.AxisListType.X
F32 = mybir.dt.float32
F32R = mybir.dt.float32r
I32 = mybir.dt.int32

B, H, W, C = 8, 16, 16, 192
NH, HD = 12, 16
WS = 14
NT = H * W
NM = WS * WS
NE = NT - NM
CH = NM // 2
NV = 4
NK = NT + NV
EK = NE + NV
ND = NM + 2 * EK
SB = NM + EK
F = 4 * C
MT = F // 128
PAIRS = NH // 2
NG = 2 * WS + 1
E0 = NM - 128
HP = 96
NVB = 3
BIG = 1.0e30
EPS1 = (1e-6, 1e-5)
KSCALE = float(HD) ** -0.5

KQ_ACT, KQ_DVE = "act", "dve"
KQ_ENGINE = (
    {"k0": KQ_ACT, "k1": KQ_ACT, "k2": KQ_ACT, "q0": KQ_DVE, "q1": KQ_DVE, "q2": KQ_ACT},
    {"k0": KQ_DVE, "k1": KQ_ACT, "k2": KQ_ACT, "q0": KQ_ACT, "q1": KQ_DVE, "q2": KQ_ACT, "q3": KQ_ACT, "q4": KQ_ACT, "q5": KQ_ACT},
)


Block = namedtuple("Block", "wqkv w1 wproj w2 ln bqkv bproj b2 b1 gamma1 gamma2 rbd")


def build(nc, x, rope_cos, rope_sin, layers, consts, out):
    ctx = ExitStack()
    with ctx:
        def sb(name, shape, dt=F32):
            return ctx.enter_context(nc.sbuf_tensor(name, shape, dt))

        def sem(name):
            return ctx.enter_context(nc.semaphore(name))

        ps = ctx.enter_context(nc.psum_tensor("ps", [128, 8, 512], F32))
        S_BANK, ST_BANK, O_BANK, MISC = 0, 2, 4, 6

        X = sb("X", [128, 2 * B, C])
        XB = sb("XB", [128, 2, C])
        xn = sb("xn", [128, 2, C + 64])
        stats = sb("stats", [128, 2, 6])
        mv = sb("mv", [128, 2, 2])
        veps = sb("veps", [128, 2])
        rstd = sb("rstd", [128, 2])
        nhalf = sb("nhalf", [128, 2])
        XH = sb("XH", [128, 2, ND], F32R)
        XL = sb("XL", [128, ND], F32R)
        WQ = sb("WQ", [128, 4, 3 * C], F32R)
        WF = [sb(f"WF{l}", [128, 4, F], F32R) for l in range(2)]
        WP = [sb(f"WP{l}", [HP, 2, C]) for l in range(2)]
        W2 = [sb(f"W2{l}", [128, MT, C]) for l in range(2)]
        b_qkv = [sb(f"b_qkv{l}", [128, 3 * C]) for l in range(2)]
        b_v0 = [sb(f"b_v0{l}", [128, 2 * C]) for l in range(2)]
        b_p = [sb(f"b_p{l}", [128, C]) for l in range(2)]
        b_2 = [sb(f"b_2{l}", [128, C]) for l in range(2)]
        b_1 = [sb(f"b_1{l}", [128, MT]) for l in range(2)]
        gam = sb("gam", [128, 2, C])
        lnp = sb("lnp", [128, 2, 4])
        g4 = sb("g4", [128, 2])
        lnb_w = sb("lnb_w", [128, 2, 2, 128])
        raw = sb("raw", [128, 2, 3 * C + F])
        ident = sb("ident", [128, 128])
        sel = sb("sel", [128, NH, CH], F32R)
        cos_t = sb("cos_t", [128, 2, HD])
        sin_t = sb("sin_t", [128, 2, HD])
        padq = sb("padq", [128, 2, 16])
        padk = sb("padk", [128, 3, 16])
        kvirt = sb("kvirt", [128, NH, NV])
        hot = sb("hot", [128, NK])
        vcon = sb("vcon", [128, 2, 2, 2])
        shm = sb("shm", [128, 4, 4], I32)
        Rbd = sb("Rbd", [HP, 6 * 2 * NG])
        QK = sb("QK", [128, 2, 2 * C])
        QKab = sb("QKab", [128, 4, 2 * C])
        QKa, QKb = QKab[:, 0:2, :], QKab[:, 2:4, :]
        QS = sb("QS", [128, 2, NH, 128], F32R)
        QS0 = QS[:, :, 0:PAIRS, :].rearrange("p t m (s d) -> p t (m s) d", s=2)
        KS = sb("KS", [128, 2, NH, 64], F32R)
        QT = [sb(f"QT{p}", [128, NH, NT], F32R) for p in range(2)]
        KM = [sb(f"KM{p}", [128, NH, NK], F32R) for p in range(2)]
        V01 = [sb(f"V01{p}", [CH, 2, NH, HD + 1]) for p in range(NVB)]
        VE = [sb(f"VE{p}", [128, PAIRS, 64]) for p in range(NVB)]
        mneg = [sb(f"mneg{p}", [128, 2, 128]) for p in range(2)]
        mT = [sb(f"mT{p}", [128, NT], F32R) for p in range(2)]
        PTb = sb("PTb", [128, 4 * 2 * NM])
        PT = PTb[0:CH, :].rearrange("p (s n) -> p s n", s=4)
        PE_ = [sb(f"PE{p}", [128, NH, EK]) for p in range(2)]
        PET = [sb(f"PET{p}", [128, PAIRS, NE]) for p in range(2)]
        OT = sb("OT", [128, 3, NT])
        rden = sb("rden", [128, 2, NH])
        ON = sb("ON", [128, 2, C])
        ONT = sb("ONT", [HP, 2, NT])
        rawf = raw[:].rearrange("p r n -> p (r n)")
        nG = 4 * NH * NG
        G = rawf[:, 0:nG].rearrange("p (a h j) -> p a h j", a=4, h=NH)
        QF = rawf[0:HP, nG:nG + 2 * NT].rearrange("p (f t) -> p f t", f=2)
        at = nG + 2 * NT
        DX = rawf[:, at:at + 2 * NH * WS].rearrange("p (a h j) -> p a h j", a=2, h=NH)
        at += 2 * NH * WS
        Mx = rawf[:, at:at + 4 * NH].rearrange("p (k a h) -> p k a h", k=2, a=2)
        SX = rawf[:, at + 4 * NH:at + 8 * NH].rearrange("p (k a h) -> p k a h", k=2, a=2)
        at += 8 * NH
        Mr = rawf[:, at:at + 3 * NH].rearrange("p (h r) -> p h r", r=3)
        at += 3 * NH
        Wr = [rawf[:, at + 3 * NH * p:at + 3 * NH * (p + 1)].rearrange("p (h r) -> p h r", r=3)
              for p in range(2)]
        KB = PE_[0][0:4, :, :]
        GT = [PTb[:, 0:MT * NT].rearrange("p (m t) -> p m t", m=MT),
              QKab[:].rearrange("p a n -> p (a n)").rearrange("p (m t) -> p m t", m=MT)]
        Y = [OT[:].rearrange("p k t -> p (k t)")[:, 2 * C * p:2 * C * p + 2 * C].rearrange("p (t c) -> p t c", t=2)
             for p in range(2)]

        def events(prefix, names):
            return namedtuple(prefix, names)(*[sem(f"{prefix}_{n}") for n in names.split()])

        ATT = ("stats aggr veps rstd xn xT xh xl xd qkmm qk vmm v01 ve "
               "t1 t2 qkr hi lo kqT kq_act kq_dve "
               "smm mneg mTmm mT eexp eTmm pet "
               "stmm pexp av ave ot oTmm rden on onTmm ont proj xb x1")
        REL = "qfT qf gmm g sh rmax rsub rexp rsum rmul qrel ew"
        E = [events("a0", ATT), events("a1", ATT + " " + REL)]
        M = [events(f"m{l}", "stats aggr veps rstd xn xT xh xl f1 gelu f2 xb y") for l in range(2)]
        x_in, c_in = sem("x_in"), sem("c_in")
        store = [sem(f"store{p}") for p in range(2)]
        w_in = [sem(f"w_in{l}") for l in range(2)]
        ready_setup = sem("ready_setup")
        s_dve, s_pe = sem("s_dve"), sem("s_pe")
        phase = sem("phase")

        SCORES = -15
        USES = (
            {"x": -31, "qk0": -28, "qk1": -28, "v01": -22, "ve": -20, "k0": -19, "q0": -17, "q1": -16, "k1": -15, "q2": -11, "k2": -10, "m": -2, "e0": -1, "e1": 0, "o0": 15, "o1": 16, "on": 16, "pr": 21},
            {"x": -34, "qk0": -32, "qk1": -32, "qf": -31, "g0": -29, "g1": -28, "g2": -28, "g3": -27, "v01": -24, "ve": -23, "q0": -20, "k0": -19, "q2": -19, "q1": -18, "k1": -15, "q3": -14, "q4": -13, "k2": -11, "q5": -11, "m": -3, "e0": 0, "e1": 0, "o0": 14, "o1": 15, "on": 17, "pr": 19},
        )
        WORK = (
            {"stats": -35, "inv_std": -35, "xn": -32, "cosine": -26, "sine": -27, "rotate": -22, "hi0": -22, "hi1": -21, "lo0": -20, "lo1": -20, "out0": 9, "out1": 13, "xb": 10, "xd": -31},
            {"stats": -39, "inv_std": -36, "xn": -35, "sh0": -27, "sh1": -26, "sh2": -25, "sh3": -24, "bounds": -23, "qrel": -22, "hi0": -23, "hi1": -22, "lo0": -22, "lo1": -21, "rexp": -22, "sums": -20, "ew": -3, "out0": 8, "out1": 12, "xb": 12, "xd": -34},
        )

        def steps(l):
            return range(min(WORK[l].values()), NH * (B - 1) + max(USES[l].values()) + 1)

        def due(g, step):
            n, r = divmod(g - step, NH)
            return n if r == 0 and 0 <= n < B else None

        def head_due(g, step):
            n, h = divmod(g - step, NH)
            return (n, h) if 0 <= n < B else None

        def uses_due(l, g):
            return [(u, due(g, s)) for u, s in USES[l].items() if due(g, s) is not None]

        def work_due(l, g, names):
            return [(w, due(g, WORK[l][w])) for w in names if w in WORK[l] and due(g, WORK[l][w]) is not None]

        def turns(l):
            return [use for g in steps(l) for use in uses_due(l, g)]

        ORDER = [turns(l) for l in range(2)]
        TURN = [{u: n for n, u in enumerate(o)} for o in ORDER]

        def kq_turn(l, u):
            return [n for n in USES[l] if n in KQ_ENGINE[l]].index(u)

        def kq_count(l, u, i):
            mine = [n for n in USES[l] if n in KQ_ENGINE[l] and KQ_ENGINE[l][n] == KQ_ENGINE[l][u]]
            return len(mine) * i + mine.index(u) + 1

        def stacks_of(l, h):
            return f"k{h // 4}", (f"q{h // 2}" if l else f"q{h // 4}")

        def misc_emptied(l, u, i):
            e = E[l]
            if u in KQ_ENGINE[l]:
                return (e.kq_act if KQ_ENGINE[l][u] == KQ_ACT else e.kq_dve), kq_count(l, u, i)
            if u[0] == "g":
                return e.g, 4 * i + int(u[1]) + 1
            return {"x": (e.xl, i + 1), "qk0": (e.qk, 2 * i + 1), "qk1": (e.qk, 2 * i + 2),
                    "v01": (e.v01, i + 1), "ve": (e.ve, i + 1),
                    "qf": (e.qf if l else None, i + 1),
                    "m": (e.mT, i + 1), "e0": (e.pet, 2 * i + 1), "e1": (e.pet, 2 * i + 2),
                    "o0": (e.on, 2 * i + 1), "o1": (e.on, 2 * i + 2), "on": (e.ont, i + 1),
                    "pr": (e.x1, i + 1)}[u]

        def misc(l, u, i):
            return ps[:, MISC + TURN[l][u, i] % 2, :]

        def wait_misc_free(pe, l, u, i):
            n = TURN[l][u, i]
            if n >= 2:
                s, v = misc_emptied(l, *ORDER[l][n - 2])
                pe.wait_ge(s, v)

        def evacuate(l, u, i, copy, eng, done):
            e, p = E[l], i % 2
            names = list(KQ_ENGINE[l])
            j = int(u[1])
            if i >= 2:
                h = 2 * j + 1 if l and u[0] == "q" else 4 * j + 3
                eng.wait_ge(e.stmm, NH * (i - 2) + h + 1)
            eng.wait_ge(e.kqT, len(names) * i + kq_turn(l, u) + 1)
            bank = misc(l, u, i).rearrange("p (m t) -> p m t", m=2)
            if u[0] == "q":
                copy(QT[p][:, 2 * j:2 * j + 2, :], bank).then_inc(done, 1)
            else:
                odd = slice(64, 128) if l == 0 else slice(0, 64)
                copy(KM[p][0:64, 4 * j:4 * j + 3:2, 0:NT], bank[0:64])
                copy(KM[p][odd, 4 * j + 1:4 * j + 4:2, 0:NT], bank[64:128]).then_inc(done, 1)

        def heads(ap, n=NH):
            return ap.rearrange("p (h d) -> p h d", h=n)

        block = ctx.enter_context(nc.Block())

        PIECES = [
            (0, 0, (0, 9), (0, WS)),
            (0, 126, (9, 10), (0, 2)),
            (1, 0, (9, 10), (2, WS)),
            (1, 12, (10, WS), (0, WS)),
            (1, E0, (0, WS), (WS, W)),
            (1, E0 + 28, (WS, H), (0, W)),
        ]

        def piece_dram(t, b0, b1, rows, cols):
            return t[b0:b1, rows[0]:rows[1], cols[0]:cols[1], :].rearrange("b h w c -> h w b c")

        def piece_size(rows, cols):
            return (rows[1] - rows[0]) * (cols[1] - cols[0])

        @block.sync
        def _(sp):
            n_x = 0
            for b0 in range(B):
                for t, p0, rows, cols in PIECES:
                    n = piece_size(rows, cols)
                    sp.dma_start(X[p0:p0 + n, 2 * b0 + t, :], x[b0, rows[0]:rows[1], cols[0]:cols[1], :])\
                        .then_inc(x_in, 16)
                if b0 == 0:
                    for dst, src in ((ident[:], consts["ident"]), (padq[:], consts["padq"]),
                                     (padk[:], consts["padk"]), (cos_t[:], rope_cos), (sin_t[:], rope_sin),
                                     (vcon[:], consts["vcon"]), (kvirt[:], consts["kvirt"]),
                                     (hot[64:128, :], consts["hot"]), (shm[:], consts["shm"]),
                                     (Rbd[:], layers[1].rbd), (gam[:, 0, :], layers[0].gamma1),
                                     (gam[:, 1, :], layers[0].gamma2)):
                        sp.dma_start(dst, src).then_inc(c_in, 16)
            for i in range(B):
                sp.wait_ge(M[1].y, i + 1)
                for t, p0, rows, cols in PIECES:
                    n = piece_size(rows, cols)
                    sp.dma_start(out[i, rows[0]:rows[1], cols[0]:cols[1], :], Y[i % 2][p0:p0 + n, t, :])\
                        .then_inc(store[i % 2], 16)
            for p in range(2):
                sp.wait_ge(store[p], 16 * len(PIECES) * B // 2)

        N_CONST = 12 * 16

        def weight_loads(q, l):
            ly = layers[l]
            if l == 1:
                q.wait_ge(s_dve, setup_count("raw", 0))
                q.wait_ge(s_pe, 1)
            for dst, src in ((raw[:, 0, 0:3 * C], ly.wqkv[0:128, :]), (raw[0:64, 1, 0:3 * C], ly.wqkv[128:C, :]),
                             (raw[64:128, 1, 0:3 * C], ly.wqkv[128:C, :]),
                             (raw[:, 0, 3 * C:], ly.w1[0:128, :]), (raw[0:64, 1, 3 * C:], ly.w1[128:C, :]),
                             (raw[64:128, 1, 3 * C:], ly.w1[128:C, :]),
                             (lnp[:], ly.ln),
                             (WP[l][:], ly.wproj), (W2[l][:], ly.w2),
                             (b_qkv[l][:], ly.bqkv), (b_v0[l][:], ly.bqkv[:, C:]), (b_p[l][:], ly.bproj),
                             (b_2[l][:], ly.b2), (b_1[l][:], ly.b1)):
                q.dma_start(dst, src).then_inc(w_in[l], 16)

        N_W = 14 * 16

        SETUP_DVE = ["consts"] + [f"{n}{l}" for l in range(2) for n in ("lnbw", "raw", "bias")] + ["bare1"]

        def setup_count(name, l):
            return SETUP_DVE.index(name if l is None else f"{name}{l}") + 1

        @block.vector
        def _(dve):
            v = nc.vector

            def chain(ins, count=[0]):
                count[0] += 1
                ins.then_inc(ready_setup, 1)
                dve.wait_ge(ready_setup, count[0])

            for p in range(2):
                v.memset(mneg[p][:], 0.0)
            v.memset(nhalf[:], -0.5)
            v.memset(XH[:].bitcast(F32), 0.0)
            v.memset(XL[:].bitcast(F32), 0.0)
            v.memset(PTb[:], 0.0)
            v.memset(ps[:, O_BANK:O_BANK + 2, :], 0.0)
            for p in range(NVB):
                v.memset(VE[p][:], 0.0)
            for p in range(2):
                v.memset(KM[p][:].bitcast(F32), 0.0)
            v.memset(QS[:].bitcast(F32), 0.0)
            chain(v.memset(KS[:].bitcast(F32), 0.0))
            for p in range(NVB):
                chain(v.memset(V01[p][:, :, :, HD:HD + 1], 1.0))
            dve.wait_ge(c_in, N_CONST)
            for t in range(2):
                v.tensor_copy(QS0[:, t, :, 48:64], padq[:, t:t + 1, :].broadcast_to([128, NH, 16]))
                v.tensor_copy(KS[:, t, :, 48:64], padk[:, t:t + 1, :].broadcast_to([128, NH, 16]))
            for h in range(NH):
                v.tensor_copy(sel[:, h, :], ident[:, h:h + 1].broadcast_to([128, CH]))
            for p in range(2):
                v.tensor_copy(KM[p][:, :, NT:NK], kvirt[:])
            chain(v.tensor_scalar(sin_t[:, :, 0:HD // 2], sin_t[:, :, 0:HD // 2], -1.0, None, ALU.mult))
            dve.drain().then_inc(s_dve, 1)

            def weights(l):
                dve.wait_ge(w_in[l], N_W)
                for k in range(2):
                    for r in range(2):
                        last = v.tensor_copy(lnb_w[:, k, r, :], lnp[:, r, 1 + 2 * k:2 + 2 * k].broadcast_to([128, 128]))
                last.then_inc(s_dve, 1)
                chain(v.tensor_scalar(g4[:], lnp[:, :, 0], KSCALE, None, ALU.mult))
                for r in range(2):
                    for k, dst, w0, n, g in ((0, WQ, 0, C, lnp[:, r, 0:1]), (0, WQ, C, C, g4[:, r:r + 1]),
                                             (0, WQ, 2 * C, C, lnp[:, r, 0:1]),
                                             (1, WF[l], 0, F, lnp[:, r, 2:3])):
                        src = raw[:, r, 3 * C * k + w0:3 * C * k + w0 + n]
                        chain(v.tensor_scalar(dst[:, 2 * r, w0:w0 + n], src, g, None, ALU.mult))
                        v.scalar_tensor_tensor(dst[:, 2 * r + 1, w0:w0 + n], src, g, dst[:, 2 * r, w0:w0 + n].bitcast(F32),
                                               ALU.mult, ALU.subtract)
                dve.drain().then_inc(s_dve, 1)
                if l == 0:
                    chain(v.tensor_tensor(WP[l][:], WP[l][:], gam[0:HP, 0:1, :].broadcast_to([HP, 2, C]), ALU.mult))
                    chain(v.tensor_tensor(W2[l][:], W2[l][:], gam[:, 1:2, :].broadcast_to([128, MT, C]), ALU.mult))
                    chain(v.tensor_tensor(b_p[l][:], b_p[l][:], gam[:, 0, :], ALU.mult))
                    chain(v.tensor_tensor(b_2[l][:], b_2[l][:], gam[:, 1, :], ALU.mult))
                dve.wait_ge(s_pe, l + 1)
                chain(v.tensor_tensor(b_qkv[l][:, 0:2 * C], ps[:, 4, 0:2 * C], b_qkv[l][:, 0:2 * C], ALU.add))
                chain(v.tensor_tensor(b_qkv[l][:, 2 * C:], ps[:, 5, 0:C], b_qkv[l][:, 2 * C:], ALU.add))
                chain(v.tensor_scalar(b_qkv[l][:, C:2 * C], b_qkv[l][:, C:2 * C], KSCALE, None, ALU.mult))
                chain(v.tensor_scalar(b_v0[l][:, 0:C], b_v0[l][:, 0:C], KSCALE, None, ALU.mult))
                v.tensor_tensor(b_1[l][:], ps[:, 4, 2 * C:2 * C + MT], b_1[l][:], ALU.add).then_inc(s_dve, 1)

            def virtual_values(l):
                for p in range(NVB):
                    for k in range(2):
                        dst = VE[p][:, :, 32 * k:32 * k + HD]
                        src = b_v0[l][:, C:].rearrange("p (m k d) -> p m k d", k=2, d=HD)[:, :, k, :]
                        chain(v.tensor_scalar(dst, src, vcon[:, l, k, 0:1], None, ALU.mult))
                        chain(v.tensor_copy(VE[p][:, :, 32 * k + HD:32 * k + HD + 1],
                                      vcon[:, l, k, 1:2].unsqueeze(1).broadcast_to([128, PAIRS, 1])))

            def statistics(e, i):
                for t in range(2):
                    last = v.bn_stats(stats[:, t, :], X[:, 2 * i + t, :])
                last.then_inc(e.stats, 1)
                dve.wait_ge(e.stats, i + 1)
                if i >= 1:
                    dve.wait_ge(e.veps, i)
                for t in range(2):
                    last = v.bn_aggr(mv[:, t, :], stats[:, t, :])
                last.then_inc(e.aggr, 1)

            def normalised_tokens(e, i):
                dve.wait_ge(e.rstd, i + 1)
                if i >= 1:
                    dve.wait_ge(e.xT, i)
                for t in range(2):
                    for dst, c0 in ((xn[:, t, 0:C], 0), (xn[:, t, C:C + 64], 128)):
                        last = v.tensor_scalar(dst, X[:, 2 * i + t, c0:C], mv[:, t, 0:1], rstd[:, t:t + 1],
                                               ALU.subtract, ALU.mult)
                last.then_inc(e.xn, 1)

            def layer_norm(e, i):
                statistics(e, i)
                normalised_tokens(e, i)

            def split_low(e, i, bank):
                dve.wait_ge(e.xh, i + 1)
                v.tensor_tensor(XL[:, 0:NT], bank[:, 0:NT], XH[:, 0, 0:NT].bitcast(F32), ALU.subtract)
                v.tensor_tensor(XH[64:128, 1, 0:NT], bank[64:128, NT:2 * NT], XH[64:128, 1, 0:NT].bitcast(F32),
                                ALU.subtract).then_inc(e.xl, 1)

            def queries_keys(l, i, t):
                e = E[l]
                dve.wait_ge(e.qkmm, 2 * i + t + 1)
                if i >= 1 and t == 0:
                    dve.wait_ge(e.lo, 2 * i)
                    if l == 0:
                        dve.wait_ge(e.t2, 2 * i)
                    else:
                        dve.wait_ge(e.hi, 2 * i)
                        dve.wait_ge(e.qfT, i)
                v.tensor_tensor(QK[:, t, :], misc(l, f"qk{t}", i)[:, 0:2 * C], b_qkv[l][:, 0:2 * C],
                                ALU.add).then_inc(e.qk, 1)

            def cosine_half(i):
                e = E[0]
                dve.wait_ge(e.qk, 2 * i + 2)
                if i >= 1:
                    dve.wait_ge(e.hi, 2 * i)
                    dve.wait_ge(e.lo, 2 * i)
                for t in range(2):
                    last = v.tensor_tensor(heads(QKa[:, t, :], 2 * NH), heads(QK[:, t, :], 2 * NH),
                                           cos_t[:, t:t + 1, :].broadcast_to([128, 2 * NH, HD]), ALU.mult)
                last.then_inc(e.t1, 1)

            def rotate(i):
                e = E[0]
                dve.wait_ge(e.t1, i + 1)
                dve.wait_ge(e.t2, 2 * i + 2)
                v.tensor_tensor(QKa, QKa, QKb, ALU.add).then_inc(e.qkr, 1)

            def main_values(l, i):
                e = E[l]
                dve.wait_ge(e.vmm, 2 * i + 1)
                if i >= NVB:
                    dve.wait_ge(e.av, NH * (i - NVB + 1))
                for c in range(2):
                    last = v.tensor_tensor(V01[i % NVB][:, c, :, 0:HD], heads(misc(l, "v01", i)[0:CH, C * c:C * c + C]),
                                           heads(b_qkv[l][0:CH, 2 * C:]), ALU.add)
                last.then_inc(e.v01, 1)

            def edge_values(l, i):
                e = E[l]
                dve.wait_ge(e.vmm, 2 * i + 2)
                if i >= NVB:
                    dve.wait_ge(e.ave, PAIRS * (i - NVB + 1))
                for k in range(2):
                    r = slice(64 * k, 64 * k + NE)
                    last = v.tensor_tensor(
                        VE[i % NVB][r, :, 32 * k:32 * k + HD],
                        misc(l, "ve", i)[r, 0:C].rearrange("p (m k d) -> p m k d", k=2, d=HD)[:, :, k, :],
                        b_qkv[l][r, 2 * C:].rearrange("p (m k d) -> p m k d", k=2, d=HD)[:, :, k, :], ALU.add)
                last.then_inc(e.ve, 1)

            def stack_low(l, i, t):
                e = E[l]
                src, qs = (QKa, QS0) if l == 0 else (QK, QS)
                dve.wait_ge(e.hi, 2 * i + t + 1)
                last = v.tensor_tensor(qs[:, t, :, 16:32], heads(src[:, t, 0:C]), qs[:, t, :, 0:16].bitcast(F32), ALU.subtract)
                if l == 1:
                    last = v.tensor_tensor(
                        qs[:, t, :, 96:96 + 2 * WS].rearrange("p h (a j) -> p a h j", a=2),
                        G[:, 2 * t:2 * t + 2, :, 0:WS],
                        qs[:, t, :, 64:64 + 2 * WS].bitcast(F32).rearrange("p h (a j) -> p a h j", a=2), ALU.subtract)
                    if t == 1:
                        dve.wait_ge(e.qrel, i + 1)
                        v.tensor_tensor(qs[:, 1, :, 124:127], Mr, qs[:, 1, :, 92:95].bitcast(F32), ALU.subtract)
                v.tensor_tensor(KS[:, t, :, 32:48], heads(src[:, t, C:]), KS[:, t, :, 0:16].bitcast(F32),
                                ALU.subtract).then_inc(e.lo, 1)

            def shift(i, k):
                e = E[1]
                s, w = ((8, 21), (4, 17), (2, 15), (1, WS))[k]
                if k == 0:
                    dve.wait_ge(e.g, 4 * i + 4)
                else:
                    dve.wait_ge(e.sh, 4 * i + k)
                v.copy_predicated(G[:, :, :, 0:w], shm[:, :, k:k + 1].unsqueeze(2).broadcast_to([128, 4, NH, w]),
                                  G[:, :, :, s:s + w]).then_inc(e.sh, 1)

            def bounds(i):
                e = E[1]
                if i >= 1:
                    dve.wait_ge(e.lo, 2 * i)
                dve.wait_ge(e.sh, 4 * i + 4)
                T1 = G[:, 2:4, :, 0:WS]
                v.tensor_reduce(Mx[:, 0, :, :], T1[:, :, :, 0:2], AX, ALU.max)
                v.tensor_reduce(Mx[:, 1, :, :], T1[:, :, :, 2:WS], AX, ALU.max).then_inc(e.rmax, 1)
                dve.wait_ge(e.rmax, i + 1)
                for k, (a, b) in enumerate(((0, 2), (2, WS))):
                    last = v.tensor_tensor(DX[:, :, :, a:b], T1[:, :, :, a:b],
                                           Mx[:, k, :, :].unsqueeze(3).broadcast_to([128, 2, NH, b - a]), ALU.subtract)
                for r, (a, b) in enumerate(((1, 1), (0, 1), (1, 0))):
                    last = v.tensor_tensor(Mr[:, :, r], Mx[:, a, 0, :], Mx[:, b, 1, :], ALU.add)
                last.then_inc(e.rsub, 1)

            def bound_rows(i):
                e = E[1]
                dve.wait_ge(e.rsub, i + 1)
                if i >= 1:
                    dve.wait_ge(e.kqT, len(KQ_ENGINE[1]) * i)
                v.tensor_copy(QS[:, 1, :, 92:95], Mr).then_inc(e.qrel, 1)

            def padding_sums(i):
                e = E[1]
                dve.wait_ge(e.rexp, i + 1)
                v.tensor_reduce(SX[:, 0, :, :], DX[:, :, :, 0:2], AX, ALU.add)
                v.tensor_reduce(SX[:, 1, :, :], DX[:, :, :, 2:WS], AX, ALU.add).then_inc(e.rsum, 1)
                dve.wait_ge(e.rsum, i + 1)
                for r, (a, b) in enumerate(((1, 1), (0, 1), (1, 0))):
                    last = v.tensor_tensor(Wr[i % 2][:, :, r], SX[:, a, 0, :], SX[:, b, 1, :], ALU.mult)
                last.then_inc(e.rmul, 1)

            def head_max(l, i, h):
                e = E[l]
                dve.wait_ge(e.smm, NH * i + h + 1)
                if i >= 2 and h == 0:
                    dve.wait_ge(e.mTmm, i - 1)
                bank = ps[:, S_BANK + h % 2, :]
                v.tensor_reduce(mneg[i % 2][:, 0, h:h + 1], bank[:, 0:NM], AX, ALU.max, negate=True)
                v.tensor_reduce(mneg[i % 2][:, 1, h:h + 1], bank[:, NM:NM + SB], AX, ALU.max, negate=True)\
                    .then_inc(e.mneg, 1)

            def normalise(l, i, t):
                e = E[l]
                dve.wait_ge(e.oTmm, 2 * i + t + 1)
                o = misc(l, f"o{t}", i)[:, 0:32 * NH].rearrange("p (h d) -> p h d", d=32)
                v.reciprocal(rden[:, t, :], o[:, :, HD]).then_inc(e.rden, 1)
                dve.wait_ge(e.rden, 2 * i + t + 1)
                if i >= 1:
                    dve.wait_ge(e.onTmm, i)
                v.tensor_tensor(heads(ON[:, t, :]), o[:, :, 0:HD],
                                rden[:, t, :].unsqueeze(2).broadcast_to([128, NH, HD]), ALU.mult).then_inc(e.on, 1)

            def residual(l, i):
                e = E[l]
                dve.wait_ge(e.proj, i + 1)
                dve.wait_ge(e.xb, i + 1)
                v.tensor_tensor(X[:, 2 * i:2 * i + 2, :], misc(l, "pr", i)[:, 0:2 * C].rearrange("p (t c) -> p t c", t=2),
                                XB[:], ALU.add).then_inc(e.x1, 1)

            def edge_weights(i):
                e = E[1]
                dve.wait_ge(e.eexp, NH * (i + 1))
                p = PE_[i % 2][:, :, NE:NE + 3]
                v.tensor_tensor(p, p, Wr[i % 2], ALU.mult).then_inc(e.ew, 1)

            def attention(l):
                e = E[l]
                work = {"stats": lambda i: statistics(e, i), "xn": lambda i: normalised_tokens(e, i),
                        "cosine": cosine_half, "rotate": rotate,
                        "sh0": lambda i: shift(i, 0), "sh1": lambda i: shift(i, 1),
                        "sh2": lambda i: shift(i, 2), "sh3": lambda i: shift(i, 3),
                        "bounds": bounds, "qrel": bound_rows, "sums": padding_sums,
                        "lo0": lambda i: stack_low(l, i, 0), "lo1": lambda i: stack_low(l, i, 1), "ew": edge_weights}
                empty = {"x": lambda i: split_low(e, i, misc(l, "x", i)),
                         "qk0": lambda i: queries_keys(l, i, 0), "qk1": lambda i: queries_keys(l, i, 1),
                         "v01": lambda i: main_values(l, i), "ve": lambda i: edge_values(l, i),
                         "o0": lambda i: normalise(l, i, 0), "o1": lambda i: normalise(l, i, 1),
                         "pr": lambda i: residual(l, i)}
                for g in steps(l):
                    if head_due(g, SCORES):
                        head_max(l, *head_due(g, SCORES))
                    for u, i in uses_due(l, g):
                        if u in empty:
                            empty[u](i)
                        elif KQ_ENGINE[l].get(u) == KQ_DVE:
                            evacuate(l, u, i, v.tensor_copy, dve, e.kq_dve)
                    for w, i in work_due(l, g, work):
                        work[w](i)

            def mlp(l):
                m = M[l]
                layer_norm(m, 0)
                split_low(m, 0, ps[:, 7, :])
                layer_norm(m, 1)
                for i in range(B):
                    if i + 1 < B:
                        split_low(m, i + 1, ps[:, 7, :])
                    if i + 2 < B:
                        layer_norm(m, i + 2)
                    dve.wait_ge(m.f2, i + 1)
                    dve.wait_ge(m.xb, i + 1)
                    o = ps[:, 6, 0:2 * C].rearrange("p (t c) -> p t c", t=2)
                    if l == 0:
                        v.tensor_tensor(X[:, 2 * i:2 * i + 2, :], o, XB[:], ALU.add).then_inc(m.y, 1)
                    else:
                        if i >= 2:
                            dve.wait_ge(store[i % 2], 16 * len(PIECES) * (i // 2))
                        v.tensor_tensor(Y[i % 2], o, XB[:], ALU.add).then_inc(m.y, 1)

            def bare_keys():
                bk = heads(b_v0[1][0:4, 0:C])
                for k in range(2):
                    chain(v.tensor_copy(KB[:, :, 16 * k:16 * k + 16].bitcast(F32R), bk))
                v.tensor_tensor(KB[:, :, 32:48].bitcast(F32R), bk, KB[:, :, 0:16], ALU.subtract)
                v.tensor_copy(KB[:, :, 48:64], padk[0:4, 2:3, :].broadcast_to([4, NH, 16]))
                dve.drain().then_inc(s_dve, 1)
                for p in range(2):
                    v.tensor_copy(KM[p][64:128, :, :], hot[64:128, :].unsqueeze(1).broadcast_to([64, NH, NK]))
                dve.wait_ge(s_pe, 3)
                bank = ps[:, 5, 0:PAIRS * NV].rearrange("p (m k) -> p m k", m=PAIRS)
                for p in range(2):
                    v.tensor_copy(KM[p][0:64, 0:NH:2, NT:NK], bank[0:64])
                    v.tensor_copy(KM[p][0:64, 1:NH:2, NT:NK], bank[64:128])

            weights(0)
            virtual_values(0)
            dve.wait_ge(x_in, 16 * len(PIECES) * B)
            dve.drain().then_inc(phase, 1)
            for l in range(2):
                dve.wait_ge(phase, 4 * (2 * l + 1))
                attention(l)
                dve.drain().then_inc(phase, 1)
                dve.wait_ge(phase, 4 * (2 * l + 2))
                if l == 0:
                    weights(1)
                    for p in range(NVB):
                        chain(v.memset(VE[p][:], 0.0))
                    chain(v.memset(QS[:].bitcast(F32), 0.0))
                    for t in range(2):
                        v.tensor_copy(QS[:, t, :, 48:64], padq[:, t:t + 1, :].broadcast_to([128, NH, 16]))
                    virtual_values(1)
                    bare_keys()
                mlp(l)
                if l == 0:
                    dve.drain().then_inc(phase, 1)

        @block.scalar
        def _(act):
            a = nc.scalar

            def copy(dst, src):
                return a.activation(dst, src, ACT.Copy)

            def split_high(e, i, bank, used, n):
                act.wait_ge(e.xT, i + 1)
                if i >= 1:
                    act.wait_ge(used, n * i)
                copy(XH[:, :, 0:NT], bank.rearrange("p (r t) -> p r t", r=2)).then_inc(e.xh, 1)

            def stack_high(l, i, t):
                e = E[l]
                src, qs = (QKa, QS0) if l == 0 else (QK, QS)
                if l == 0:
                    act.wait_ge(e.qkr, i + 1)
                else:
                    act.wait_ge(e.qk, 2 * i + t + 1)
                    act.wait_ge(e.sh, 4 * i + 4)
                if i >= 1:
                    act.wait_ge(e.kqT, len(KQ_ENGINE[l]) * i)
                q = heads(src[:, t, 0:C]).unsqueeze(2).broadcast_to([128, NH, 2, HD])
                k = heads(src[:, t, C:]).unsqueeze(2).broadcast_to([128, NH, 2, HD])
                copy(qs[:, t, :, 0:64].rearrange("p h (s d) -> p h s d", s=2)[:, :, :, 0:HD], q)
                if l == 1:
                    copy(qs[:, t, :, 64:64 + 2 * WS].rearrange("p h (a j) -> p a h j", a=2),
                         G[:, 2 * t:2 * t + 2, :, 0:WS])
                copy(KS[:, t, :, 0:32].rearrange("p h (s d) -> p h s d", s=2), k).then_inc(e.hi, 1)

            def queries_T(i):
                e = E[1]
                act.wait_ge(e.qfT, i + 1)
                if i >= 1:
                    act.wait_ge(e.gmm, 4 * i)
                copy(QF, misc(1, "qf", i)[0:HP, :].rearrange("p (f t) -> p f t", f=2)).then_inc(e.qf, 1)

            def relative_terms(i, n):
                e = E[1]
                if i >= 1:
                    act.wait_ge(e.lo, 2 * i)
                t, f = n // 2, n % 2
                act.wait_ge(e.gmm, 4 * i + n + 1)
                copy(G[:, 2 * t:2 * t + 2, 6 * f:6 * f + 6, :],
                     misc(1, f"g{n}", i)[:, 0:12 * NG].rearrange("p (h a j) -> p a h j", h=6, a=2))\
                    .then_inc(e.g, 1)

            def relative_exp(i):
                e = E[1]
                act.wait_ge(e.rsub, i + 1)
                a.activation(DX, DX, ACT.Exp).then_inc(e.rexp, 1)

            def probabilities(l, i, h):
                e = E[l]
                n = NH * i + h
                act.wait_ge(e.stmm, n + 1)
                if n >= 4:
                    act.wait_ge(e.av, n - 3)
                a.activation(PT[:, h % 4, :], ps[0:CH, ST_BANK + h % 2, 0:2 * NM], ACT.Exp).then_inc(e.pexp, 1)

            def output(l, i, part):
                e = E[l]
                act.wait_ge(e.ave, PAIRS * i + (4, 6)[part])
                if i >= 1 and part == 0:
                    act.wait_ge(e.oTmm, 2 * i)
                if part == 0:
                    copy(OT[:, 0:2, :], ps[:, O_BANK, :].rearrange("p (k t) -> p k t", k=2)).then_inc(e.ot, 1)
                else:
                    copy(OT[:, 2, :], ps[:, O_BANK + 1, 0:NT]).then_inc(e.ot, 1)

            def output_T(l, i):
                e = E[l]
                act.wait_ge(e.onTmm, i + 1)
                if i >= 1:
                    act.wait_ge(e.proj, i)
                copy(ONT[:], misc(l, "on", i)[0:HP, :].rearrange("p (f t) -> p f t", f=2)).then_inc(e.ont, 1)

            def maxima(l, i):
                e, p = E[l], i % 2
                act.wait_ge(e.mTmm, i + 1)
                if i >= 2:
                    act.wait_ge(e.stmm, NH * (i - 1))
                copy(mT[p][:], misc(l, "m", i)[:, 0:NT]).then_inc(e.mT, 1)

            def edge_exp(l, i, h):
                e, p = E[l], i % 2
                act.wait_ge(e.mneg, NH * i + h + 1)
                if i >= 2 and h == 0:
                    act.wait_ge(e.eTmm, 2 * (i - 1))
                a.activation(PE_[p][:, h, :], ps[:, S_BANK + h % 2, 2 * NM:2 * NM + EK], ACT.Exp,
                             bias=mneg[p][:, 1, h:h + 1]).then_inc(e.eexp, 1)

            def edges(l, i, n):
                e, p = E[l], i % 2
                m0, m1 = ((0, 4), (4, 6))[n]
                act.wait_ge(e.eTmm, 2 * i + n + 1)
                if i >= 2:
                    act.wait_ge(e.ave, PAIRS * (i - 1))
                src = misc(l, f"e{n}", i)[:, 0:128 * (m1 - m0)].rearrange("p (m q) -> p m q", q=128)
                copy(PET[p][:, m0:m1, :], src[:, :, E0:128]).then_inc(e.pet, 1)

            def attention(l):
                e = E[l]
                work = {"hi0": lambda i: stack_high(l, i, 0), "hi1": lambda i: stack_high(l, i, 1),
                        "rexp": relative_exp,
                        "out0": lambda i: output(l, i, 0), "out1": lambda i: output(l, i, 1)}
                empty = {"x": lambda i: split_high(e, i, misc(l, "x", i), e.vmm, 2), "qf": queries_T,
                         "g0": lambda i: relative_terms(i, 0), "g1": lambda i: relative_terms(i, 1),
                         "g2": lambda i: relative_terms(i, 2), "g3": lambda i: relative_terms(i, 3),
                         "m": lambda i: maxima(l, i), "e0": lambda i: edges(l, i, 0), "e1": lambda i: edges(l, i, 1),
                         "on": lambda i: output_T(l, i)}
                for g in steps(l):
                    if head_due(g, 0):
                        probabilities(l, *head_due(g, 0))
                    if head_due(g, SCORES):
                        edge_exp(l, *head_due(g, SCORES))
                    for u, i in uses_due(l, g):
                        if u in empty:
                            empty[u](i)
                        elif KQ_ENGINE[l].get(u) == KQ_ACT:
                            evacuate(l, u, i, copy, act, e.kq_act)
                    for w, i in work_due(l, g, work):
                        work[w](i)

            def mlp(l):
                m = M[l]
                split_high(m, 0, ps[:, 7, :], m.f1, 3)
                for i in range(B):
                    for k in range(MT):
                        n = 3 * i + k // 2
                        act.wait_ge(m.f1, n + 1)
                        if i >= 2 and k == 0:
                            act.wait_ge(m.f2, i - 1)
                        a.activation(GT[i % 2][:, k, :], ps[:, n % 4, NT * (k % 2):NT * (k % 2) + NT], ACT.Gelu,
                                     bias=b_1[l][:, k:k + 1]).then_inc(m.gelu, 1)
                    if i + 1 < B:
                        split_high(m, i + 1, ps[:, 7, :], m.f1, 3)

            act.drain().then_inc(phase, 1)
            for l in range(2):
                act.wait_ge(phase, 4 * (2 * l + 1))
                attention(l)
                act.drain().then_inc(phase, 1)
                act.wait_ge(phase, 4 * (2 * l + 2))
                if l == 0:
                    act.wait_ge(s_dve, setup_count("consts", None))
                mlp(l)
                if l == 0:
                    act.drain().then_inc(phase, 1)

        @block.gpsimd
        def _(pool):
            g = nc.gpsimd

            def inv_std(e, i, l):
                pool.wait_ge(e.aggr, i + 1)
                g.tensor_scalar(veps[:], mv[:, :, 1], EPS1[l], 1.0, ALU.add, ALU.mult).then_inc(e.veps, 1)
                pool.wait_ge(e.veps, i + 1)
                if i >= 1:
                    pool.wait_ge(e.xn, i)
                g.tensor_tensor(rstd[:], veps[:], nhalf[:], ALU.pow).then_inc(e.rstd, 1)

            def edge_copies(e, i):
                pool.wait_ge(e.xl, i + 1)
                for ap in (XH[:, 0, :], XH[:, 1, :], XL[:, :]):
                    g.tensor_scalar(ap[:, NK:NK + NE], ap[:, NM:NT].bitcast(F32), 1.0, 0.0, ALU.mult, ALU.add)\
                        .then_inc(e.xd, 1)

            def sine_half(i):
                e = E[0]
                pool.wait_ge(e.qk, 2 * i + 2)
                if i >= 1:
                    pool.wait_ge(e.qkr, i)
                half = HD // 2
                for k in range(2):
                    for t in range(2):
                        last = g.tensor_tensor(
                            heads(QKb[:, t, :], 2 * NH)[:, :, half * k:half * k + half],
                            heads(QK[:, t, :], 2 * NH)[:, :, half - half * k:HD - half * k],
                            sin_t[:, t:t + 1, half * k:half * k + half].broadcast_to([128, 2 * NH, half]), ALU.mult)
                    last.then_inc(e.t2, 1)

            def residual_bias(e, i, bias, done):
                if i >= 1:
                    pool.wait_ge(done, i)
                for t in range(2):
                    last = g.tensor_tensor(XB[:, t, :], X[:, 2 * i + t, :], bias[:], ALU.add)
                last.then_inc(e.xb, 1)

            weight_loads(pool, 0)
            weight_loads(pool, 1)
            pool.wait_ge(s_dve, setup_count("bias", 0))
            pool.wait_ge(x_in, 16 * len(PIECES) * B)
            pool.drain().then_inc(phase, 1)
            for l in range(2):
                e, m = E[l], M[l]
                pool.wait_ge(phase, 4 * (2 * l + 1))
                work = {"inv_std": lambda i: inv_std(e, i, l), "xd": lambda i: edge_copies(e, i), "sine": sine_half,
                        "xb": lambda i: residual_bias(e, i, b_p[l], e.x1)}
                for s in steps(l):
                    for w, i in work_due(l, s, work):
                        work[w](i)
                pool.drain().then_inc(phase, 1)
                pool.wait_ge(phase, 4 * (2 * l + 2))
                inv_std(m, 0, l)
                inv_std(m, 1, l)
                for i in range(B):
                    if i + 2 < B:
                        inv_std(m, i + 2, l)
                    residual_bias(m, i, b_2[l], m.y)
                if l == 0:
                    pool.drain().then_inc(phase, 1)

        @block.tensor
        def _(pe):
            mm = nc.tensor.matmul
            T = nc.tensor.transpose

            def fold_biases(l):
                pe.wait_ge(s_dve, setup_count("lnbw", l))
                for w0, n, o in ((0, 2 * C, ps[:, 4, 0:2 * C]), (2 * C, C, ps[:, 5, 0:C])):
                    mm(o, lnb_w[:, 0, 0, :], raw[:, 0, w0:w0 + n], start=True, stop=False)
                    mm(o, lnb_w[0:64, 0, 1, :], raw[0:64, 1, w0:w0 + n], start=False, stop=True)
                for k in range(MT):
                    w0 = 3 * C + 128 * k
                    o = ps[:, 4, 2 * C + k:2 * C + k + 1]
                    mm(o, raw[:, 0, w0:w0 + 128], lnp[:, 0, 3:4], start=True, stop=False)
                    last = mm(o, raw[0:64, 1, w0:w0 + 128], lnp[0:64, 1, 3:4], start=False, stop=True)
                last.then_inc(s_pe, 1)

            def bare_keys():
                pe.wait_ge(s_dve, setup_count("bare1", None))
                for k in range(PAIRS):
                    last = T(ps[:, 5, NV * k:NV * k + NV], KB[:, 2 * k:2 * k + 2, :], ident[0:NV, 0:NV])
                last.then_inc(s_pe, 1)

            def transpose_tokens(e, i, bank):
                pe.wait_ge(e.xn, i + 1)
                for t in range(2):
                    T(bank[:, 128 * t:128 * t + 128], xn[:, t, 0:128], ident[:])
                    last = T(bank[:, NT + 128 * t:NT + 128 * t + 128],
                             xn[:, t, 128:C + 64], ident[:])
                last.then_inc(e.xT, 1)

            def split_product(o, parts, w, flip=False):
                x0, xl, x1 = parts
                steps = ((x0, w[0]), (xl, w[0]), (x0, w[1]), (x1, w[2]), (x1, w[3]))
                for n, (x_, w_) in enumerate(steps):
                    last = mm(o, w_ if flip else x_, x_ if flip else w_, start=n == 0, stop=n == 4)
                return last

            def project_qk(l, i, t):
                e = E[l]
                pe.wait_ge(e.xl, i + 1)
                wait_misc_free(pe, l, f"qk{t}", i)
                c = slice(128 * t, 128 * t + 128)
                split_product(misc(l, f"qk{t}", i)[:, 0:2 * C], (XH[:, 0, c], XL[:, c], XH[:, 1, c]),
                              [WQ[:, k, 0:2 * C] for k in range(4)]).then_inc(e.qkmm, 1)

            def project_v(l, i):
                e = E[l]
                w = [WQ[:, k, 2 * C:] for k in range(4)]
                wait_misc_free(pe, l, "v01", i)
                for n in range(2):
                    c = slice(CH * n, CH * n + CH)
                    last = split_product(misc(l, "v01", i)[0:CH, C * n:C * n + C],
                                         (XH[:, 0, c], XL[:, c], XH[:, 1, c]), w)
                last.then_inc(e.vmm, 1)

            def project_edge_v(l, i):
                e = E[l]
                w = [WQ[:, k, 2 * C:] for k in range(4)]
                wait_misc_free(pe, l, "ve", i)
                pe.wait_ge(e.xd, 3 * (i + 1))
                split_product(misc(l, "ve", i)[:, 0:C], (XH[:, 0, NM:ND], XL[:, NM:ND], XH[:, 1, NM:ND]), w)\
                    .then_inc(e.vmm, 1)

            def transpose_queries(i):
                e = E[1]
                pe.wait_ge(e.qk, 2 * i + 2)
                wait_misc_free(pe, 1, "qf", i)
                bank = misc(1, "qf", i)
                for f in range(2):
                    for t in range(2):
                        last = T(bank[0:HP, NT * f + 128 * t:NT * f + 128 * t + 128], QK[:, t, HP * f:HP * f + HP],
                                 ident[:])
                last.then_inc(e.qfT, 1)

            def relative_products(i, n):
                e = E[1]
                pe.wait_ge(e.qf, i + 1)
                wait_misc_free(pe, 1, f"g{n}", i)
                t, f = n // 2, n % 2
                mm(misc(1, f"g{n}", i)[:, 0:12 * NG], QF[:, f, 128 * t:128 * t + 128], Rbd[:],
                   start=True, stop=True).then_inc(e.gmm, 1)

            def transpose_stacks(l, u, i):
                e = E[l]
                pe.wait_ge(e.lo, 2 * i + 2)
                wait_misc_free(pe, l, u, i)
                j = int(u[1])
                for m in range(2):
                    for t in range(2):
                        if u[0] == "k":
                            src = KS[:, t, 4 * j + 2 * m:4 * j + 2 * m + 2, :]
                        elif l == 0:
                            src = QS0[:, t, 4 * j + 2 * m:4 * j + 2 * m + 2, :]
                        else:
                            src = QS[:, t, 2 * j + m, :]
                        last = T(misc(l, u, i)[:, NT * m + 128 * t:NT * m + 128 * t + 128], src.bitcast(F32), ident[:])
                last.then_inc(e.kqT, 1)

            def query(l, i, h):
                return QT[i % 2][:, h // 2 if l == 0 else h, :]

            def scores(l, i, h):
                e, p = E[l], i % 2
                n = NH * i + h
                for u in stacks_of(l, h):
                    pe.wait_ge(*misc_emptied(l, u, i))
                if n >= 2:
                    pe.wait_ge(e.eexp, n - 1)
                q = query(l, i, h)
                bank = ps[:, S_BANK + h % 2, :]
                mm(bank[:, 0:NM], q[:, 0:128], KM[p][:, h, 0:NM], start=True, stop=True)
                mm(bank[:, NM:NM + SB], q[:, 128:NT], KM[p][:, h, :], start=True, stop=True).then_inc(e.smm, 1)

            def transpose_maxima(l, i):
                e = E[l]
                pe.wait_ge(e.mneg, NH * (i + 1))
                wait_misc_free(pe, l, "m", i)
                for t in range(2):
                    last = T(misc(l, "m", i)[:, 128 * t:128 * t + 128], mneg[i % 2][:, t, :], ident[:])
                last.then_inc(e.mTmm, 1)

            def transpose_edges(l, i, n):
                e = E[l]
                if l:
                    pe.wait_ge(e.ew, i + 1)
                else:
                    pe.wait_ge(e.eexp, NH * (i + 1))
                wait_misc_free(pe, l, f"e{n}", i)
                m0, m1 = ((0, 4), (4, 6))[n]
                for m in range(m0, m1):
                    last = T(misc(l, f"e{n}", i)[:, 128 * (m - m0):128 * (m - m0) + 128],
                             PE_[i % 2][:, 2 * m:2 * m + 2, :], ident[:])
                last.then_inc(e.eTmm, 1)

            def scores_T(l, i, h):
                e, p = E[l], i % 2
                n = NH * i + h
                if h == 0:
                    pe.wait_ge(e.mT, i + 1)
                if n >= 2:
                    pe.wait_ge(e.pexp, n - 1)
                q = query(l, i, h)
                for c in range(2):
                    o = ps[0:CH, ST_BANK + h % 2, NM * c:NM * c + NM]
                    mm(o, KM[p][:, h, CH * c:CH * c + CH], q[:, 0:NM], start=True, stop=False)
                    last = mm(o, sel[:, h, :], mT[p][:, 0:NM], start=False, stop=True)
                last.then_inc(e.stmm, 1)

            def weighted_values(l, i, h):
                e, p = E[l], i % 2
                n = NH * i + h
                pe.wait_ge(e.pexp, n + 1)
                if h == 0:
                    pe.wait_ge(e.v01, i + 1)
                    pe.wait_ge(e.ve, i + 1)
                    pe.wait_ge(e.pet, 2 * i + 2)
                if i >= 1 and h in (0, 8):
                    pe.wait_ge(e.ot, 2 * i - (h == 0))
                k, j = h // 4, h % 4
                block_o = ps[:, O_BANK + k // 2, NT * (k % 2):NT * (k % 2) + NT]
                for c in range(2):
                    last = mm(block_o[32 * j:32 * j + HD + 1, 0:NM], V01[i % NVB][:, c, h, :],
                              PT[:, h % 4, NM * c:NM * c + NM], start=c == 0, stop=c == 1)
                last.then_inc(e.av, 1)
                if h % 2:
                    m = h // 2
                    r = 64 * (m % 2)
                    mm(block_o[r:r + 64, NM:NT], VE[i % NVB][:, m, :], PET[p][:, m, :], start=True, stop=True)\
                        .then_inc(e.ave, 1)

            def transpose_output(l, i, t):
                e = E[l]
                pe.wait_ge(e.ot, 2 * i + 2)
                wait_misc_free(pe, l, f"o{t}", i)
                for k in range(3):
                    last = T(misc(l, f"o{t}", i)[:, 128 * k:128 * k + 128], OT[:, k, 128 * t:128 * t + 128],
                             ident[:])
                last.then_inc(e.oTmm, 1)

            def transpose_normalised(l, i):
                e = E[l]
                pe.wait_ge(e.on, 2 * i + 2)
                wait_misc_free(pe, l, "on", i)
                for f in range(2):
                    for t in range(2):
                        last = T(misc(l, "on", i)[0:HP, NT * f + 128 * t:NT * f + 128 * t + 128],
                                 ON[:, t, HP * f:HP * f + HP], ident[:])
                last.then_inc(e.onTmm, 1)

            def project_output(l, i):
                e = E[l]
                pe.wait_ge(e.ont, i + 1)
                wait_misc_free(pe, l, "pr", i)
                for t in range(2):
                    for f in range(2):
                        last = mm(misc(l, "pr", i)[:, C * t:C * t + C], ONT[:, f, 128 * t:128 * t + 128],
                                  WP[l][:, f, :], start=f == 0, stop=f == 1)
                last.then_inc(e.proj, 1)

            def attention(l):
                e = E[l]

                def tokens(i):
                    wait_misc_free(pe, l, "x", i)
                    transpose_tokens(e, i, misc(l, "x", i))

                fill = {"x": tokens, "qk0": lambda i: project_qk(l, i, 0), "qk1": lambda i: project_qk(l, i, 1),
                        "v01": lambda i: project_v(l, i), "ve": lambda i: project_edge_v(l, i),
                        "qf": transpose_queries,
                        "g0": lambda i: relative_products(i, 0), "g1": lambda i: relative_products(i, 1),
                        "g2": lambda i: relative_products(i, 2), "g3": lambda i: relative_products(i, 3),
                        "m": lambda i: transpose_maxima(l, i),
                        "e0": lambda i: transpose_edges(l, i, 0), "e1": lambda i: transpose_edges(l, i, 1),
                        "o0": lambda i: transpose_output(l, i, 0), "o1": lambda i: transpose_output(l, i, 1),
                        "on": lambda i: transpose_normalised(l, i), "pr": lambda i: project_output(l, i)}
                for g in steps(l):
                    uses = uses_due(l, g)

                    def fill_bank(u, i):
                        if u in fill:
                            fill[u](i)
                        else:
                            transpose_stacks(l, u, i)

                    if head_due(g, SCORES):
                        scores(l, *head_due(g, SCORES))
                    for u, i in uses[0:1]:
                        fill_bank(u, i)
                    if head_due(g, 0):
                        scores_T(l, *head_due(g, 0))
                    for u, i in uses[1:2]:
                        fill_bank(u, i)
                    if head_due(g, 1):
                        weighted_values(l, *head_due(g, 1))
                    for u, i in uses[2:]:
                        fill_bank(u, i)

            def hidden(l, i):
                m = M[l]
                pe.wait_ge(m.xl, i + 1)
                for j in range(3):
                    n = 3 * i + j
                    if n >= 4:
                        pe.wait_ge(m.gelu, 2 * (n - 3))
                    for k in (2 * j, 2 * j + 1):
                        w = [WF[l][:, r, 128 * k:128 * k + 128] for r in range(4)]
                        last = split_product(ps[:, n % 4, NT * (k % 2):NT * (k % 2) + NT],
                                             (XH[:, 0, 0:NT], XL[:, 0:NT], XH[:, 1, 0:NT]), w, flip=True)
                    last.then_inc(m.f1, 1)

            def down(l, i):
                m = M[l]
                pe.wait_ge(m.gelu, MT * (i + 1))
                if i >= 1:
                    pe.wait_ge(m.y, i)
                for t in range(2):
                    for k in range(MT):
                        last = mm(ps[:, 6, C * t:C * t + C], GT[i % 2][:, k, 128 * t:128 * t + 128], W2[l][:, k, :],
                                  start=k == 0, stop=k == MT - 1)
                last.then_inc(m.f2, 1)

            def mlp(l):
                m = M[l]
                transpose_tokens(m, 0, ps[:, 7, :])
                for i in range(B):
                    hidden(l, i)
                    if i + 1 < B:
                        transpose_tokens(m, i + 1, ps[:, 7, :])
                    if i:
                        down(l, i - 1)
                down(l, B - 1)

            pe.wait_ge(w_in[0], N_W)
            pe.wait_ge(s_dve, setup_count("consts", None))
            fold_biases(0)
            pe.drain().then_inc(phase, 1)
            for l in range(2):
                pe.wait_ge(phase, 4 * (2 * l + 1))
                attention(l)
                pe.drain().then_inc(phase, 1)
                pe.wait_ge(phase, 4 * (2 * l + 2))
                if l == 0:
                    fold_biases(1)
                    bare_keys()
                mlp(l)
                if l == 0:
                    pe.drain().then_inc(phase, 1)


def tables():
    import numpy as np

    rows = np.array([n // WS for n in range(NM)] + [r for r in range(WS) for _ in range(W - WS)]
                    + [r for r in range(WS, H) for _ in range(W)])
    cols = np.array([n % WS for n in range(NM)] + [c for _ in range(WS) for c in range(WS, W)]
                    + [c for _ in range(WS, H) for c in range(W)])
    group = np.where((rows < WS) & (cols < WS), 3, np.where(rows < WS, 0, np.where(cols < WS, 1, 2)))
    qr, qc = rows % WS, cols % WS
    onehot = (group[:, None] == np.arange(4)[None, :]).astype(np.float32)
    t = {"ident": np.eye(128, dtype=np.float32)}

    def tiles(a):
        return np.ascontiguousarray(a.reshape(2, 128, *a.shape[1:]).swapaxes(0, 1))

    padq = np.zeros((NT, 16), np.float32)
    padq[:, 0:4] = onehot
    padk = np.zeros((NT, 16), np.float32)
    padk[:, 0:4] = -BIG * (1 - onehot)
    seen = np.array([[1, 1, 1, 0], [1, 0, 1, 0], [0, 1, 1, 0], [0, 0, 0, 0]], np.float32)
    virt = np.zeros((128, 1, 16), np.float32)
    virt[0:4, 0, 0:4] = -BIG * (1 - seen)
    t["padq"] = tiles(padq)
    t["padk"] = np.concatenate([tiles(padk), virt], 1)
    own = np.concatenate([np.eye(4, dtype=np.float32)[0:3], np.zeros((1, 4), np.float32)])
    kv = np.zeros((128, NH, NV), np.float32)
    for h in range(NH):
        r = 64 * (h % 2) + 48
        kv[r:r + 4, h, :] = -BIG * (1 - own.T)
    t["kvirt"] = kv
    hot = np.zeros((64, NK), np.float32)
    for r0 in (0, 32):
        hot[r0 + qr, np.arange(NT)] = 1
        hot[r0 + WS + qc, np.arange(NT)] = 1
        hot[r0 + 2 * WS + np.arange(3), NT + np.arange(3)] = 1
    t["hot"] = hot
    vc = np.zeros((128, 2, 2, 2), np.float32)
    counts = [NM - WS * (W - WS), NM - WS * (H - WS), NM - (H - WS) * (W - WS)]
    for k in range(2):
        r = 64 * k
        vc[r:r + NE, :, k, 1] = 1
        for g in range(3):
            vc[r + NE + g, 0, k, :] = counts[g]
            vc[r + NE + g, 1, k, :] = 1
    t["vcon"] = vc
    shm = np.zeros((NT, 2, 4), np.int32)
    for k, s in enumerate((8, 4, 2, 1)):
        shm[:, 0, k] = ((WS - 1 - qr) & s) > 0
        shm[:, 1, k] = ((WS - 1 - qc) & s) > 0
    t["shm"] = np.ascontiguousarray(tiles(shm).reshape(128, 4, 4))
    token = rows * W + cols
    return t, token


def kernel(**inputs):
    import numpy as np
    import concourse.bacc as bacc
    from concourse.bass_utils import run_bass_kernel_spmd

    a = {k: np.asarray(v) for k, v in inputs.items()}
    tab, token = tables()
    arrays = {"x": a["x"]}

    def bc(v):
        return np.ascontiguousarray(np.broadcast_to(v, (128, v.shape[-1])))

    def by_tile(v):
        return np.ascontiguousarray(v.reshape(2, 128, -1).swapaxes(0, 1))

    rope = a["L0_conv_rope_2d"].reshape(NT, HD)[token]
    half = HD // 2
    sin, cos = rope[:, :half], rope[:, half:]
    arrays["cos"] = by_tile(np.concatenate([cos, cos], 1))
    arrays["sin"] = by_tile(np.concatenate([sin, sin], 1))
    for n, v in tab.items():
        arrays[n] = v
    arrays["gamma1"], arrays["gamma2"] = bc(a["L0_conv_gamma_1"]), bc(a["L0_conv_gamma_2"])
    R = np.zeros((2, NG, HD), np.float32)
    for k, n in enumerate(("h", "w")):
        R[k, 0:2 * WS - 1] = a[f"L1_conv_rel_pos_{n}"][::-1]
    rbd = np.zeros((6, HD, 6, 2, NG), np.float32)
    for h in range(6):
        rbd[h, :, h] = R.transpose(2, 0, 1)
    arrays["rbd"] = rbd.reshape(HP, 6 * 2 * NG)
    for l in range(2):
        g = (lambda n: a[f"L0_conv_{n}"]) if l == 0 else (lambda n: a[f"L1_conv_{n}"])
        if l == 0:
            wqkv, wproj, w1, w2 = g("w_qkv").T, g("w_proj").T, g("w_fc1").T, g("w_fc2").T
            ln = [g("ln1_g"), g("ln1_b"), g("ln2_g"), g("ln2_b")]
            bs = [g("b_qkv"), g("b_proj"), g("b_fc1"), g("b_fc2")]
        else:
            wqkv, wproj, w1, w2 = g("qkv_w"), g("proj_w"), g("fc1_w"), g("fc2_w")
            ln = [g("ln1_w"), g("ln1_b"), g("ln2_w"), g("ln2_b")]
            bs = [g("qkv_b"), g("proj_b"), g("fc1_b"), g("fc2_b")]
        arrays[f"wqkv{l}"] = wqkv
        arrays[f"w1{l}"] = w1
        arrays[f"wproj{l}"] = wproj.reshape(2, HP, C).swapaxes(0, 1)
        arrays[f"w2{l}"] = w2.reshape(MT, 128, C).swapaxes(0, 1)
        ln = np.stack(ln, 1)
        arrays[f"ln{l}"] = np.stack([ln[0:128], np.concatenate([ln[128:C], ln[128:C]])], 1)
        arrays[f"bqkv{l}"], arrays[f"bproj{l}"], arrays[f"b2{l}"] = bc(bs[0]), bc(bs[1]), bc(bs[3])
        arrays[f"b1{l}"] = bs[2].reshape(MT, 128).T

    nc = bacc.Bacc("TRN2", target_bir_lowering=False, num_devices=1)
    arrays = {f"in_{n}": np.ascontiguousarray(v) for n, v in arrays.items()}
    d = {n[3:]: nc.dram_tensor(n, v.shape, mybir.dt.from_np(v.dtype), kind="ExternalInput").ap()
         for n, v in arrays.items()}
    out = nc.dram_tensor("out_0", (B, H, W, C), F32, kind="ExternalOutput").ap()
    names = ("wqkv", "w1", "wproj", "w2", "ln", "bqkv", "bproj", "b2", "b1")
    extra = (dict(gamma1=d["gamma1"], gamma2=d["gamma2"], rbd=None), dict(gamma1=None, gamma2=None, rbd=d["rbd"]))
    layers = [Block(**{n: d[f"{n}{l}"] for n in names}, **extra[l]) for l in range(2)]
    build(nc, d["x"], d["cos"], d["sin"], layers, {n: d[n] for n in tab}, out)
    r = run_bass_kernel_spmd(nc, [arrays], core_ids=[0])
    return r.results[0]["out_0"]
```

```python
from collections import namedtuple
from contextlib import ExitStack

import concourse.bass as bass
from concourse import mybir

ALU = mybir.AluOpType
ACT = mybir.ActivationFunctionType
AX = mybir.AxisListType.X
F32 = mybir.dt.float32
F32R = mybir.dt.float32r
I32 = mybir.dt.int32

B, H, W, C = 8, 16, 16, 192
NH, HD = 12, 16
WS = 14
NT = H * W
NM = WS * WS
NE = NT - NM
CH = NM // 2
NV = 4
NK = NT + NV
EK = NE + NV
ND = NM + 2 * EK
SB = NM + EK
F = 4 * C
MT = F // 128
PAIRS = NH // 2
NG = 2 * WS + 1
E0 = NM - 128
HP = 96
NVB = 3
BIG = 1.0e30
EPS1 = (1e-6, 1e-5)
KSCALE = float(HD) ** -0.5

KQ_ACT, KQ_DVE = "act", "dve"
KQ_ENGINE = (
    {"k0": KQ_DVE, "k1": KQ_DVE, "k2": KQ_ACT, "q0": KQ_DVE, "q1": KQ_DVE, "q2": KQ_ACT},
    {"k0": KQ_ACT, "k1": KQ_ACT, "k2": KQ_ACT, "q0": KQ_ACT, "q1": KQ_ACT, "q2": KQ_ACT, "q3": KQ_ACT, "q4":
     KQ_ACT, "q5": KQ_ACT},
)


Norm = namedtuple("Norm", "stats mv veps rstd xn XH XL")
Block = namedtuple("Block", "wqkv w1 wproj w2 ln bqkv bproj b2 b1 gamma1 gamma2 rbd")


def build(nc, x, rope_cos, rope_sin, layers, consts, out):
    ctx = ExitStack()
    with ctx:
        def sb(name, shape, dt=F32):
            return ctx.enter_context(nc.sbuf_tensor(name, shape, dt))

        def sem(name):
            return ctx.enter_context(nc.semaphore(name))

        ps = ctx.enter_context(nc.psum_tensor("ps", [128, 8, 512], F32))
        S_BANK, ST_BANK, O_BANK, MISC = 0, 2, 4, 6

        X = sb("X", [128, 2 * B, C])
        XB = sb("XB", [128, 2, C])
        nhalf = sb("nhalf", [128, 2])
        WQ = sb("WQ", [128, 4, 3 * C], F32R)
        WF = [sb(f"WF{l}", [128, 4, F], F32R) for l in range(2)]
        WP = [sb(f"WP{l}", [HP, 2, C]) for l in range(2)]
        W2 = [sb(f"W2{l}", [128, MT, C]) for l in range(2)]
        b_qkv = [sb(f"b_qkv{l}", [128, 3 * C]) for l in range(2)]
        b_v0 = [sb(f"b_v0{l}", [128, 2 * C]) for l in range(2)]
        b_p = [sb(f"b_p{l}", [128, C]) for l in range(2)]
        b_2 = [sb(f"b_2{l}", [128, C]) for l in range(2)]
        b_1 = [sb(f"b_1{l}", [128, MT]) for l in range(2)]
        gam = sb("gam", [128, 2, C])
        lnp = sb("lnp", [128, 2, 4])
        g4 = sb("g4", [128, 2])
        lnb_w = sb("lnb_w", [128, 2, 2, 128])
        raw = sb("raw", [128, 2, 3 * C + F])
        ident = sb("ident", [128, 128])
        sel = sb("sel", [128, NH, CH], F32R)
        cos_t = sb("cos_t", [128, 2, HD])
        sin_t = sb("sin_t", [128, 2, HD])
        padq = sb("padq", [128, 2, 16])
        padk = sb("padk", [128, 3, 16])
        kvirt = sb("kvirt", [128, NH, NV])
        hot = sb("hot", [128, NK])
        vcon = sb("vcon", [128, 2, 2, 2])
        shm = sb("shm", [128, 4, 4], I32)
        Rbd = sb("Rbd", [HP, 6 * 2 * NG])
        QK = sb("QK", [128, 2, 2 * C])
        QKab = sb("QKab", [128, 4, 2 * C])
        QKa, QKb = QKab[:, 0:2, :], QKab[:, 2:4, :]
        QS = sb("QS", [128, 2, NH, 128], F32R)
        QS0 = QS[:, :, 0:PAIRS, :].rearrange("p t m (s d) -> p t (m s) d", s=2)
        KS = sb("KS", [128, 2, NH, 64], F32R)
        QT = [sb(f"QT{p}", [128, NH, NT], F32R) for p in range(2)]
        KM = [sb(f"KM{p}", [128, NH, NK], F32R) for p in range(2)]
        V01 = [sb(f"V01{p}", [CH, 2, NH, HD + 1]) for p in range(NVB)]
        VE = [sb(f"VE{p}", [128, PAIRS, 64]) for p in range(NVB)]
        mneg = [sb(f"mneg{p}", [128, 2, 128]) for p in range(2)]
        mT = [sb(f"mT{p}", [128, NT], F32R) for p in range(2)]
        PTb = sb("PTb", [128, 4 * 2 * NM])
        PT = PTb[0:CH, :].rearrange("p (s n) -> p s n", s=4)
        PE_ = [sb(f"PE{p}", [128, NH, EK]) for p in range(2)]
        PET = [sb(f"PET{p}", [128, PAIRS, NE]) for p in range(2)]
        OT = sb("OT", [128, 3, NT])
        rden = sb("rden", [128, 2, NH])
        ON = sb("ON", [128, 2, C])
        ONT = sb("ONT", [HP, 2, NT])
        def norm_buffers(k, xn, XH, XL):
            return Norm(sb(f"stats{k}", [128, 2, 6]), sb(f"mv{k}", [128, 2, 2]), sb(f"veps{k}", [128, 2]),
                        sb(f"rstd{k}", [128, 2]), xn, XH, XL)

        NA = norm_buffers("a", sb("xn", [128, 2, C + 64]), sb("XH", [128, 2, ND], F32R), sb("XL", [128, ND], F32R))
        NP = norm_buffers("m", PE_[0][:].rearrange("p h k -> p (h k)")[:, 0:2 * (C + 64)].rearrange("p (t c) -> p t c", t=2),
                           QT[1][:, 0:2, :], QT[1][:, 2, :])
        rawf = raw[:].rearrange("p r n -> p (r n)")
        nG = 4 * NH * NG
        G = rawf[:, 0:nG].rearrange("p (a h j) -> p a h j", a=4, h=NH)
        QF = rawf[0:HP, nG:nG + 2 * NT].rearrange("p (f t) -> p f t", f=2)
        at = nG + 2 * NT
        DX = rawf[:, at:at + 2 * NH * WS].rearrange("p (a h j) -> p a h j", a=2, h=NH)
        at += 2 * NH * WS
        Mx = rawf[:, at:at + 4 * NH].rearrange("p (k a h) -> p k a h", k=2, a=2)
        SX = rawf[:, at + 4 * NH:at + 8 * NH].rearrange("p (k a h) -> p k a h", k=2, a=2)
        at += 8 * NH
        Mr = rawf[:, at:at + 3 * NH].rearrange("p (h r) -> p h r", r=3)
        at += 3 * NH
        Wr = [rawf[:, at + 3 * NH * p:at + 3 * NH * (p + 1)].rearrange("p (h r) -> p h r", r=3)
              for p in range(2)]
        KB = QT[0][0:NV, 0:3, :].rearrange("p a t -> p (a t)").rearrange("p (h d) -> p h d", h=NH)
        GT = [PTb[:, 0:MT * NT].rearrange("p (m t) -> p m t", m=MT),
              QKab[:].rearrange("p a n -> p (a n)").rearrange("p (m t) -> p m t", m=MT)]
        Y = [OT[:].rearrange("p k t -> p (k t)")[:, 2 * C * p:2 * C * p + 2 * C].rearrange("p (t c) -> p t c", t=2)
             for p in range(2)]

        def events(prefix, names):
            return namedtuple(prefix, names)(*[sem(f"{prefix}_{n}") for n in names.split()])

        ATT = ("stats aggr veps rstd xn xT xh xl xd qkmm qk vmm v01 ve "
               "t1 t2 qkr hi lo kqT kq_act kq_dve "
               "smm mneg mTmm mT eexp eTmm pet "
               "stmm pexp av ave ot oTmm rden on onTmm ont proj xb x1")
        REL = "qfT qf gmm g sh rmax rsub rexp rsum rmul qrel ew"
        E = [events("a0", ATT), events("a1", ATT + " " + REL)]
        M = [events(f"m{l}", "stats aggr veps rstd xn xT xh xl f1 gelu f2 xb y") for l in range(2)]
        x_in = [sem(f"x_in{i}") for i in range(B)]
        c_in = sem("c_in")
        store = [sem(f"store{p}") for p in range(2)]
        wq_in = [sem(f"wq_in{l}") for l in range(2)]
        wf_in = [sem(f"wf_in{l}") for l in range(2)]
        ready_setup = sem("ready_setup")
        S = events("setup", "cleared lnb fold_qkv fold_fc1 wq wf b_qkv b_fc1 scales bare bareT")
        phase = sem("phase")

        SCORES = -15
        USES = (
            {"x": -31, "qk0": -30, "qk1": -26, "v01": -21, "ve": -20, "k0": -19, "q0": -17, "q1": -16, "k1":
             -15, "q2": -11, "k2": -11, "m": -1, "e0": -1, "e1": 0, "o0": 14, "o1": 14, "on": 16, "pr": 19},
            {"x": -34, "qk0": -32, "qk1": -32, "qf": -30, "g0": -28, "g1": -28, "g2": -27, "g3": -27, "v01":
             -24, "ve": -23, "k0": -19, "q0": -18, "q2": -18, "q1": -17, "q3": -16, "k1": -14, "q4": -13, "k2":
             -13, "q5": -11, "m": -2, "e0": 0, "e1": 0, "o0": 14, "o1": 15, "on": 17, "pr": 19},
        )
        WORK = (
            {"stats": -37, "inv_std": -36, "xn": -31, "cosine": -24, "sine": -26, "rotate": -22, "hi0": -21,
             "hi1": -21, "lo0": -20, "lo1": -20, "out0": 11, "out1": 12, "xb": 11, "xd": -29, "hk0": -21, "hk1":
             -21, "lk0": -20, "lk1": -20},
            {"stats": -39, "inv_std": -39, "xn": -38, "sh0": -26, "sh1": -25, "sh2": -24, "sh3": -24, "bounds":
             -23, "qrel": -22, "hi0": -24, "hi1": -22, "lo0": -23, "lo1": -21, "rexp": -22, "sums": -18, "ew":
             -1, "out0": 9, "out1": 12, "xb": 18, "xd": -36, "hk0": -23, "hk1": -21, "lk0": -21, "lk1": -21},
        )

        def steps(l):
            return range(min(WORK[l].values()), NH * (B - 1) + max(USES[l].values()) + 1)

        FILL_FROM, FILL_PER = 1, 3
        first = steps(1)[0]
        fill_end = [min(SCORES, first + FILL_PER * max(i - FILL_FROM, 0)) for i in range(B + 1)] + [SCORES]
        FILL = [range(fill_end[i], fill_end[i + 1]) for i in range(B + 1)]
        REST = range(SCORES, steps(1)[-1] + 1)
        MLP_AT = NH * B + 1
        NORM_AT = MLP_AT - 5

        def due(g, step):
            n, r = divmod(g - step, NH)
            return n if r == 0 and 0 <= n < B else None

        def head_due(g, step):
            n, h = divmod(g - step, NH)
            return (n, h) if 0 <= n < B else None

        def uses_due(l, g):
            return [(u, due(g, s)) for u, s in USES[l].items() if due(g, s) is not None]

        EARLY = ("stats", "inv_std", "xn")

        def work_due(l, g, names):
            return [(w, due(g, WORK[l][w])) for w in names if w in WORK[l] and due(g, WORK[l][w]) is not None
                    and not (l == 0 and due(g, WORK[l][w]) == 0 and w in EARLY)]

        def turns(l):
            return [use for g in steps(l) for use in uses_due(l, g)]

        ORDER = [turns(l) for l in range(2)]
        TURN = [{u: n for n, u in enumerate(o)} for o in ORDER]

        def kq_turn(l, u):
            return [n for n in USES[l] if n in KQ_ENGINE[l]].index(u)

        def kq_count(l, u, i):
            mine = [n for n in USES[l] if n in KQ_ENGINE[l] and KQ_ENGINE[l][n] == KQ_ENGINE[l][u]]
            return len(mine) * i + mine.index(u) + 1

        def stacks_of(l, h):
            return f"k{h // 4}", (f"q{h // 2}" if l else f"q{h // 4}")

        def misc_emptied(l, u, i):
            e = E[l]
            if u in KQ_ENGINE[l]:
                return (e.kq_act if KQ_ENGINE[l][u] == KQ_ACT else e.kq_dve), kq_count(l, u, i)
            if u[0] == "g":
                return e.g, 4 * i + int(u[1]) + 1
            return {"x": (e.xl, i + 1), "qk0": (e.qk, 2 * i + 1), "qk1": (e.qk, 2 * i + 2),
                    "v01": (e.v01, i + 1), "ve": (e.ve, i + 1),
                    "qf": (e.qf if l else None, i + 1),
                    "m": (e.mT, i + 1), "e0": (e.pet, 2 * i + 1), "e1": (e.pet, 2 * i + 2),
                    "o0": (e.on, 2 * i + 1), "o1": (e.on, 2 * i + 2), "on": (e.ont, i + 1),
                    "pr": (e.x1, i + 1)}[u]

        def misc(l, u, i):
            return ps[:, MISC + TURN[l][u, i] % 2, :]

        def wait_misc_free(pe, l, u, i):
            n = TURN[l][u, i]
            if l == 1 and n < 2:
                pe.wait_ge(E[0].x1, B)
            if n >= 2:
                s, v = misc_emptied(l, *ORDER[l][n - 2])
                pe.wait_ge(s, v)

        def evacuate(l, u, i, copy, eng, done):
            e, p = E[l], i % 2
            names = list(KQ_ENGINE[l])
            j = int(u[1])
            if i >= 2:
                h = 2 * j + 1 if l and u[0] == "q" else 4 * j + 3
                eng.wait_ge(e.stmm, NH * (i - 2) + h + 1)
            eng.wait_ge(e.kqT, len(names) * i + kq_turn(l, u) + 1)
            bank = misc(l, u, i).rearrange("p (m t) -> p m t", m=2)
            if u[0] == "q":
                copy(QT[p][:, 2 * j:2 * j + 2, :], bank).then_inc(done, 1)
            else:
                odd = slice(64, 128) if l == 0 else slice(0, 64)
                copy(KM[p][0:64, 4 * j:4 * j + 3:2, 0:NT], bank[0:64])
                copy(KM[p][odd, 4 * j + 1:4 * j + 4:2, 0:NT], bank[64:128]).then_inc(done, 1)

        def heads(ap, n=NH):
            return ap.rearrange("p (h d) -> p h d", h=n)

        def normalised_tokens(eng, tensor_scalar, e, b, i):
            eng.wait_ge(e.rstd, i + 1)
            if i >= 1:
                eng.wait_ge(e.xT, i)
            for t in range(2):
                for dst, c0 in ((b.xn[:, t, 0:C], 0), (b.xn[:, t, C:C + 64], 128)):
                    last = tensor_scalar(dst, X[:, 2 * i + t, c0:C], b.mv[:, t, 0:1], b.rstd[:, t:t + 1],
                                         ALU.subtract, ALU.mult)
            last.then_inc(e.xn, 1)

        block = ctx.enter_context(nc.Block())

        PIECES = [
            (0, 0, (0, 9), (0, WS)),
            (0, 126, (9, 10), (0, 2)),
            (1, 0, (9, 10), (2, WS)),
            (1, 12, (10, WS), (0, WS)),
            (1, E0, (0, WS), (WS, W)),
            (1, E0 + 28, (WS, H), (0, W)),
        ]

        def piece_size(rows, cols):
            return (rows[1] - rows[0]) * (cols[1] - cols[0])

        N_CONST = 12 * 16
        N_WQ, N_WF = 6 * 16, 8 * 16

        def weight_loads(q, l):
            ly = layers[l]
            for dst, src in ((raw[:, 0, 0:3 * C], ly.wqkv[0:128, :]), (raw[0:64, 1, 0:3 * C], ly.wqkv[128:C, :]),
                             (raw[64:128, 1, 0:3 * C], ly.wqkv[128:C, :]), (lnp[:], ly.ln),
                             (b_qkv[l][:], ly.bqkv), (b_v0[l][:], ly.bqkv[:, C:])):
                q.dma_start(dst, src).then_inc(wq_in[l], 16)
            for dst, src in ((raw[:, 0, 3 * C:], ly.w1[0:128, :]), (raw[0:64, 1, 3 * C:], ly.w1[128:C, :]),
                             (raw[64:128, 1, 3 * C:], ly.w1[128:C, :]),
                             (WP[l][:], ly.wproj), (W2[l][:], ly.w2),
                             (b_p[l][:], ly.bproj), (b_2[l][:], ly.b2), (b_1[l][:], ly.b1)):
                q.dma_start(dst, src).then_inc(wf_in[l], 16)

        @block.sync
        def _(sp):
            def load_image(b0):
                for t, p0, rows, cols in PIECES:
                    n = piece_size(rows, cols)
                    sp.dma_start(X[p0:p0 + n, 2 * b0 + t, :], x[b0, rows[0]:rows[1], cols[0]:cols[1], :])\
                        .then_inc(x_in[b0], 16)

            load_image(0)
            for dst, src in ((ident[:], consts["ident"]), (padq[:], consts["padq"]),
                             (padk[:], consts["padk"]), (cos_t[:], rope_cos), (sin_t[:], rope_sin),
                             (vcon[:], consts["vcon"]), (kvirt[:], consts["kvirt"]),
                             (hot[64:128, :], consts["hot"]), (shm[:], consts["shm"]),
                             (Rbd[:], layers[1].rbd), (gam[:, 0, :], layers[0].gamma1),
                             (gam[:, 1, :], layers[0].gamma2)):
                sp.dma_start(dst, src).then_inc(c_in, 16)
            for b0 in range(1, B):
                load_image(b0)
            sp.wait_ge(S.wf, 1)
            sp.wait_ge(S.fold_fc1, 1)
            weight_loads(sp, 1)
            for i in range(B):
                sp.wait_ge(M[1].y, i + 1)
                for t, p0, rows, cols in PIECES:
                    n = piece_size(rows, cols)
                    sp.dma_start(out[i, rows[0]:rows[1], cols[0]:cols[1], :], Y[i % 2][p0:p0 + n, t, :])\
                        .then_inc(store[i % 2], 16)
            for p in range(2):
                sp.wait_ge(store[p], 16 * len(PIECES) * B // 2)


        @block.vector
        def _(dve):
            v = nc.vector

            def chain(ins, count=[0]):
                count[0] += 1
                ins.then_inc(ready_setup, 1)
                dve.wait_ge(ready_setup, count[0])

            def scaled(l, r, dst, w0, n, src0, gain):
                src = raw[:, r, src0:src0 + n]
                chain(v.tensor_scalar(dst[:, 2 * r, w0:w0 + n], src, gain, None, ALU.mult))
                return v.scalar_tensor_tensor(dst[:, 2 * r + 1, w0:w0 + n], src, gain,
                                              dst[:, 2 * r, w0:w0 + n].bitcast(F32), ALU.mult, ALU.subtract)

            def spread_biases(l):
                dve.wait_ge(wq_in[l], N_WQ)
                for k in range(2):
                    for r in range(2):
                        last = v.tensor_copy(lnb_w[:, k, r, :], lnp[:, r, 1 + 2 * k:2 + 2 * k].broadcast_to([128, 128]))
                last.then_inc(S.lnb, 1)

            def qkv_weights(l):
                chain(v.tensor_scalar(g4[:], lnp[:, :, 0], KSCALE, None, ALU.mult))
                for r in range(2):
                    scaled(l, r, WQ, 0, C, 0, lnp[:, r, 0:1])
                    scaled(l, r, WQ, C, C, C, g4[:, r:r + 1])
                    last = scaled(l, r, WQ, 2 * C, C, 2 * C, lnp[:, r, 0:1])
                last.then_inc(S.wq, 1)

            def qkv_biases(l):
                dve.wait_ge(S.fold_qkv, l + 1)
                chain(v.tensor_tensor(b_qkv[l][:, 0:2 * C], ps[:, 4, 0:2 * C], b_qkv[l][:, 0:2 * C], ALU.add))
                chain(v.tensor_tensor(b_qkv[l][:, 2 * C:], ps[:, 5, 0:C], b_qkv[l][:, 2 * C:], ALU.add))
                v.tensor_scalar(b_v0[l][:, 0:C], b_v0[l][:, 0:C], KSCALE, None, ALU.mult)
                v.tensor_scalar(b_qkv[l][:, C:2 * C], b_qkv[l][:, C:2 * C], KSCALE, None, ALU.mult)\
                    .then_inc(S.b_qkv, 1)

            def fc1_weights(l, r):
                dve.wait_ge(wf_in[l], N_WF)
                last = scaled(l, r, WF[l], 0, F, 3 * C, lnp[:, r, 2:3])
                if r:
                    last.then_inc(S.wf, 1)

            def fc1_biases(l):
                dve.wait_ge(S.fold_fc1, l + 1)
                v.tensor_tensor(b_1[l][:], ps[:, 3, 0:MT], b_1[l][:], ALU.add).then_inc(S.b_fc1, 1)

            def layer_scales(k):
                dve.wait_ge(wf_in[0], N_WF)
                if k == 0:
                    chain(v.tensor_tensor(WP[0][:], WP[0][:], gam[0:HP, 0:1, :].broadcast_to([HP, 2, C]), ALU.mult))
                    chain(v.tensor_tensor(b_p[0][:], b_p[0][:], gam[:, 0, :], ALU.mult))
                    v.tensor_tensor(b_2[0][:], b_2[0][:], gam[:, 1, :], ALU.mult).then_inc(S.scales, 1)
                else:
                    v.tensor_tensor(W2[0][:], W2[0][:], gam[:, 1:2, :].broadcast_to([128, MT, C]), ALU.mult)

            def constants():
                dve.wait_ge(c_in, N_CONST)
                dve.wait_ge(S.cleared, 1)
                for t in range(2):
                    v.tensor_copy(QS0[:, t, :, 48:64], padq[:, t:t + 1, :].broadcast_to([128, NH, 16]))
                    v.tensor_copy(KS[:, t, :, 48:64], padk[:, t:t + 1, :].broadcast_to([128, NH, 16]))
                for p in range(NVB):
                    v.memset(V01[p][:, :, :, HD:HD + 1], 1.0)
                for p in range(2):
                    v.tensor_copy(KM[p][:, :, NT:NK], kvirt[:])
                v.tensor_copy(sel[:], ident[:, 0:NH].unsqueeze(2).broadcast_to([128, NH, CH]))
                chain(v.tensor_scalar(sin_t[:, :, 0:HD // 2], sin_t[:, :, 0:HD // 2], -1.0, None, ALU.mult))

            def virtual_values(l):
                for p in range(NVB):
                    for k in range(2):
                        dst = VE[p][:, :, 32 * k:32 * k + HD]
                        src = b_v0[l][:, C:].rearrange("p (m k d) -> p m k d", k=2, d=HD)[:, :, k, :]
                        v.tensor_scalar(dst, src, vcon[:, l, k, 0:1], None, ALU.mult)
                        last = v.tensor_copy(VE[p][:, :, 32 * k + HD:32 * k + HD + 1],
                                             vcon[:, l, k, 1:2].unsqueeze(1).broadcast_to([128, PAIRS, 1]))
                chain(last)

            def statistics(e, b, i, ready, count):
                dve.wait_ge(ready, count)
                if i >= 1:
                    dve.wait_ge(e.aggr, i)
                for t in range(2):
                    last = v.bn_stats(b.stats[:, t, :], X[:, 2 * i + t, :])
                last.then_inc(e.stats, 1)
                dve.wait_ge(e.stats, i + 1)
                if i >= 1:
                    dve.wait_ge(e.veps, i)
                    dve.wait_ge(e.xn, i)
                for t in range(2):
                    last = v.bn_aggr(b.mv[:, t, :], b.stats[:, t, :])
                last.then_inc(e.aggr, 1)

            def split_low(e, b, i, bank):
                dve.wait_ge(e.xh, i + 1)
                v.tensor_tensor(b.XL[:, 0:NT], bank[:, 0:NT], b.XH[:, 0, 0:NT].bitcast(F32), ALU.subtract)
                v.tensor_tensor(b.XH[64:128, 1, 0:NT], bank[64:128, NT:2 * NT], b.XH[64:128, 1, 0:NT].bitcast(F32),
                                ALU.subtract).then_inc(e.xl, 1)

            def queries_keys(l, i, t):
                e = E[l]
                dve.wait_ge(e.qkmm, 2 * i + t + 1)
                if i >= 1 and t == 0:
                    dve.wait_ge(e.lo, 4 * i)
                    if l == 0:
                        dve.wait_ge(e.t2, 2 * i)
                    else:
                        dve.wait_ge(e.hi, 4 * i)
                        dve.wait_ge(e.qfT, i)
                v.tensor_tensor(QK[:, t, :], misc(l, f"qk{t}", i)[:, 0:2 * C], b_qkv[l][:, 0:2 * C],
                                ALU.add).then_inc(e.qk, 1)

            def cosine_half(i):
                e = E[0]
                dve.wait_ge(e.qk, 2 * i + 2)
                if i >= 1:
                    dve.wait_ge(e.hi, 4 * i)
                    dve.wait_ge(e.lo, 4 * i)
                for t in range(2):
                    last = v.tensor_tensor(heads(QKa[:, t, :], 2 * NH), heads(QK[:, t, :], 2 * NH),
                                           cos_t[:, t:t + 1, :].broadcast_to([128, 2 * NH, HD]), ALU.mult)
                last.then_inc(e.t1, 1)

            def rotate(i):
                e = E[0]
                dve.wait_ge(e.t1, i + 1)
                dve.wait_ge(e.t2, 2 * i + 2)
                v.tensor_tensor(QKa, QKa, QKb, ALU.add).then_inc(e.qkr, 1)

            def main_values(l, i):
                e = E[l]
                dve.wait_ge(e.vmm, 2 * i + 1)
                if i >= NVB:
                    dve.wait_ge(e.av, NH * (i - NVB + 1))
                for c in range(2):
                    last = v.tensor_tensor(V01[i % NVB][:, c, :, 0:HD], heads(misc(l, "v01", i)[0:CH, C * c:C * c + C]),
                                           heads(b_qkv[l][0:CH, 2 * C:]), ALU.add)
                last.then_inc(e.v01, 1)

            def edge_values(l, i):
                e = E[l]
                dve.wait_ge(e.vmm, 2 * i + 2)
                if i >= NVB:
                    dve.wait_ge(e.ave, PAIRS * (i - NVB + 1))
                for k in range(2):
                    r = slice(64 * k, 64 * k + NE)
                    last = v.tensor_tensor(
                        VE[i % NVB][r, :, 32 * k:32 * k + HD],
                        misc(l, "ve", i)[r, 0:C].rearrange("p (m k d) -> p m k d", k=2, d=HD)[:, :, k, :],
                        b_qkv[l][r, 2 * C:].rearrange("p (m k d) -> p m k d", k=2, d=HD)[:, :, k, :], ALU.add)
                last.then_inc(e.ve, 1)

            def stack_low(l, i, t, keys):
                e = E[l]
                src, qs = (QKa, QS0) if l == 0 else (QK, QS)
                dve.wait_ge(e.hi, 4 * i + 2 * t + keys + 1)
                if keys:
                    last = v.tensor_tensor(KS[:, t, :, 32:48], heads(src[:, t, C:]), KS[:, t, :, 0:16].bitcast(F32),
                                           ALU.subtract)
                else:
                    last = v.tensor_tensor(qs[:, t, :, 16:32], heads(src[:, t, 0:C]), qs[:, t, :, 0:16].bitcast(F32),
                                           ALU.subtract)
                    if l == 1:
                        last = v.tensor_tensor(
                            qs[:, t, :, 96:96 + 2 * WS].rearrange("p h (a j) -> p a h j", a=2),
                            G[:, 2 * t:2 * t + 2, :, 0:WS],
                            qs[:, t, :, 64:64 + 2 * WS].bitcast(F32).rearrange("p h (a j) -> p a h j", a=2),
                            ALU.subtract)
                    if l == 1 and t == 1:
                        dve.wait_ge(e.qrel, i + 1)
                        last = v.tensor_tensor(qs[:, 1, :, 124:127], Mr, qs[:, 1, :, 92:95].bitcast(F32), ALU.subtract)
                last.then_inc(e.lo, 1)

            def shift(i, k):
                e = E[1]
                s, w = ((8, 21), (4, 17), (2, 15), (1, WS))[k]
                if k == 0:
                    dve.wait_ge(e.g, 4 * i + 4)
                else:
                    dve.wait_ge(e.sh, 4 * i + k)
                v.copy_predicated(G[:, :, :, 0:w], shm[:, :, k:k + 1].unsqueeze(2).broadcast_to([128, 4, NH, w]),
                                  G[:, :, :, s:s + w]).then_inc(e.sh, 1)

            def bounds(i):
                e = E[1]
                if i >= 1:
                    dve.wait_ge(e.lo, 4 * i)
                dve.wait_ge(e.sh, 4 * i + 4)
                T1 = G[:, 2:4, :, 0:WS]
                v.tensor_reduce(Mx[:, 0, :, :], T1[:, :, :, 0:2], AX, ALU.max)
                v.tensor_reduce(Mx[:, 1, :, :], T1[:, :, :, 2:WS], AX, ALU.max).then_inc(e.rmax, 1)
                dve.wait_ge(e.rmax, i + 1)
                for k, (a, b) in enumerate(((0, 2), (2, WS))):
                    last = v.tensor_tensor(DX[:, :, :, a:b], T1[:, :, :, a:b],
                                           Mx[:, k, :, :].unsqueeze(3).broadcast_to([128, 2, NH, b - a]), ALU.subtract)
                for r, (a, b) in enumerate(((1, 1), (0, 1), (1, 0))):
                    last = v.tensor_tensor(Mr[:, :, r], Mx[:, a, 0, :], Mx[:, b, 1, :], ALU.add)
                last.then_inc(e.rsub, 1)

            def bound_rows(i):
                e = E[1]
                dve.wait_ge(e.rsub, i + 1)
                if i >= 1:
                    dve.wait_ge(e.kqT, len(KQ_ENGINE[1]) * i)
                v.tensor_copy(QS[:, 1, :, 92:95], Mr).then_inc(e.qrel, 1)

            def padding_sums(i):
                e = E[1]
                dve.wait_ge(e.rexp, i + 1)
                v.tensor_reduce(SX[:, 0, :, :], DX[:, :, :, 0:2], AX, ALU.add)
                v.tensor_reduce(SX[:, 1, :, :], DX[:, :, :, 2:WS], AX, ALU.add).then_inc(e.rsum, 1)
                dve.wait_ge(e.rsum, i + 1)
                for r, (a, b) in enumerate(((1, 1), (0, 1), (1, 0))):
                    last = v.tensor_tensor(Wr[i % 2][:, :, r], SX[:, a, 0, :], SX[:, b, 1, :], ALU.mult)
                last.then_inc(e.rmul, 1)

            def head_max(l, i, h):
                e = E[l]
                dve.wait_ge(e.smm, NH * i + h + 1)
                if i >= 2 and h == 0:
                    dve.wait_ge(e.mTmm, i - 1)
                bank = ps[:, S_BANK + h % 2, :]
                v.tensor_reduce(mneg[i % 2][:, 0, h:h + 1], bank[:, 0:NM], AX, ALU.max, negate=True)
                v.tensor_reduce(mneg[i % 2][:, 1, h:h + 1], bank[:, NM:NM + SB], AX, ALU.max, negate=True)\
                    .then_inc(e.mneg, 1)

            def normalise(l, i, t):
                e = E[l]
                dve.wait_ge(e.oTmm, 2 * i + t + 1)
                o = misc(l, f"o{t}", i)[:, 0:32 * NH].rearrange("p (h d) -> p h d", d=32)
                v.reciprocal(rden[:, t, :], o[:, :, HD]).then_inc(e.rden, 1)
                dve.wait_ge(e.rden, 2 * i + t + 1)
                if i >= 1:
                    dve.wait_ge(e.onTmm, i)
                v.tensor_tensor(heads(ON[:, t, :]), o[:, :, 0:HD],
                                rden[:, t, :].unsqueeze(2).broadcast_to([128, NH, HD]), ALU.mult).then_inc(e.on, 1)

            def residual(l, i):
                e = E[l]
                dve.wait_ge(e.proj, i + 1)
                dve.wait_ge(e.xb, i + 1)
                v.tensor_tensor(X[:, 2 * i:2 * i + 2, :], misc(l, "pr", i)[:, 0:2 * C].rearrange("p (t c) -> p t c", t=2),
                                XB[:], ALU.add).then_inc(e.x1, 1)

            def edge_weights(i):
                e = E[1]
                dve.wait_ge(e.eexp, NH * (i + 1))
                p = PE_[i % 2][:, :, NE:NE + 3]
                v.tensor_tensor(p, p, Wr[i % 2], ALU.mult).then_inc(e.ew, 1)

            def attention(l, steps_):
                e = E[l]

                def image_statistics(i):
                    if l == 0:
                        statistics(e, NA, i, x_in[i], 16 * len(PIECES))
                    else:
                        statistics(e, NA, i, M[0].y, i + 1)

                work = {"stats": image_statistics,
                        "cosine": cosine_half, "rotate": rotate,
                        "sh0": lambda i: shift(i, 0), "sh1": lambda i: shift(i, 1),
                        "sh2": lambda i: shift(i, 2), "sh3": lambda i: shift(i, 3),
                        "bounds": bounds, "qrel": bound_rows, "sums": padding_sums,
                        "lo0": lambda i: stack_low(l, i, 0, False), "lk0": lambda i: stack_low(l, i, 0, True),
                        "lo1": lambda i: stack_low(l, i, 1, False), "lk1": lambda i: stack_low(l, i, 1, True),
                        "ew": edge_weights}
                empty = {"x": lambda i: split_low(e, NA, i, misc(l, "x", i)),
                         "qk0": lambda i: queries_keys(l, i, 0), "qk1": lambda i: queries_keys(l, i, 1),
                         "v01": lambda i: main_values(l, i), "ve": lambda i: edge_values(l, i),
                         "o0": lambda i: normalise(l, i, 0), "o1": lambda i: normalise(l, i, 1),
                         "pr": lambda i: residual(l, i)}
                for g in steps_:
                    if head_due(g, SCORES):
                        head_max(l, *head_due(g, SCORES))
                    for u, i in uses_due(l, g):
                        if u in empty:
                            empty[u](i)
                        elif KQ_ENGINE[l].get(u) == KQ_DVE:
                            evacuate(l, u, i, v.tensor_copy, dve, e.kq_dve)
                    for w, i in work_due(l, g, work):
                        work[w](i)
                    if l == 0 and g in setup:
                        setup[g]()
                    if g == NORM_AT:
                        statistics(M[l], NP, 0, e.x1, 1)
                        normalised_tokens(dve, v.tensor_scalar, M[l], NP, 0)
                    if g == MLP_AT:
                        mlp(l, [0])

            g0 = steps(0)[0]
            setup = {g0 + 1: lambda: layer_scales(0),
                     g0 + 3: lambda: fc1_weights(0, 0), g0 + 4: lambda: fc1_weights(0, 1),
                     g0 + 5: lambda: fc1_biases(0), g0 + 6: lambda: layer_scales(1),
                     g0 + 11: lambda: spread_biases(1), g0 + 12: lambda: fc1_weights(1, 0),
                     g0 + 13: lambda: fc1_weights(1, 1), g0 + 14: lambda: qkv_biases(1), g0 + 15: lambda: fc1_biases(1),
                     NH * B - 9: lambda: qkv_weights(1)}

            def mlp(l, part):
                m = M[l]

                def result(i):
                    dve.wait_ge(m.f2, i + 1)
                    dve.wait_ge(m.xb, i + 1)
                    o = ps[:, 5, 0:2 * C].rearrange("p (t c) -> p t c", t=2)
                    if l == 0:
                        v.tensor_tensor(X[:, 2 * i:2 * i + 2, :], o, XB[:], ALU.add).then_inc(m.y, 1)
                    else:
                        if i >= 2:
                            dve.wait_ge(store[i % 2], 16 * len(PIECES) * (i // 2))
                        v.tensor_tensor(Y[i % 2], o, XB[:], ALU.add).then_inc(m.y, 1)

                def norm(i):
                    if i < B:
                        statistics(m, NP, i, E[l].x1, i + 1)
                        normalised_tokens(dve, v.tensor_scalar, m, NP, i)

                for i in part:
                    if i == 0:
                        split_low(m, NP, 0, ps[:, 4, :])
                        norm(1)
                        continue
                    for n in ((1, 2) if i == 1 else (i + 1,)):
                        if n < B:
                            split_low(m, NP, n, ps[:, 4, :])
                        norm(n + 1)
                    result(i - 1)
                    if l == 0:
                        if i == 1:
                            stack_pads()
                            virtual_values(1)
                            bare_stack()
                        if i == 2:
                            bare_keys()
                        attention(1, FILL[i])

            def stack_pads():
                dve.wait_ge(S.cleared, 2)
                for t in range(2):
                    v.tensor_copy(QS[:, t, :, 48:64], padq[:, t:t + 1, :].broadcast_to([128, NH, 16]))

            def bare_stack():
                bk = heads(b_v0[1][0:4, 0:C])
                v.tensor_copy(KB[:, :, 16:32], bk)
                v.tensor_copy(KB[:, :, 48:64], padk[0:4, 2:3, :].broadcast_to([4, NH, 16]))
                chain(v.tensor_copy(KB[:, :, 0:16], bk))
                v.tensor_tensor(KB[:, :, 32:48], bk, KB[:, :, 0:16].bitcast(F32), ALU.subtract).then_inc(S.bare, 1)

            def bare_keys():
                dve.wait_ge(S.bareT, 1)
                bank = ps[:, MISC + 1, 0:PAIRS * NV].rearrange("p (m k) -> p m k", m=PAIRS)
                for p in range(2):
                    v.tensor_copy(KM[p][0:64, 0:NH:2, NT:NK], bank[0:64])
                    last = v.tensor_copy(KM[p][0:64, 1:NH:2, NT:NK], bank[64:128])
                chain(last)

            v.memset(nhalf[:], -0.5)
            v.memset(ps[:, O_BANK:O_BANK + 2, :], 0.0)
            spread_biases(0)
            statistics(E[0], NA, 0, x_in[0], 16 * len(PIECES))
            qkv_weights(0)
            constants()
            virtual_values(0)
            qkv_biases(0)
            attention(0, steps(0))
            mlp(0, range(1, B + 1))
            dve.drain().then_inc(phase, 1)
            dve.wait_ge(phase, 4)
            attention(1, REST)
            mlp(1, range(1, B + 1))

        @block.scalar
        def _(act):
            a = nc.scalar

            def copy(dst, src):
                return a.activation(dst, src, ACT.Copy)

            def split_high(e, b, i, bank, used, n):
                act.wait_ge(e.xT, i + 1)
                if i >= 1:
                    act.wait_ge(used, n * i)
                copy(b.XH[:, :, 0:NT], bank.rearrange("p (r t) -> p r t", r=2)).then_inc(e.xh, 1)

            def stack_high(l, i, t, keys):
                e = E[l]
                src, qs = (QKa, QS0) if l == 0 else (QK, QS)
                if l == 0:
                    act.wait_ge(e.qkr, i + 1)
                else:
                    act.wait_ge(e.qk, 2 * i + t + 1)
                    if not keys:
                        act.wait_ge(e.sh, 4 * i + 4)
                if i >= 1:
                    act.wait_ge(e.kqT, len(KQ_ENGINE[l]) * i)
                if keys:
                    k = heads(src[:, t, C:]).unsqueeze(2).broadcast_to([128, NH, 2, HD])
                    last = copy(KS[:, t, :, 0:32].rearrange("p h (s d) -> p h s d", s=2), k)
                else:
                    q = heads(src[:, t, 0:C]).unsqueeze(2).broadcast_to([128, NH, 2, HD])
                    last = copy(qs[:, t, :, 0:64].rearrange("p h (s d) -> p h s d", s=2)[:, :, :, 0:HD], q)
                    if l == 1:
                        last = copy(qs[:, t, :, 64:64 + 2 * WS].rearrange("p h (a j) -> p a h j", a=2),
                                    G[:, 2 * t:2 * t + 2, :, 0:WS])
                last.then_inc(e.hi, 1)

            def queries_T(i):
                e = E[1]
                act.wait_ge(e.qfT, i + 1)
                if i >= 1:
                    act.wait_ge(e.gmm, 4 * i)
                copy(QF, misc(1, "qf", i)[0:HP, :].rearrange("p (f t) -> p f t", f=2)).then_inc(e.qf, 1)

            def relative_terms(i, n):
                e = E[1]
                if i >= 1:
                    act.wait_ge(e.lo, 4 * i)
                t, f = n // 2, n % 2
                act.wait_ge(e.gmm, 4 * i + n + 1)
                copy(G[:, 2 * t:2 * t + 2, 6 * f:6 * f + 6, :],
                     misc(1, f"g{n}", i)[:, 0:12 * NG].rearrange("p (h a j) -> p a h j", h=6, a=2))\
                    .then_inc(e.g, 1)

            def relative_exp(i):
                e = E[1]
                act.wait_ge(e.rsub, i + 1)
                a.activation(DX, DX, ACT.Exp).then_inc(e.rexp, 1)

            def probabilities(l, i, h):
                e = E[l]
                n = NH * i + h
                act.wait_ge(e.stmm, n + 1)
                if n >= 4:
                    act.wait_ge(e.av, n - 3)
                a.activation(PT[:, h % 4, :], ps[0:CH, ST_BANK + h % 2, 0:2 * NM], ACT.Exp).then_inc(e.pexp, 1)

            def output(l, i, part):
                e = E[l]
                act.wait_ge(e.ave, PAIRS * i + (4, 6)[part])
                if i >= 1 and part == 0:
                    act.wait_ge(e.oTmm, 2 * i)
                if part == 0:
                    copy(OT[:, 0:2, :], ps[:, O_BANK, :].rearrange("p (k t) -> p k t", k=2)).then_inc(e.ot, 1)
                else:
                    copy(OT[:, 2, :], ps[:, O_BANK + 1, 0:NT]).then_inc(e.ot, 1)

            def output_T(l, i):
                e = E[l]
                act.wait_ge(e.onTmm, i + 1)
                if i >= 1:
                    act.wait_ge(e.proj, i)
                copy(ONT[:], misc(l, "on", i)[0:HP, :].rearrange("p (f t) -> p f t", f=2)).then_inc(e.ont, 1)

            def maxima(l, i):
                e, p = E[l], i % 2
                act.wait_ge(e.mTmm, i + 1)
                if i >= 2:
                    act.wait_ge(e.stmm, NH * (i - 1))
                copy(mT[p][:], misc(l, "m", i)[:, 0:NT]).then_inc(e.mT, 1)

            def edge_exp(l, i, h):
                e, p = E[l], i % 2
                act.wait_ge(e.mneg, NH * i + h + 1)
                if i >= 2 and h == 0:
                    act.wait_ge(e.eTmm, 2 * (i - 1))
                a.activation(PE_[p][:, h, :], ps[:, S_BANK + h % 2, 2 * NM:2 * NM + EK], ACT.Exp,
                             bias=mneg[p][:, 1, h:h + 1]).then_inc(e.eexp, 1)

            def edges(l, i, n):
                e, p = E[l], i % 2
                m0, m1 = ((0, 4), (4, 6))[n]
                act.wait_ge(e.eTmm, 2 * i + n + 1)
                if i >= 2:
                    act.wait_ge(e.ave, PAIRS * (i - 1))
                src = misc(l, f"e{n}", i)[:, 0:128 * (m1 - m0)].rearrange("p (m q) -> p m q", q=128)
                copy(PET[p][:, m0:m1, :], src[:, :, E0:128]).then_inc(e.pet, 1)

            def attention(l, steps_):
                e = E[l]
                work = {"hi0": lambda i: stack_high(l, i, 0, False), "hk0": lambda i: stack_high(l, i, 0, True),
                        "hi1": lambda i: stack_high(l, i, 1, False), "hk1": lambda i: stack_high(l, i, 1, True),
                        "rexp": relative_exp,
                        "out0": lambda i: output(l, i, 0), "out1": lambda i: output(l, i, 1)}
                empty = {"x": lambda i: split_high(e, NA, i, misc(l, "x", i), e.vmm, 2), "qf": queries_T,
                         "g0": lambda i: relative_terms(i, 0), "g1": lambda i: relative_terms(i, 1),
                         "g2": lambda i: relative_terms(i, 2), "g3": lambda i: relative_terms(i, 3),
                         "m": lambda i: maxima(l, i), "e0": lambda i: edges(l, i, 0), "e1": lambda i: edges(l, i, 1),
                         "on": lambda i: output_T(l, i)}
                for g in steps_:
                    for u, i in uses_due(l, g):
                        if u in empty:
                            empty[u](i)
                        elif KQ_ENGINE[l].get(u) == KQ_ACT:
                            evacuate(l, u, i, copy, act, e.kq_act)
                    if head_due(g, 0):
                        probabilities(l, *head_due(g, 0))
                    if head_due(g, SCORES):
                        edge_exp(l, *head_due(g, SCORES))
                    for w, i in work_due(l, g, work):
                        work[w](i)
                    if g == MLP_AT:
                        mlp(l, [0])

            def mlp(l, part):
                m = M[l]
                for i in part:
                    if i == 0:
                        act.wait_ge(E[l].av, NH * B)
                    if i < 2:
                        split_high(m, NP, i, ps[:, 4, :], m.f1, 3)
                    if i < B:
                        for k in range(MT):
                            n = 3 * i + k // 2
                            act.wait_ge(m.f1, n + 1)
                            if i >= 2 and k == 0:
                                act.wait_ge(m.f2, i - 1)
                            a.activation(GT[i % 2][:, k, :], ps[:, n % 4, NT * (k % 2):NT * (k % 2) + NT], ACT.Gelu,
                                         bias=b_1[l][:, k:k + 1]).then_inc(m.gelu, 1)
                    if 0 < i < B - 1:
                        split_high(m, NP, i + 1, ps[:, 4, :], m.f1, 3)
                    if l == 0 and i in (1, 2):
                        copy(KM[i - 1][64:128, :, :], hot[64:128, :].unsqueeze(1).broadcast_to([64, NH, NK]))
                    if l == 0:
                        attention(1, FILL[i])

            weight_loads(act, 0)
            attention(0, steps(0))
            mlp(0, range(1, B + 1))
            act.drain().then_inc(phase, 1)
            act.wait_ge(phase, 4)
            attention(1, REST)
            mlp(1, range(1, B + 1))

        @block.gpsimd
        def _(pool):
            g = nc.gpsimd

            def inv_std(e, b, i, l):
                pool.wait_ge(e.aggr, i + 1)
                g.tensor_scalar(b.veps[:], b.mv[:, :, 1], EPS1[l], 1.0, ALU.add, ALU.mult).then_inc(e.veps, 1)
                pool.wait_ge(e.veps, i + 1)
                if i >= 1:
                    pool.wait_ge(e.xn, i)
                g.tensor_tensor(b.rstd[:], b.veps[:], nhalf[:], ALU.pow).then_inc(e.rstd, 1)

            def edge_copies(e, i):
                pool.wait_ge(e.xl, i + 1)
                for ap in (NA.XH[:, 0, :], NA.XH[:, 1, :], NA.XL[:, :]):
                    g.tensor_scalar(ap[:, NK:NK + NE], ap[:, NM:NT].bitcast(F32), 1.0, 0.0, ALU.mult, ALU.add)\
                        .then_inc(e.xd, 1)

            def sine_half(i):
                e = E[0]
                pool.wait_ge(e.qk, 2 * i + 2)
                if i >= 1:
                    pool.wait_ge(e.qkr, i)
                half = HD // 2
                for k in range(2):
                    for t in range(2):
                        last = g.tensor_tensor(
                            heads(QKb[:, t, :], 2 * NH)[:, :, half * k:half * k + half],
                            heads(QK[:, t, :], 2 * NH)[:, :, half - half * k:HD - half * k],
                            sin_t[:, t:t + 1, half * k:half * k + half].broadcast_to([128, 2 * NH, half]), ALU.mult)
                    last.then_inc(e.t2, 1)

            def residual_bias(e, i, bias, done):
                if bias is b_p[0] and i == 0:
                    pool.wait_ge(S.scales, 1)
                if e in M and i == 0:
                    pool.wait_ge(E[M.index(e)].x1, B)
                if i >= 1:
                    pool.wait_ge(done, i)
                for t in range(2):
                    last = g.tensor_tensor(XB[:, t, :], X[:, 2 * i + t, :], bias[:], ALU.add)
                last.then_inc(e.xb, 1)

            def clear(l):
                if l == 0:
                    for b in (KS, KM[0], KM[1]):
                        g.memset(b[:].bitcast(F32), 0.0)
                    for p in range(2):
                        g.memset(mneg[p][:], 0.0)
                else:
                    pool.wait_ge(E[0].ave, PAIRS * B)
                    pool.wait_ge(E[0].kqT, len(KQ_ENGINE[0]) * B)
                for p in range(NVB):
                    g.memset(VE[p][:], 0.0)
                g.memset(QS[:].bitcast(F32), 0.0).then_inc(S.cleared, 1)

            def attention(l, steps_):
                e = E[l]
                work = {"inv_std": lambda i: inv_std(e, NA, i, l),
                        "xn": lambda i: normalised_tokens(pool, g.tensor_scalar, e, NA, i),
                        "xd": lambda i: edge_copies(e, i), "sine": sine_half,
                        "xb": lambda i: residual_bias(e, i, b_p[l], e.x1)}
                for step in steps_:
                    for w, i in work_due(l, step, work):
                        work[w](i)
                    if step == NORM_AT:
                        inv_std(M[l], NP, 0, l)
                    if step == MLP_AT:
                        mlp(l, [0])

            def mlp(l, part):
                m = M[l]
                for i in part:
                    if i == 0:
                        inv_std(m, NP, 1, l)
                        if l == 0:
                            clear(1)
                        continue
                    for n in ((2, 3) if i == 1 else (i + 2,)):
                        if n < B:
                            inv_std(m, NP, n, l)
                    residual_bias(m, i - 1, b_2[l], m.y)
                    if l == 0:
                        attention(1, FILL[i])

            g.memset(NA.XH[:].bitcast(F32), 0.0)
            g.memset(NA.XL[:].bitcast(F32), 0.0)
            inv_std(E[0], NA, 0, 0)
            normalised_tokens(pool, g.tensor_scalar, E[0], NA, 0)
            clear(0)
            attention(0, steps(0))
            mlp(0, range(1, B + 1))
            pool.drain().then_inc(phase, 1)
            pool.wait_ge(phase, 4)
            attention(1, REST)
            mlp(1, range(1, B + 1))

        @block.tensor
        def _(pe):
            mm = nc.tensor.matmul
            T = nc.tensor.transpose

            def fold_qkv(l):
                pe.wait_ge(S.lnb, l + 1)
                for w0, n, o in ((0, 2 * C, ps[:, 4, 0:2 * C]), (2 * C, C, ps[:, 5, 0:C])):
                    mm(o, lnb_w[:, 0, 0, :], raw[:, 0, w0:w0 + n], start=True, stop=False)
                    last = mm(o, lnb_w[0:64, 0, 1, :], raw[0:64, 1, w0:w0 + n], start=False, stop=True)
                last.then_inc(S.fold_qkv, 1)

            def fold_fc1(l):
                pe.wait_ge(S.lnb, l + 1)
                pe.wait_ge(wf_in[l], N_WF)
                for k in range(MT):
                    w0 = 3 * C + 128 * k
                    o = ps[:, 3, k:k + 1]
                    mm(o, raw[:, 0, w0:w0 + 128], lnp[:, 0, 3:4], start=True, stop=False)
                    last = mm(o, raw[0:64, 1, w0:w0 + 128], lnp[0:64, 1, 3:4], start=False, stop=True)
                last.then_inc(S.fold_fc1, 1)

            def bare_keys():
                pe.wait_ge(S.bare, 1)
                pe.wait_ge(E[0].x1, B)
                for k in range(PAIRS):
                    last = T(ps[:, MISC + 1, NV * k:NV * k + NV], KB[:, 2 * k:2 * k + 2, :].bitcast(F32),
                             ident[0:NV, 0:NV])
                last.then_inc(S.bareT, 1)

            def transpose_tokens(e, b, i, bank):
                pe.wait_ge(e.xn, i + 1)
                for t in range(2):
                    T(bank[:, 128 * t:128 * t + 128], b.xn[:, t, 0:128], ident[:])
                    last = T(bank[:, NT + 128 * t:NT + 128 * t + 128],
                             b.xn[:, t, 128:C + 64], ident[:])
                last.then_inc(e.xT, 1)

            def split_product(o, parts, w, flip=False):
                x0, xl, x1 = parts
                steps = ((x0, w[0]), (xl, w[0]), (x0, w[1]), (x1, w[2]), (x1, w[3]))
                for n, (x_, w_) in enumerate(steps):
                    last = mm(o, w_ if flip else x_, x_ if flip else w_, start=n == 0, stop=n == 4)
                return last

            def project_qk(l, i, t):
                e = E[l]
                pe.wait_ge(e.xl, i + 1)
                wait_misc_free(pe, l, f"qk{t}", i)
                c = slice(128 * t, 128 * t + 128)
                if i == 0:
                    pe.wait_ge(S.wq, l + 1)
                split_product(misc(l, f"qk{t}", i)[:, 0:2 * C], (NA.XH[:, 0, c], NA.XL[:, c], NA.XH[:, 1, c]),
                              [WQ[:, k, 0:2 * C] for k in range(4)]).then_inc(e.qkmm, 1)

            def project_v(l, i):
                e = E[l]
                w = [WQ[:, k, 2 * C:] for k in range(4)]
                wait_misc_free(pe, l, "v01", i)
                for n in range(2):
                    c = slice(CH * n, CH * n + CH)
                    last = split_product(misc(l, "v01", i)[0:CH, C * n:C * n + C],
                                         (NA.XH[:, 0, c], NA.XL[:, c], NA.XH[:, 1, c]), w)
                last.then_inc(e.vmm, 1)

            def project_edge_v(l, i):
                e = E[l]
                w = [WQ[:, k, 2 * C:] for k in range(4)]
                wait_misc_free(pe, l, "ve", i)
                pe.wait_ge(e.xd, 3 * (i + 1))
                split_product(misc(l, "ve", i)[:, 0:C], (NA.XH[:, 0, NM:ND], NA.XL[:, NM:ND], NA.XH[:, 1, NM:ND]), w)\
                    .then_inc(e.vmm, 1)

            def transpose_queries(i):
                e = E[1]
                pe.wait_ge(e.qk, 2 * i + 2)
                wait_misc_free(pe, 1, "qf", i)
                bank = misc(1, "qf", i)
                for f in range(2):
                    for t in range(2):
                        last = T(bank[0:HP, NT * f + 128 * t:NT * f + 128 * t + 128], QK[:, t, HP * f:HP * f + HP],
                                 ident[:])
                last.then_inc(e.qfT, 1)

            def relative_products(i, n):
                e = E[1]
                pe.wait_ge(e.qf, i + 1)
                wait_misc_free(pe, 1, f"g{n}", i)
                t, f = n // 2, n % 2
                mm(misc(1, f"g{n}", i)[:, 0:12 * NG], QF[:, f, 128 * t:128 * t + 128], Rbd[:],
                   start=True, stop=True).then_inc(e.gmm, 1)

            def transpose_stacks(l, u, i):
                e = E[l]
                pe.wait_ge(e.lo, 4 * i + 4)
                wait_misc_free(pe, l, u, i)
                j = int(u[1])
                for m in range(2):
                    for t in range(2):
                        if u[0] == "k":
                            src = KS[:, t, 4 * j + 2 * m:4 * j + 2 * m + 2, :]
                        elif l == 0:
                            src = QS0[:, t, 4 * j + 2 * m:4 * j + 2 * m + 2, :]
                        else:
                            src = QS[:, t, 2 * j + m, :]
                        last = T(misc(l, u, i)[:, NT * m + 128 * t:NT * m + 128 * t + 128], src.bitcast(F32), ident[:])
                last.then_inc(e.kqT, 1)

            def query(l, i, h):
                return QT[i % 2][:, h // 2 if l == 0 else h, :]

            def scores(l, i, h):
                e, p = E[l], i % 2
                n = NH * i + h
                for u in stacks_of(l, h):
                    pe.wait_ge(*misc_emptied(l, u, i))
                if n >= 2:
                    pe.wait_ge(e.eexp, n - 1)
                q = query(l, i, h)
                bank = ps[:, S_BANK + h % 2, :]
                mm(bank[:, 0:NM], q[:, 0:128], KM[p][:, h, 0:NM], start=True, stop=True)
                mm(bank[:, NM:NM + SB], q[:, 128:NT], KM[p][:, h, :], start=True, stop=True).then_inc(e.smm, 1)

            def transpose_maxima(l, i):
                e = E[l]
                pe.wait_ge(e.mneg, NH * (i + 1))
                wait_misc_free(pe, l, "m", i)
                for t in range(2):
                    last = T(misc(l, "m", i)[:, 128 * t:128 * t + 128], mneg[i % 2][:, t, :], ident[:])
                last.then_inc(e.mTmm, 1)

            def transpose_edges(l, i, n):
                e = E[l]
                if l:
                    pe.wait_ge(e.ew, i + 1)
                else:
                    pe.wait_ge(e.eexp, NH * (i + 1))
                wait_misc_free(pe, l, f"e{n}", i)
                m0, m1 = ((0, 4), (4, 6))[n]
                for m in range(m0, m1):
                    last = T(misc(l, f"e{n}", i)[:, 128 * (m - m0):128 * (m - m0) + 128],
                             PE_[i % 2][:, 2 * m:2 * m + 2, :], ident[:])
                last.then_inc(e.eTmm, 1)

            def scores_T(l, i, h):
                e, p = E[l], i % 2
                n = NH * i + h
                if l == 0 and n == 0:
                    pe.wait_ge(S.b_fc1, 2)
                if h == 0:
                    pe.wait_ge(e.mT, i + 1)
                if n >= 2:
                    pe.wait_ge(e.pexp, n - 1)
                q = query(l, i, h)
                for c in range(2):
                    o = ps[0:CH, ST_BANK + h % 2, NM * c:NM * c + NM]
                    mm(o, KM[p][:, h, CH * c:CH * c + CH], q[:, 0:NM], start=True, stop=False)
                    last = mm(o, sel[:, h, :], mT[p][:, 0:NM], start=False, stop=True)
                last.then_inc(e.stmm, 1)

            def weighted_values(l, i, h):
                e, p = E[l], i % 2
                n = NH * i + h
                pe.wait_ge(e.pexp, n + 1)
                if h == 0:
                    pe.wait_ge(e.v01, i + 1)
                    pe.wait_ge(e.ve, i + 1)
                    pe.wait_ge(e.pet, 2 * i + 2)
                if i >= 1 and h in (0, 8):
                    pe.wait_ge(e.ot, 2 * i - (h == 0))
                k, j = h // 4, h % 4
                block_o = ps[:, O_BANK + k // 2, NT * (k % 2):NT * (k % 2) + NT]
                for c in range(2):
                    last = mm(block_o[32 * j:32 * j + HD + 1, 0:NM], V01[i % NVB][:, c, h, :],
                              PT[:, h % 4, NM * c:NM * c + NM], start=c == 0, stop=c == 1)
                last.then_inc(e.av, 1)
                if h % 2:
                    m = h // 2
                    r = 64 * (m % 2)
                    mm(block_o[r:r + 64, NM:NT], VE[i % NVB][:, m, :], PET[p][:, m, :], start=True, stop=True)\
                        .then_inc(e.ave, 1)

            def transpose_output(l, i, t):
                e = E[l]
                pe.wait_ge(e.ot, 2 * i + 2)
                wait_misc_free(pe, l, f"o{t}", i)
                for k in range(3):
                    last = T(misc(l, f"o{t}", i)[:, 128 * k:128 * k + 128], OT[:, k, 128 * t:128 * t + 128],
                             ident[:])
                last.then_inc(e.oTmm, 1)

            def transpose_normalised(l, i):
                e = E[l]
                pe.wait_ge(e.on, 2 * i + 2)
                wait_misc_free(pe, l, "on", i)
                for f in range(2):
                    for t in range(2):
                        last = T(misc(l, "on", i)[0:HP, NT * f + 128 * t:NT * f + 128 * t + 128],
                                 ON[:, t, HP * f:HP * f + HP], ident[:])
                last.then_inc(e.onTmm, 1)

            def project_output(l, i):
                e = E[l]
                pe.wait_ge(e.ont, i + 1)
                wait_misc_free(pe, l, "pr", i)
                for t in range(2):
                    for f in range(2):
                        last = mm(misc(l, "pr", i)[:, C * t:C * t + C], ONT[:, f, 128 * t:128 * t + 128],
                                  WP[l][:, f, :], start=f == 0, stop=f == 1)
                last.then_inc(e.proj, 1)

            def attention(l, steps_):
                e = E[l]

                def tokens(i):
                    wait_misc_free(pe, l, "x", i)
                    transpose_tokens(e, NA, i, misc(l, "x", i))

                fill = {"x": tokens, "qk0": lambda i: project_qk(l, i, 0), "qk1": lambda i: project_qk(l, i, 1),
                        "v01": lambda i: project_v(l, i), "ve": lambda i: project_edge_v(l, i),
                        "qf": transpose_queries,
                        "g0": lambda i: relative_products(i, 0), "g1": lambda i: relative_products(i, 1),
                        "g2": lambda i: relative_products(i, 2), "g3": lambda i: relative_products(i, 3),
                        "m": lambda i: transpose_maxima(l, i),
                        "e0": lambda i: transpose_edges(l, i, 0), "e1": lambda i: transpose_edges(l, i, 1),
                        "o0": lambda i: transpose_output(l, i, 0), "o1": lambda i: transpose_output(l, i, 1),
                        "on": lambda i: transpose_normalised(l, i), "pr": lambda i: project_output(l, i)}
                for g in steps_:
                    uses = uses_due(l, g)

                    def fill_bank(u, i):
                        if u in fill:
                            fill[u](i)
                        else:
                            transpose_stacks(l, u, i)

                    if head_due(g, SCORES):
                        scores(l, *head_due(g, SCORES))
                    for u, i in uses[0:2]:
                        fill_bank(u, i)
                    if head_due(g, 0):
                        scores_T(l, *head_due(g, 0))
                    if head_due(g, 1):
                        weighted_values(l, *head_due(g, 1))
                    for u, i in uses[2:]:
                        fill_bank(u, i)
                    if l == 0 and g == steps(0)[0] + 1:
                        fold_fc1(0)
                    if l == 0 and g == steps(0)[0] + 12:
                        fold_qkv(1)
                        fold_fc1(1)
                    if g == MLP_AT:
                        mlp(l, [0])

            def hidden(l, i):
                m = M[l]
                pe.wait_ge(m.xl, i + 1)
                if i == 0:
                    pe.wait_ge(E[l].eexp, NH * B)
                    pe.wait_ge(E[l].pexp, NH * B)
                for j in range(3):
                    n = 3 * i + j
                    if n >= 4:
                        pe.wait_ge(m.gelu, 2 * (n - 3))
                    for k in (2 * j, 2 * j + 1):
                        w = [WF[l][:, r, 128 * k:128 * k + 128] for r in range(4)]
                        last = split_product(ps[:, n % 4, NT * (k % 2):NT * (k % 2) + NT],
                                             (NP.XH[:, 0, 0:NT], NP.XL[:, 0:NT], NP.XH[:, 1, 0:NT]), w, flip=True)
                    last.then_inc(m.f1, 1)

            def down(l, i):
                m = M[l]
                pe.wait_ge(m.gelu, MT * (i + 1))
                if i >= 1:
                    pe.wait_ge(m.y, i)
                for t in range(2):
                    for k in range(MT):
                        last = mm(ps[:, 5, C * t:C * t + C], GT[i % 2][:, k, 128 * t:128 * t + 128], W2[l][:, k, :],
                                  start=k == 0, stop=k == MT - 1)
                last.then_inc(m.f2, 1)

            def mlp(l, part):
                m = M[l]
                for i in part:
                    if i == 0:
                        pe.wait_ge(E[l].ot, 2 * B)
                        transpose_tokens(m, NP, 0, ps[:, 4, :])
                    if i < B:
                        hidden(l, i)
                    if i + 1 < B:
                        transpose_tokens(m, NP, i + 1, ps[:, 4, :])
                    if i:
                        down(l, i - 1)
                    if l == 0:
                        if i == 1:
                            bare_keys()
                        attention(1, FILL[i])

            pe.wait_ge(c_in, N_CONST)
            pe.wait_ge(wq_in[0], N_WQ)
            fold_qkv(0)
            attention(0, steps(0))
            mlp(0, range(1, B + 1))
            pe.drain().then_inc(phase, 1)
            pe.wait_ge(phase, 4)
            attention(1, REST)
            mlp(1, range(1, B + 1))


def tables():
    import numpy as np

    rows = np.array([n // WS for n in range(NM)] + [r for r in range(WS) for _ in range(W - WS)]
                    + [r for r in range(WS, H) for _ in range(W)])
    cols = np.array([n % WS for n in range(NM)] + [c for _ in range(WS) for c in range(WS, W)]
                    + [c for _ in range(WS, H) for c in range(W)])
    group = np.where((rows < WS) & (cols < WS), 3, np.where(rows < WS, 0, np.where(cols < WS, 1, 2)))
    qr, qc = rows % WS, cols % WS
    onehot = (group[:, None] == np.arange(4)[None, :]).astype(np.float32)
    t = {"ident": np.eye(128, dtype=np.float32)}

    def tiles(a):
        return np.ascontiguousarray(a.reshape(2, 128, *a.shape[1:]).swapaxes(0, 1))

    padq = np.zeros((NT, 16), np.float32)
    padq[:, 0:4] = onehot
    padk = np.zeros((NT, 16), np.float32)
    padk[:, 0:4] = -BIG * (1 - onehot)
    seen = np.array([[1, 1, 1, 0], [1, 0, 1, 0], [0, 1, 1, 0], [0, 0, 0, 0]], np.float32)
    virt = np.zeros((128, 1, 16), np.float32)
    virt[0:4, 0, 0:4] = -BIG * (1 - seen)
    t["padq"] = tiles(padq)
    t["padk"] = np.concatenate([tiles(padk), virt], 1)
    own = np.concatenate([np.eye(4, dtype=np.float32)[0:3], np.zeros((1, 4), np.float32)])
    kv = np.zeros((128, NH, NV), np.float32)
    for h in range(NH):
        r = 64 * (h % 2) + 48
        kv[r:r + 4, h, :] = -BIG * (1 - own.T)
    t["kvirt"] = kv
    hot = np.zeros((64, NK), np.float32)
    for r0 in (0, 32):
        hot[r0 + qr, np.arange(NT)] = 1
        hot[r0 + WS + qc, np.arange(NT)] = 1
        hot[r0 + 2 * WS + np.arange(3), NT + np.arange(3)] = 1
    t["hot"] = hot
    vc = np.zeros((128, 2, 2, 2), np.float32)
    counts = [NM - WS * (W - WS), NM - WS * (H - WS), NM - (H - WS) * (W - WS)]
    for k in range(2):
        r = 64 * k
        vc[r:r + NE, :, k, 1] = 1
        for g in range(3):
            vc[r + NE + g, 0, k, :] = counts[g]
            vc[r + NE + g, 1, k, :] = 1
    t["vcon"] = vc
    shm = np.zeros((NT, 2, 4), np.int32)
    for k, s in enumerate((8, 4, 2, 1)):
        shm[:, 0, k] = ((WS - 1 - qr) & s) > 0
        shm[:, 1, k] = ((WS - 1 - qc) & s) > 0
    t["shm"] = np.ascontiguousarray(tiles(shm).reshape(128, 4, 4))
    token = rows * W + cols
    return t, token


def kernel(**inputs):
    import numpy as np
    import concourse.bacc as bacc
    from concourse.bass_utils import run_bass_kernel_spmd

    a = {k: np.asarray(v) for k, v in inputs.items()}
    tab, token = tables()
    arrays = {"x": a["x"]}

    def bc(v):
        return np.ascontiguousarray(np.broadcast_to(v, (128, v.shape[-1])))

    def by_tile(v):
        return np.ascontiguousarray(v.reshape(2, 128, -1).swapaxes(0, 1))

    rope = a["L0_conv_rope_2d"].reshape(NT, HD)[token]
    half = HD // 2
    sin, cos = rope[:, :half], rope[:, half:]
    arrays["cos"] = by_tile(np.concatenate([cos, cos], 1))
    arrays["sin"] = by_tile(np.concatenate([sin, sin], 1))
    for n, v in tab.items():
        arrays[n] = v
    arrays["gamma1"], arrays["gamma2"] = bc(a["L0_conv_gamma_1"]), bc(a["L0_conv_gamma_2"])
    R = np.zeros((2, NG, HD), np.float32)
    for k, n in enumerate(("h", "w")):
        R[k, 0:2 * WS - 1] = a[f"L1_conv_rel_pos_{n}"][::-1]
    rbd = np.zeros((6, HD, 6, 2, NG), np.float32)
    for h in range(6):
        rbd[h, :, h] = R.transpose(2, 0, 1)
    arrays["rbd"] = rbd.reshape(HP, 6 * 2 * NG)
    for l in range(2):
        g = (lambda n: a[f"L0_conv_{n}"]) if l == 0 else (lambda n: a[f"L1_conv_{n}"])
        if l == 0:
            wqkv, wproj, w1, w2 = g("w_qkv").T, g("w_proj").T, g("w_fc1").T, g("w_fc2").T
            ln = [g("ln1_g"), g("ln1_b"), g("ln2_g"), g("ln2_b")]
            bs = [g("b_qkv"), g("b_proj"), g("b_fc1"), g("b_fc2")]
        else:
            wqkv, wproj, w1, w2 = g("qkv_w"), g("proj_w"), g("fc1_w"), g("fc2_w")
            ln = [g("ln1_w"), g("ln1_b"), g("ln2_w"), g("ln2_b")]
            bs = [g("qkv_b"), g("proj_b"), g("fc1_b"), g("fc2_b")]
        arrays[f"wqkv{l}"] = wqkv
        arrays[f"w1{l}"] = w1
        arrays[f"wproj{l}"] = wproj.reshape(2, HP, C).swapaxes(0, 1)
        arrays[f"w2{l}"] = w2.reshape(MT, 128, C).swapaxes(0, 1)
        ln = np.stack(ln, 1)
        arrays[f"ln{l}"] = np.stack([ln[0:128], np.concatenate([ln[128:C], ln[128:C]])], 1)
        arrays[f"bqkv{l}"], arrays[f"bproj{l}"], arrays[f"b2{l}"] = bc(bs[0]), bc(bs[1]), bc(bs[3])
        arrays[f"b1{l}"] = bs[2].reshape(MT, 128).T

    nc = bacc.Bacc("TRN2", target_bir_lowering=False, num_devices=1)
    arrays = {f"in_{n}": np.ascontiguousarray(v) for n, v in arrays.items()}
    d = {n[3:]: nc.dram_tensor(n, v.shape, mybir.dt.from_np(v.dtype), kind="ExternalInput").ap()
         for n, v in arrays.items()}
    out = nc.dram_tensor("out_0", (B, H, W, C), F32, kind="ExternalOutput").ap()
    names = ("wqkv", "w1", "wproj", "w2", "ln", "bqkv", "bproj", "b2", "b1")
    extra = (dict(gamma1=d["gamma1"], gamma2=d["gamma2"], rbd=None), dict(gamma1=None, gamma2=None, rbd=d["rbd"]))
    layers = [Block(**{n: d[f"{n}{l}"] for n in names}, **extra[l]) for l in range(2)]
    build(nc, d["x"], d["cos"], d["sin"], layers, {n: d[n] for n in tab}, out)
    r = run_bass_kernel_spmd(nc, [arrays], core_ids=[0])
    return r.results[0]["out_0"]
```
